# Optimizing a Trainium2 kernel written in Bass

```python
import numpy as np
import jax
import jax.numpy as jnp

def _softmax(x, axis=-1):
    return jax.nn.softmax(x, axis=axis)

def _gelu(x):
    return jax.nn.gelu(x, approximate=True)

def _silu(x):
    return jax.nn.silu(x)

def _sigmoid(x):
    return jax.nn.sigmoid(x)

def _layernorm(x, axis=-1, eps=1e-05):
    m = jnp.mean(x, axis=axis, keepdims=True)
    v = jnp.var(x, axis=axis, keepdims=True)
    return (x - m) / jnp.sqrt(v + eps)

def _scatter_add(tgt, idx, src, axis=0):
    return tgt.at[idx].add(src)

def _segment_sum(src, seg, n):
    return jax.ops.segment_sum(src, seg, n)
kernel_name = 'mk_xattn_seq_d4_seqx_r8_71b4a1'

def setup_inputs(seed: int=0):
    np.random.seed(seed)
    _w = jnp.asarray

    def _rec_inputs():
        import jax
        import jax.numpy as jnp
        _rk = jax.random.key(seed)
        x = -7.109e-05 + 0.9999 * jax.random.normal(jax.random.fold_in(_rk, 1), (8, 256, 128), jnp.float32)
        _lenS = 256 - jax.random.randint(jax.random.fold_in(_rk, 7), (8,), 0, max(1, 256 // 4) + 1, jnp.int32)
        _lenS2 = 64 - jax.random.randint(jax.random.fold_in(_rk, 8), (8,), 0, max(1, 64 // 4) + 1, jnp.int32)
        _ctx_512P = jax.random.normal(jax.random.fold_in(_rk, 11), (8, 16, 64), jnp.float32)
        _ctx_512c = jax.random.dirichlet(jax.random.fold_in(_rk, 511), 0.3 * jnp.ones((16,), jnp.float32), (8, 64))
        _ctx_512t = jnp.einsum('bsk,bkd->bsd', _ctx_512c, _ctx_512P)
        _ctx_512t = _ctx_512t * jax.lax.rsqrt(jnp.mean(jnp.square(_ctx_512t)) + 1e-12) * 0.953939
        ctx_512 = 0.000227908 + 0.99994 * (_ctx_512t + 0.3 * jax.random.normal(jax.random.fold_in(_rk, 611), (8, 64, 64), jnp.float32))
        _validS = jnp.arange(256)[None, :] < _lenS[:, None]
        _validS2 = jnp.arange(64)[None, :] < _lenS2[:, None]
        _causal = jnp.tril(jnp.ones((256, 256), dtype=bool))
        mask_BxSxS_ik0 = jnp.where(jnp.broadcast_to(_validS[:, None, :], (8, 256, 256)), 0, 1).astype(jnp.int32)
        mask_Bx1xS2_if1 = jnp.where(jnp.ones((8, 1, 64), dtype=bool), 1, 0).astype(jnp.int32)
        return (x, ctx_512, mask_BxSxS_ik0, mask_Bx1xS2_if1)
    x, ctx_512, mask_BxSxS_ik0, mask_Bx1xS2_if1 = _rec_inputs()

    def _L0_xattn_setup():
        import jax, jax.numpy as jnp
        import numpy as np
        ENTROPY_THRESHOLD = 1.0
        N_HEADS = 16
        LN_EPS = 1e-05

        def _layernorm(x, scale, bias):
            mu = jnp.mean(x, axis=-1, keepdims=True)
            var = jnp.mean(jnp.square(x - mu), axis=-1, keepdims=True)
            return (x - mu) * jax.lax.rsqrt(var + LN_EPS) * scale + bias
        key = jax.random.key(seed)
        ks = jax.random.split(key, 16)
        B, L, M = (32, 256, 64)
        d_model, d_mem, dg = (128, 64, 64)
        s = 0.02
        return {'hidden_states': jax.random.normal(ks[0], (B, L, d_model), jnp.float32), 'memory_vectors': jax.random.normal(ks[1], (B, M, d_mem), jnp.float32), 'memory_keys': jax.random.normal(ks[2], (B, M, d_mem), jnp.float32), 'Wq': jax.random.normal(ks[3], (d_model, d_model), jnp.float32) * s, 'Wk': jax.random.normal(ks[4], (d_model, d_mem), jnp.float32) * s, 'Wv': jax.random.normal(ks[5], (d_model, d_mem), jnp.float32) * s, 'Wo': jax.random.normal(ks[6], (d_model, d_model), jnp.float32) * s, 'gate_w1': jax.random.normal(ks[7], (dg, d_model + d_mem), jnp.float32) * s, 'gate_b1': jnp.zeros((dg,), jnp.float32), 'gate_w2': jax.random.normal(ks[8], (1, dg), jnp.float32) * s, 'gate_b2': jnp.zeros((1,), jnp.float32), 'ent_w': jax.random.normal(ks[9], (1, d_model), jnp.float32) * s, 'ent_b': jnp.zeros((1,), jnp.float32), 'ln_scale': jnp.ones((d_model,), jnp.float32), 'ln_bias': jnp.zeros((d_model,), jnp.float32), 'mem_pos_embed': jax.random.normal(ks[10], (1, 64, d_model), jnp.float32) * s}
    _L0_xattn_all = _L0_xattn_setup()
    _L0_xattn_in = {k: v for k, v in _L0_xattn_all.items() if k in ('Wq', 'Wk', 'Wv', 'Wo', 'gate_w1', 'gate_b1', 'gate_w2', 'gate_b2', 'ent_w', 'ent_b', 'ln_scale', 'ln_bias', 'mem_pos_embed')}
    del _L0_xattn_all

    def _L1_xattn_setup():
        import jax, jax.numpy as jnp
        import numpy as np
        QUERY_DIM = 128
        KEY_DIM = 64
        HIDDEN_DIM = 128
        B, LQ, LK = (8, 256, 256)
        key = jax.random.key(seed)
        ks = jax.random.split(key, 10)
        s_q = 1.0 / np.sqrt(QUERY_DIM)
        s_k = 1.0 / np.sqrt(KEY_DIM)
        s_h = 1.0 / np.sqrt(HIDDEN_DIM)
        return {'query': jax.random.normal(ks[0], (B, LQ, QUERY_DIM), jnp.float32), 'key': jax.random.normal(ks[1], (B, LK, KEY_DIM), jnp.float32), 'Wq': jax.random.uniform(ks[2], (QUERY_DIM, HIDDEN_DIM), jnp.float32, -s_q, s_q), 'bq': jax.random.uniform(ks[3], (HIDDEN_DIM,), jnp.float32, -s_q, s_q), 'Wk': jax.random.uniform(ks[4], (KEY_DIM, HIDDEN_DIM), jnp.float32, -s_k, s_k), 'bk': jax.random.uniform(ks[5], (HIDDEN_DIM,), jnp.float32, -s_k, s_k), 'Wv': jax.random.uniform(ks[6], (KEY_DIM, HIDDEN_DIM), jnp.float32, -s_k, s_k), 'bv': jax.random.uniform(ks[7], (HIDDEN_DIM,), jnp.float32, -s_k, s_k), 'Wo': jax.random.uniform(ks[8], (HIDDEN_DIM, QUERY_DIM), jnp.float32, -s_h, s_h), 'bo': jax.random.uniform(ks[9], (QUERY_DIM,), jnp.float32, -s_h, s_h)}
    _L1_xattn_all = _L1_xattn_setup()
    _L1_xattn_in = {k: v for k, v in _L1_xattn_all.items() if k in ('Wq', 'bq', 'Wk', 'bk', 'Wv', 'bv', 'Wo', 'bo')}
    del _L1_xattn_all

    def _L2_xattn_setup():
        import jax, jax.numpy as jnp
        import numpy as np
        B, ST, SS = (8, 64, 72)
        TD, SD = (128, 64)
        L, H, D, FF = (6, 16, 64, 512)

        def _ln(x, g, b, eps=1e-05):
            m = jnp.mean(x, axis=-1, keepdims=True)
            v = jnp.mean(jnp.square(x - m), axis=-1, keepdims=True)
            return (x - m) / jnp.sqrt(v + eps) * g + b

        def _heads(x):
            b, s, _ = x.shape
            return x.reshape(b, s, H, D).transpose(0, 2, 1, 3)

        def _mha(s, t, kv_w, q_w, o_w, o_b, mask):
            kv = s @ kv_w
            k, v = jnp.split(kv, 2, axis=-1)
            q = t @ q_w
            k, v, q = (_heads(k), _heads(v), _heads(q))
            scores = jnp.einsum('bhqd,bhkd->bhqk', q, k) * D ** (-0.5)
            scores = jnp.where(mask[:, None] == 0, jnp.float32(-1000000000.0), scores)
            attn = jax.nn.softmax(scores, axis=-1)
            o = jnp.einsum('bhqk,bhkd->bhqd', attn, v)
            o = o.transpose(0, 2, 1, 3).reshape(t.shape[0], t.shape[1], H * D)
            return o @ o_w + o_b
        key = jax.random.key(seed)
        ks = jax.random.split(key, 18)
        sc = 0.02
        inp = {'src': jax.random.normal(ks[0], (B, SS, SD), jnp.float32), 'tgt': jax.random.normal(ks[1], (B, ST, TD), jnp.float32), 'tgt_mask': jnp.broadcast_to(jnp.tril(jnp.ones((ST, ST), jnp.int32)), (B, ST, ST)), 'src_mask': jnp.ones((B, 1, SS), jnp.int32), 'norm_g': jnp.ones((TD,), jnp.float32), 'norm_b': jnp.zeros((TD,), jnp.float32), 'sa_kv': jax.random.normal(ks[2], (L, TD, 2 * H * D), jnp.float32) * sc, 'sa_q': jax.random.normal(ks[3], (L, TD, H * D), jnp.float32) * sc, 'sa_ow': jax.random.normal(ks[4], (L, H * D, TD), jnp.float32) * sc, 'sa_ob': jnp.zeros((L, TD), jnp.float32), 'ca_kv': jax.random.normal(ks[5], (L, SD, 2 * H * D), jnp.float32) * sc, 'ca_q': jax.random.normal(ks[6], (L, TD, H * D), jnp.float32) * sc, 'ca_ow': jax.random.normal(ks[7], (L, H * D, TD), jnp.float32) * sc, 'ca_ob': jnp.zeros((L, TD), jnp.float32), 'ff_w1': jax.random.normal(ks[8], (L, TD, FF), jnp.float32) * sc, 'ff_b1': jnp.zeros((L, FF), jnp.float32), 'ff_w2': jax.random.normal(ks[9], (L, FF, TD), jnp.float32) * sc, 'ff_b2': jnp.zeros((L, TD), jnp.float32), 'pre_g': jnp.ones((L, TD), jnp.float32), 'pre_b': jnp.zeros((L, TD), jnp.float32)}
        return inp
    _L2_xattn_all = _L2_xattn_setup()
    _L2_xattn_in = {k: v for k, v in _L2_xattn_all.items() if k in ('norm_g', 'norm_b', 'sa_kv', 'sa_q', 'sa_ow', 'sa_ob', 'ca_kv', 'ca_q', 'ca_ow', 'ca_ob', 'ff_w1', 'ff_b1', 'ff_w2', 'ff_b2', 'pre_g', 'pre_b')}
    del _L2_xattn_all

    def _L3_xattn_setup():
        import jax, jax.numpy as jnp
        import numpy as np
        B, T, E = (8, 512, 128)
        M, L = (32, 64)
        EPS = 1e-06
        key = jax.random.key(seed)
        ks = jax.random.split(key, 5)
        return {'emb': jax.random.normal(ks[0], (B, T, E), dtype=jnp.float32), 'latent': jax.random.normal(ks[1], (B, M, L), dtype=jnp.float32), 'Wq': jax.random.normal(ks[2], (E, E), dtype=jnp.float32) * (1.0 / np.sqrt(E)), 'bq': jnp.zeros((E,), dtype=jnp.float32), 'Wk': jax.random.normal(ks[3], (L, E), dtype=jnp.float32) * (1.0 / np.sqrt(L)), 'bk': jnp.zeros((E,), dtype=jnp.float32), 'Wv': jax.random.normal(ks[4], (L, E), dtype=jnp.float32) * (1.0 / np.sqrt(L)), 'bv': jnp.zeros((E,), dtype=jnp.float32), 'gamma': jnp.ones((E,), dtype=jnp.float32), 'beta': jnp.zeros((E,), dtype=jnp.float32)}
    _L3_xattn_all = _L3_xattn_setup()
    _L3_xattn_in = {k: v for k, v in _L3_xattn_all.items() if k in ('Wq', 'bq', 'Wk', 'bk', 'Wv', 'bv', 'gamma', 'beta')}
    del _L3_xattn_all
    return {'x': x, 'ctx_512': ctx_512, 'mask_BxSxS_ik0': mask_BxSxS_ik0, 'mask_Bx1xS2_if1': mask_Bx1xS2_if1, 'L0_xattn_Wq': _L0_xattn_in['Wq'], 'L0_xattn_Wk': _L0_xattn_in['Wk'], 'L0_xattn_Wv': _L0_xattn_in['Wv'], 'L0_xattn_Wo': _L0_xattn_in['Wo'], 'L0_xattn_gate_w1': _L0_xattn_in['gate_w1'], 'L0_xattn_gate_b1': _L0_xattn_in['gate_b1'], 'L0_xattn_gate_w2': _L0_xattn_in['gate_w2'], 'L0_xattn_gate_b2': _L0_xattn_in['gate_b2'], 'L0_xattn_ent_w': _L0_xattn_in['ent_w'], 'L0_xattn_ent_b': _L0_xattn_in['ent_b'], 'L0_xattn_ln_scale': _L0_xattn_in['ln_scale'], 'L0_xattn_ln_bias': _L0_xattn_in['ln_bias'], 'L0_xattn_mem_pos_embed': _L0_xattn_in['mem_pos_embed'], 'L1_xattn_Wq': _L1_xattn_in['Wq'], 'L1_xattn_bq': _L1_xattn_in['bq'], 'L1_xattn_Wk': _L1_xattn_in['Wk'], 'L1_xattn_bk': _L1_xattn_in['bk'], 'L1_xattn_Wv': _L1_xattn_in['Wv'], 'L1_xattn_bv': _L1_xattn_in['bv'], 'L1_xattn_Wo': _L1_xattn_in['Wo'], 'L1_xattn_bo': _L1_xattn_in['bo'], 'L2_xattn_norm_g': _L2_xattn_in['norm_g'], 'L2_xattn_norm_b': _L2_xattn_in['norm_b'], 'L2_xattn_sa_kv': _L2_xattn_in['sa_kv'], 'L2_xattn_sa_q': _L2_xattn_in['sa_q'], 'L2_xattn_sa_ow': _L2_xattn_in['sa_ow'], 'L2_xattn_sa_ob': _L2_xattn_in['sa_ob'], 'L2_xattn_ca_kv': _L2_xattn_in['ca_kv'], 'L2_xattn_ca_q': _L2_xattn_in['ca_q'], 'L2_xattn_ca_ow': _L2_xattn_in['ca_ow'], 'L2_xattn_ca_ob': _L2_xattn_in['ca_ob'], 'L2_xattn_ff_w1': _L2_xattn_in['ff_w1'], 'L2_xattn_ff_b1': _L2_xattn_in['ff_b1'], 'L2_xattn_ff_w2': _L2_xattn_in['ff_w2'], 'L2_xattn_ff_b2': _L2_xattn_in['ff_b2'], 'L2_xattn_pre_g': _L2_xattn_in['pre_g'], 'L2_xattn_pre_b': _L2_xattn_in['pre_b'], 'L3_xattn_Wq': _L3_xattn_in['Wq'], 'L3_xattn_bq': _L3_xattn_in['bq'], 'L3_xattn_Wk': _L3_xattn_in['Wk'], 'L3_xattn_bk': _L3_xattn_in['bk'], 'L3_xattn_Wv': _L3_xattn_in['Wv'], 'L3_xattn_bv': _L3_xattn_in['bv'], 'L3_xattn_gamma': _L3_xattn_in['gamma'], 'L3_xattn_beta': _L3_xattn_in['beta']}

def reference(x, ctx_512, mask_BxSxS_ik0, mask_Bx1xS2_if1, L0_xattn_Wq, L0_xattn_Wk, L0_xattn_Wv, L0_xattn_Wo, L0_xattn_gate_w1, L0_xattn_gate_b1, L0_xattn_gate_w2, L0_xattn_gate_b2, L0_xattn_ent_w, L0_xattn_ent_b, L0_xattn_ln_scale, L0_xattn_ln_bias, L0_xattn_mem_pos_embed, L1_xattn_Wq, L1_xattn_bq, L1_xattn_Wk, L1_xattn_bk, L1_xattn_Wv, L1_xattn_bv, L1_xattn_Wo, L1_xattn_bo, L2_xattn_norm_g, L2_xattn_norm_b, L2_xattn_sa_kv, L2_xattn_sa_q, L2_xattn_sa_ow, L2_xattn_sa_ob, L2_xattn_ca_kv, L2_xattn_ca_q, L2_xattn_ca_ow, L2_xattn_ca_ob, L2_xattn_ff_w1, L2_xattn_ff_b1, L2_xattn_ff_w2, L2_xattn_ff_b2, L2_xattn_pre_g, L2_xattn_pre_b, L3_xattn_Wq, L3_xattn_bq, L3_xattn_Wk, L3_xattn_bk, L3_xattn_Wv, L3_xattn_bv, L3_xattn_gamma, L3_xattn_beta):
    import jax
    import jax.numpy as jnp

    def _L0_xattn_ref(hidden_states, memory_vectors, memory_keys, Wq, Wk, Wv, Wo, gate_w1, gate_b1, gate_w2, gate_b2, ent_w, ent_b, ln_scale, ln_bias, mem_pos_embed):
        import jax, jax.numpy as jnp
        import numpy as np
        ENTROPY_THRESHOLD = 1.0
        N_HEADS = 16
        LN_EPS = 1e-05

        def _layernorm(x, scale, bias):
            mu = jnp.mean(x, axis=-1, keepdims=True)
            var = jnp.mean(jnp.square(x - mu), axis=-1, keepdims=True)
            return (x - mu) * jax.lax.rsqrt(var + LN_EPS) * scale + bias
        B, L, d_model = hidden_states.shape
        M = memory_vectors.shape[1]
        H = N_HEADS
        D = d_model // H
        scale = D ** (-0.5)
        logits = jnp.einsum('bld,od->blo', hidden_states, ent_w)[..., 0] + ent_b[0]
        aw = jax.nn.softmax(logits, axis=-1)
        entropy = -jnp.sum(aw * jnp.log(aw + 1e-09), axis=-1)
        read_mask = entropy > ENTROPY_THRESHOLD
        q = jnp.einsum('bld,ed->ble', hidden_states, Wq).reshape(B, L, H, D).transpose(0, 2, 1, 3)
        k = jnp.einsum('bmd,ed->bme', memory_keys, Wk).reshape(B, M, H, D).transpose(0, 2, 1, 3)
        v = jnp.einsum('bmd,ed->bme', memory_vectors, Wv).reshape(B, M, H, D).transpose(0, 2, 1, 3)
        pos = mem_pos_embed[:, :M, :].reshape(1, M, H, D).transpose(0, 2, 1, 3)
        k = k + pos
        scores = jnp.einsum('bhld,bhmd->bhlm', q, k) * scale
        attn = jax.nn.softmax(scores, axis=-1)
        attn_out = jnp.einsum('bhlm,bhmd->bhld', attn, v)
        attn_out = attn_out.transpose(0, 2, 1, 3).reshape(B, L, d_model)
        memory_output = jnp.einsum('ble,oe->blo', attn_out, Wo)
        pooled = jnp.mean(memory_vectors, axis=1, keepdims=True)
        pooled = jnp.broadcast_to(pooled, (B, L, pooled.shape[-1]))
        gate_in = jnp.concatenate([hidden_states, pooled], axis=-1)
        h1 = jax.nn.silu(jnp.einsum('blf,gf->blg', gate_in, gate_w1) + gate_b1)
        gate = jax.nn.sigmoid(jnp.einsum('blg,og->blo', h1, gate_w2) + gate_b2)
        enhanced = _layernorm(hidden_states + gate * memory_output, ln_scale, ln_bias)
        return jnp.where(read_mask[:, None, None], enhanced, hidden_states)

    def _L1_xattn_ref(query, key, Wq, bq, Wk, bk, Wv, bv, Wo, bo):
        import jax, jax.numpy as jnp
        import numpy as np
        QUERY_DIM = 128
        KEY_DIM = 64
        HIDDEN_DIM = 128
        B, LQ, LK = (8, 256, 256)
        scale = HIDDEN_DIM ** (-0.5)
        Q = jnp.einsum('bqd,dh->bqh', query, Wq) + bq
        K = jnp.einsum('bkd,dh->bkh', key, Wk) + bk
        V = jnp.einsum('bkd,dh->bkh', key, Wv) + bv
        scores = jnp.einsum('bqh,bkh->bqk', Q, K) * scale
        weights = jax.nn.softmax(scores, axis=-1)
        attended = jnp.einsum('bqk,bkh->bqh', weights, V)
        out = jnp.einsum('bqh,hd->bqd', attended, Wo) + bo
        return query + out

    def _L2_xattn_ref(src, tgt, tgt_mask, src_mask, norm_g, norm_b, sa_kv, sa_q, sa_ow, sa_ob, ca_kv, ca_q, ca_ow, ca_ob, ff_w1, ff_b1, ff_w2, ff_b2, pre_g, pre_b):
        import jax, jax.numpy as jnp
        import numpy as np
        B, ST, SS = (8, 64, 72)
        TD, SD = (128, 64)
        L, H, D, FF = (6, 16, 64, 512)

        def _ln(x, g, b, eps=1e-05):
            m = jnp.mean(x, axis=-1, keepdims=True)
            v = jnp.mean(jnp.square(x - m), axis=-1, keepdims=True)
            return (x - m) / jnp.sqrt(v + eps) * g + b

        def _heads(x):
            b, s, _ = x.shape
            return x.reshape(b, s, H, D).transpose(0, 2, 1, 3)

        def _mha(s, t, kv_w, q_w, o_w, o_b, mask):
            kv = s @ kv_w
            k, v = jnp.split(kv, 2, axis=-1)
            q = t @ q_w
            k, v, q = (_heads(k), _heads(v), _heads(q))
            scores = jnp.einsum('bhqd,bhkd->bhqk', q, k) * D ** (-0.5)
            scores = jnp.where(mask[:, None] == 0, jnp.float32(-1000000000.0), scores)
            attn = jax.nn.softmax(scores, axis=-1)
            o = jnp.einsum('bhqk,bhkd->bhqd', attn, v)
            o = o.transpose(0, 2, 1, 3).reshape(t.shape[0], t.shape[1], H * D)
            return o @ o_w + o_b
        stacked = (sa_kv, sa_q, sa_ow, sa_ob, ca_kv, ca_q, ca_ow, ca_ob, ff_w1, ff_b1, ff_w2, ff_b2, pre_g, pre_b)

        def step(t, p):
            skv, sq, sow, sob, ckv, cq, cow, cob, w1, b1, w2, b2, pg, pb = p
            tn = _ln(t, norm_g, norm_b)
            t = _mha(tn, tn, skv, sq, sow, sob, tgt_mask) + t
            tn = _ln(t, norm_g, norm_b)
            t = _mha(src, tn, ckv, cq, cow, cob, src_mask) + t
            tn = _ln(t, pg, pb)
            t = t + (jax.nn.relu(tn @ w1 + b1) @ w2 + b2)
            return (t, None)
        out, _ = jax.lax.scan(step, tgt, stacked)
        return out

    def _L3_xattn_ref(emb, latent, Wq, bq, Wk, bk, Wv, bv, gamma, beta):
        import jax, jax.numpy as jnp
        import numpy as np
        B, T, E = (8, 512, 128)
        M, L = (32, 64)
        EPS = 1e-06
        q = jnp.einsum('bte,ef->btf', emb, Wq) + bq
        k = jnp.einsum('bml,le->bme', latent, Wk) + bk
        v = jnp.einsum('bml,le->bme', latent, Wv) + bv
        scale = 1.0 / jnp.sqrt(jnp.asarray(E, dtype=q.dtype))
        w = jnp.einsum('bte,bme->btm', q, k) * scale
        w = jax.nn.softmax(w, axis=1)
        pred = jnp.einsum('btm,bme->bte', w, v)
        x = pred + emb
        mu = jnp.mean(x, axis=-1, keepdims=True)
        var = jnp.var(x, axis=-1, keepdims=True)
        return (x - mu) * jax.lax.rsqrt(var + EPS) * gamma + beta
    x = _L0_xattn_ref(x, ctx_512, ctx_512, L0_xattn_Wq, L0_xattn_Wk, L0_xattn_Wv, L0_xattn_Wo, L0_xattn_gate_w1, L0_xattn_gate_b1, L0_xattn_gate_w2, L0_xattn_gate_b2, L0_xattn_ent_w, L0_xattn_ent_b, L0_xattn_ln_scale, L0_xattn_ln_bias, L0_xattn_mem_pos_embed)
    x = _L1_xattn_ref(x, ctx_512, L1_xattn_Wq, L1_xattn_bq, L1_xattn_Wk, L1_xattn_bk, L1_xattn_Wv, L1_xattn_bv, L1_xattn_Wo, L1_xattn_bo)
    x = _L2_xattn_ref(ctx_512, x, mask_BxSxS_ik0, mask_Bx1xS2_if1, L2_xattn_norm_g, L2_xattn_norm_b, L2_xattn_sa_kv, L2_xattn_sa_q, L2_xattn_sa_ow, L2_xattn_sa_ob, L2_xattn_ca_kv, L2_xattn_ca_q, L2_xattn_ca_ow, L2_xattn_ca_ob, L2_xattn_ff_w1, L2_xattn_ff_b1, L2_xattn_ff_w2, L2_xattn_ff_b2, L2_xattn_pre_g, L2_xattn_pre_b)
    x = _L3_xattn_ref(x, ctx_512, L3_xattn_Wq, L3_xattn_bq, L3_xattn_Wk, L3_xattn_bk, L3_xattn_Wv, L3_xattn_bv, L3_xattn_gamma, L3_xattn_beta)
    return x

_drawn_inputs = setup_inputs


def setup_inputs(seed=0):
    import zlib

    import numpy as np

    out = dict(_drawn_inputs(seed))
    spreads = {'L0_xattn_gate_b1': (0.0, 0.8),
     'L0_xattn_ln_scale': (1.0, 0.2),
     'L0_xattn_ln_bias': (0.0, 0.1),
     'L2_xattn_norm_g': (1.0, 0.6),
     'L2_xattn_norm_b': (0.0, 0.1),
     'L2_xattn_sa_ob': (0.0, 0.1),
     'L2_xattn_ca_ob': (0.0, 0.1),
     'L2_xattn_ff_b1': (0.0, 0.1),
     'L2_xattn_ff_b2': (0.0, 0.1),
     'L2_xattn_pre_g': (1.0, 0.2),
     'L2_xattn_pre_b': (0.0, 0.558),
     'L3_xattn_bq': (0.0, 2.0),
     'L3_xattn_bk': (0.0, 0.546),
     'L3_xattn_bv': (0.0, 0.341),
     'L3_xattn_gamma': (1.0, 0.2),
     'L3_xattn_beta': (0.0, 0.1)}
    factors = {'L0_xattn_Wq': 8.0,
     'L0_xattn_Wk': 8.0,
     'L0_xattn_Wv': 5.873,
     'L0_xattn_Wo': 6.089,
     'L0_xattn_gate_w1': 8.0,
     'L0_xattn_gate_w2': 8.0,
     'L0_xattn_mem_pos_embed': 8.0,
     'L1_xattn_bq': 29.457,
     'L1_xattn_bk': 64.0,
     'L2_xattn_sa_q': 8.0,
     'L2_xattn_ca_q': 23.139}
    for name, (base, spread) in spreads.items():
        noise = np.random.default_rng([zlib.crc32(name.encode()), seed]).standard_normal(out[name].shape)
        drawn = base * np.exp(spread * noise) if base else spread * noise
        out[name] = jnp.asarray(drawn.astype(out[name].dtype))
    for name, factor in factors.items():
        out[name] = (out[name] * factor).astype(out[name].dtype)
    return out
```

```python
from contextlib import ExitStack

import numpy as np
import concourse.bass as bass
from concourse import mybir

F32 = mybir.dt.float32
F32R = mybir.dt.float32r
BF16 = mybir.dt.bfloat16
I32 = mybir.dt.int32
ALU = mybir.AluOpType
ACT = mybir.ActivationFunctionType
AX = mybir.AxisListType

NB, SEQ, DM = 8, 256, 128
NCTX, DC = 64, 64
TOK = NB * SEQ
NT = TOK // 128
NLAYER, NH, HD, FF = 6, 16, 64, 512
NHP = NH // 2
CK = NB * NCTX
H0 = 16
NG, GT = 4, 4
GTOK = GT * 128
NEG = -float(2 ** 33)
BIG = 3.0e38

COLS = ["gate_b1", "gate_b2", "ent_b", "l1_bq", "l1_bk", "l1_bv", "l3_bq", "l3_bk", "norm_g", "norm_b"]
COL = {n: i for i, n in enumerate(COLS)}
PRE_G, PRE_B, FFB = len(COLS), len(COLS) + NLAYER, len(COLS) + 2 * NLAYER
NCOL = FFB + NLAYER * 4
ROWS = ["ln_scale", "ln_bias", "l1_bo"]
ROWS3 = ["l3_bv", "l3_gamma", "l3_beta"]
ROW = {n: i for r in (ROWS, ROWS3) for i, n in enumerate(r)}
SMALL = [("wq0", 128, 128), ("wk0T", 64, 128), ("wv0", 128, 64), ("wo0T", 128, 128), ("pos0T", 128, 64),
         ("g1x", 128, 64), ("g1p", 64, 64), ("g2", 64, 1), ("entw", 128, 1),
         ("wq1", 128, 128), ("wk1", 64, 128), ("wv1", 64, 128), ("wo1", 128, 128)]
SMALL3 = [("wq3", 128, 128), ("wk3", 64, 128), ("wv3", 64, 128)]


def offsets(parts):
    at, out = 0, {}
    for name, rows, n in parts:
        out[name] = (at, rows, n)
        at += n
    return out, at


class Queues:

    def __init__(self, names):
        self.work = {n: [] for n in names}
        self.count = {}
        self.waited = {n: {} for n in names}

    def put(self, engine, call, after=(), signal=True, by=1, sem=None):
        waits = []
        for s, v in flat(after):
            if v > self.waited[engine].get(s, 0):
                self.waited[engine][s] = v
                waits = [w for w in waits if w[0] != s] + [(s, v)]
        sem = sem or engine
        if signal:
            self.count[sem] = self.count.get(sem, 0) + by
        self.work[engine].append((waits, call, sem if signal else None, by))
        return (sem, self.count.get(sem, 0))

    def run(self, engine, handle, sems):
        for waits, call, sem, by in self.work[engine]:
            for s, v in waits:
                handle.wait_ge(sems[s], v)
            ins = call(handle)
            if sem:
                ins.then_inc(sems[sem], by)


def flat(after):
    if isinstance(after, tuple) and len(after) == 2 and isinstance(after[0], str):
        return [after]
    out = []
    for a in after:
        out += flat(a)
    return out


class Ring:

    def __init__(self, views):
        self.views, self.freed, self.at = views, [[] for _ in views], 0
        self.held = [False] * len(views)

    def take(self):
        while self.held[self.at]:
            self.at = (self.at + 1) % len(self.views)
        i = self.at
        self.held[i] = True
        self.at = (i + 1) % len(self.views)
        return i, self.views[i], self.freed[i]

    def free(self, i, after):
        self.freed[i], self.held[i] = flat(after), False


def decoder_kernel(nc, A, out):
    q = Queues(["pe", "act", "dve", "pool", "sp"])
    ctx = ExitStack()
    with ctx:
        def sb(name, shape, dt=F32):
            return ctx.enter_context(nc.sbuf_tensor(name, shape, dt))

        def mm(o, l, r, start=True, stop=True, after=(), signal=False):
            return q.put("pe", lambda e: e.matmul(o, l, r, start=start, stop=stop), after, signal)

        def mm3(o, l, r, after=(), signal=False, more=False):
            mm(o, l[0], r[0], True, False, after)
            mm(o, l[0], r[1], False, False)
            return mm(o, l[1], r[0], False, not more, (), signal)

        def tr(o, i, after=(), signal=False):
            return q.put("pe", lambda e: e.transpose(o, i, ident[:, :]), after, signal)

        def act(o, i, f=ACT.Copy, bias=0.0, scale=1.0, accum=None, after=()):
            if f == ACT.Copy:
                return q.put("act", lambda e: e.copy(o, i), after)
            if accum is None:
                return q.put("act", lambda e: e.activation(o, i, f, bias=bias, scale=scale), after)
            return q.put("act", lambda e: e.activation(o, i, f, bias=bias, scale=scale, accum_out=accum), after)

        def copy(eng, o, i, after=()):
            if eng == "act":
                return act(o, i, after=after)
            return q.put(eng, lambda e: e.tensor_copy(o, i), after)

        def tt(eng, o, a, b, op, after=()):
            return q.put(eng, lambda e: e.tensor_tensor(o, a, b, op), after)

        def ts(eng, o, a, s1, s2, op0, op1=None, after=()):
            if op1 is None:
                return q.put(eng, lambda e: e.tensor_scalar(o, a, s1, None, op0), after)
            return q.put(eng, lambda e: e.tensor_scalar(o, a, s1, s2, op0, op1), after)

        def stt(o, a, s, b, op0, op1, after=()):
            return q.put("dve", lambda e: e.scalar_tensor_tensor(out=o, in0=a, scalar=s, in1=b, op0=op0, op1=op1), after)

        def red(o, i, op, after=()):
            return q.put("dve", lambda e: e.tensor_reduce(o, i, AX.X, op), after)

        def recip(o, i, after=()):
            return q.put("dve", lambda e: e.reciprocal(o, i), after)

        def fill(eng, o, v, after=()):
            return q.put(eng, lambda e: e.memset(o, v), after)

        def load(o, i, group, after=()):
            return q.put("sp", lambda e: e.dma_start(o, i), after, by=16, sem="ld_" + group)

        t = sb("t", [128, NT, DM])
        tn_hi = sb("tn_hi", [128, TOK], F32R)
        tn_lo = sb("tn_lo", [128, TOK], F32R)
        maskb = sb("maskb", [128, NT, SEQ], BF16)
        big_hi = sb("big_hi", [128, 8192], F32R)
        big_lo = sb("big_lo", [128, 8192], F32R)
        vals = sb("vals", [128, 8192])
        ag_hi = sb("ag_hi", [128, 2048], F32R)
        ag_lo = sb("ag_lo", [128, 2048], F32R)
        wv_hi = sb("wv_hi", [128, 1024], F32R)
        wv_lo = sb("wv_lo", [128, 1024], F32R)
        w1_hi, w1_lo = wv_hi[:, 0:FF], wv_lo[:, 0:FF]
        wo = sb("wo", [128, NHP, DM])
        w2 = wo[:, 0:4, :]
        stage = sb("stage", [128, 3072])
        ctxT = stage[:, 2560:3072]
        uHH = sb("uHH", [128, CK + NCTX], F32R)
        uLL = sb("uLL", [128, CK + NCTX], F32R)
        mHH = sb("mHH", [128, CK], F32R)
        mLL = sb("mLL", [128, CK], F32R)
        work = sb("work", [128, 4, 1024])
        pt = sb("pt", [128, 2, 1024])
        ident = sb("ident", [128, 128])
        cols = sb("cols", [128, NCOL])
        rows = sb("rows", [128, len(ROWS), DM])
        lrows = sb("lrows", [128, 3, DM])
        rowscale = sb("rowscale", [128, NT])
        maskrow = sb("maskrow", [1, CK], BF16)
        ones = sb("ones", [1, 128], BF16)
        hmask = sb("hmask", [128, H0])
        st = sb("st", [128, 2, GT, 6])
        mv = sb("mv", [128, 2, GT, 2])
        ve = sb("ve", [128, 2, 3, GT])
        nmx = sb("nmx", [128, 4, 4])
        den = sb("den", [128, 4, 4])
        rden = sb("rden", [128, 4, 4])
        cmx = sb("cmx", [128, 3, 16])
        csum = sb("csum", [128, 3, 16])
        crec = sb("crec", [128, 3, 16])
        gate = sb("gate", [128, NT])
        rmask = sb("rmask", [128, NB])
        rinv = sb("rinv", [128, NB])
        psums = [ctx.enter_context(nc.psum_tensor(f"ps{i}", [128, 512], F32)) for i in range(8)]
        bank = Ring(psums)
        slot = Ring([work[:, i, :] for i in range(4)])
        ptslot = Ring([pt[:, i, :] for i in range(2)])
        smslot = Ring(list(range(4)))
        csslot = Ring(list(range(3)))
        lnslot = Ring(list(range(2)))
        vals_free = [[] for _ in range(4)]
        tn_free = [[] for _ in range(NG)]
        tn_ready = [None] * NG
        t_ready = [[] for _ in range(NT)]

        def f(ap):
            return ap.bitcast(F32)

        def col(name):
            return cols[:, COL[name]:COL[name] + 1]

        def split(i, hi, lo, bank_after, release=None):
            a = act(hi, i, after=bank_after)
            return tt("dve", lo, i, f(hi), ALU.subtract, after=[a])

        S = {}

        so, n_small = offsets(SMALL)
        so3, n_small3 = offsets(SMALL3)

        def small(name, o=so):
            at, r, n = o[name]
            return stage[0:r, at:at + n]

        load(stage[:, 0:n_small], A["small"], "in")
        load(ctxT[0:64, :], A["ctxT"], "in")
        load(ctxT[64:128, :], A["ctxT"], "in")
        load(cols[:, :], A["cols"], "in")
        load(hmask[:, :], A["hmask"], "in")
        load(rows[:, :, :], A["rows"].rearrange("(o r) d -> o r d", o=1).to_broadcast([128, len(ROWS), DM]), "in")
        loaded = load(ident[:, :], A["ident"], "in")
        xT = vals[:, 0:TOK]
        loaded_xT = load(xT, A["xT"], "xT")
        mi = pt[:, 0, 0:CK].bitcast(I32)
        loaded_m2 = load(mi, A["mask2"].rearrange("(o k) -> o k", o=1).to_broadcast([128, CK]), "m2")
        loaded_x = load(t[:, :, :], A["x"].rearrange("(n p) d -> p n d", p=128), "x")
        for n in range(NT):
            t_ready[n] = [loaded_x]

        ones_set = fill("pool", ones[:, :], 1.0)

        m01 = ts("dve", pt[:, 1, 0:CK], mi, 0.0, None, ALU.not_equal, after=[loaded_m2])
        mrow = ts("dve", maskrow[0:1, :], mi[0:1, :], 0.0, NEG, ALU.is_equal, ALU.mult, after=[loaded_m2])
        cm = tt("dve", pt[:, 0, 512:1024], ctxT, pt[:, 1, 0:CK], ALU.mult, after=[m01, loaded])
        a = act(mHH[:, :], pt[:, 0, 512:1024], after=[cm])
        m_parts = tt("dve", mLL[:, :], pt[:, 0, 512:1024], f(mHH[:, :]), ALU.subtract, after=[a])
        u_parts = []
        for dst, src in ((slice(0, CK), slice(0, CK)), (slice(CK, CK + NCTX), slice(0, NCTX))):
            a = act(uHH[:, dst], ctxT[:, src], after=[loaded])
            u_parts.append(tt("dve", uLL[:, dst], ctxT[:, src], f(uHH[:, dst]), ALU.subtract, after=[a]))

        mask_v = A["mask"].rearrange("(n p) k -> p n k", p=128)
        for g in range(NG):
            i, buf, freed = slot.take()
            raw = buf.bitcast(I32).rearrange("p (n k) -> p n k", n=GT)
            l = load(raw, mask_v[:, GT * g:GT * g + GT, :], f"mask{g}", after=freed)
            m = ts("dve", maskb[:, GT * g:GT * g + GT, :], raw, 0.0, NEG, ALU.is_equal, ALU.mult, after=[l])
            slot.free(i, m)
            r = red(rowscale[:, GT * g:GT * g + GT], maskb[:, GT * g:GT * g + GT, :], ALU.max, after=[m])
            mask_ready = ts("dve", rowscale[:, GT * g:GT * g + GT], rowscale[:, GT * g:GT * g + GT], 0.0, -0.125,
                            ALU.is_equal, ALU.mult, after=[r])

        for g in range(NG):
            s = slice(GTOK * g, GTOK * g + GTOK)
            a = act(tn_hi[:, s], xT[:, s], after=[loaded_xT])
            tn_ready[g] = tt("pool", tn_lo[:, s], xT[:, s], f(tn_hi[:, s]), ALU.subtract, after=[a])

        entw = pt[:, 1, 512:512 + NB * NB].rearrange("p (b c) -> p b c", b=NB)
        z = fill("dve", entw, 0.0)
        for b in range(NB):
            z2 = copy("dve", entw[:, b, b:b + 1], small("entw"), after=[z, loaded])
        i, ps, freed = bank.take()
        for b in range(NB):
            last = mm(ps[0:NB, 0:SEQ], entw[:, b, :], xT[:, SEQ * b:SEQ * b + SEQ], b == 0, b == NB - 1,
                      after=[freed, z2, loaded_xT], signal=(b == NB - 1))
        j, buf, freed = slot.take()
        e_l, e_p, e_g = buf[0:NB, 0:256], buf[0:NB, 256:512], buf[0:NB, 512:768]
        e_s = buf[0:NB, 768:800]
        k = ts("dve", e_l, ps[0:NB, 0:SEQ], cols[0:NB, COL["ent_b"]:COL["ent_b"] + 1], None, ALU.add,
               after=[freed, last])
        bank.free(i, k)
        ptslot.free(0, [m_parts, mrow])
        ptslot.free(1, [cm, last])
        k = red(e_s[:, 0:1], e_l, ALU.max, after=[k])
        k = ts("dve", e_l, e_l, e_s[:, 0:1], None, ALU.subtract, after=[k])
        k = act(e_p, e_l, ACT.Exp, accum=e_s[:, 1:2], after=[k])
        k = recip(e_s[:, 2:3], e_s[:, 1:2], after=[k])
        k = ts("dve", e_p, e_p, e_s[:, 2:3], None, ALU.mult, after=[k])
        k2 = ts("dve", e_l, e_p, 1e-9, None, ALU.add, after=[k])
        k = act(e_g, e_l, ACT.Ln, after=[k2])
        k = tt("dve", e_g, e_g, e_p, ALU.mult, after=[k])
        k = red(e_s[:, 3:4], e_g, ALU.add, after=[k])
        k = ts("dve", e_s[:, 4:5], e_s[:, 3:4], -1.0, None, ALU.is_lt, after=[k])
        k = ts("dve", e_s[:, 8:16], ident[0:NB, 0:NB], e_s[:, 4:5], None, ALU.mult, after=[k])
        o8 = fill("pool", buf[0:NB, 896:1024], 1.0, after=[freed])
        i, ps, freed = bank.take()
        k = mm(ps[:, 0:NB], buf[0:NB, 896:1024], e_s[:, 8:16], after=[freed, k, o8], signal=True)
        k = copy("dve", rmask[:, :], ps[:, 0:NB], after=[k])
        bank.free(i, k)
        slot.free(j, k)
        rm_ready = ts("dve", rinv[:, :], rmask[:, :], -1.0, 1.0, ALU.mult, ALU.add, after=[k])

        j, buf, jfreed = slot.take()
        pooled, gbias = buf[0:64, 0:NB], buf[0:64, 8:16]
        k = red(pooled, ctxT[0:64, :].rearrange("c (b k) -> c b k", b=NB), ALU.add, after=[jfreed, loaded])
        k = ts("dve", pooled, pooled, 1.0 / NCTX, None, ALU.mult, after=[k])
        i, ps, freed = bank.take()
        k = mm(ps[0:64, 0:NB], small("g1p"), pooled, after=[freed, k], signal=True)
        k = ts("dve", gbias, ps[0:64, 0:NB], cols[0:64, COL["gate_b1"]:COL["gate_b1"] + 1], None, ALU.add, after=[k])
        bank.free(i, k)
        gi, gps, gfreed = bank.take()
        used = []
        for g in range(NG):
            i, ps, freed = bank.take()
            m = mm(ps[0:64, :], small("g1x"), xT[:, GTOK * g:GTOK * g + GTOK], after=[freed, loaded_xT], signal=True)
            zb, sg = buf[0:64, 16:16 + GTOK // 2], buf[0:64, 300:300 + GTOK // 2]
            for b in range(2):
                c = slice(SEQ * b, SEQ * b + SEQ)
                za = ts("dve", zb, ps[0:64, c], gbias[:, 2 * g + b:2 * g + b + 1], None, ALU.add, after=[m, k, used])
                a = act(sg, zb, ACT.Sigmoid, after=[za, used])
                h = tt("dve", zb, zb, sg, ALU.mult, after=[a])
                for n in range(2):
                    c2 = GT * g + 2 * b + n
                    last = mm(gps[:, c2:c2 + 1], zb[:, 128 * n:128 * n + 128], small("g2"), after=[h, gfreed], signal=True)
                used = [last]
            bank.free(i, za)
        gate_ready = act(gate[:, :], gps[:, 0:NT], ACT.Sigmoid, bias=col("gate_b2"), after=[used])
        bank.free(gi, gate_ready)
        slot.free(j, [used, h])
        xT_read = [used, tn_ready]

        C_hi = big_hi[:, :].rearrange("p (b h k) -> p b h k", b=NB, h=NH)
        C_lo = big_lo[:, :].rearrange("p (b h k) -> p b h k", b=NB, h=NH)
        Vp = vals[:, :].rearrange("p (b h d) -> p b h d", b=NB, h=NHP)
        big_free = []

        def values_through(H, after, free_of):
            ready = []
            for b in range(NB):
                for par in range(2):
                    for half in range(2):
                        i, ps, freed = bank.take()
                        r = H[:, 1024 * par + 512 * half:1024 * par + 512 * half + 512]
                        at = NCTX * ((b - par) % NB)
                        for n, part in enumerate((uHH, uLL)):
                            l = part[:, at:at + 2 * NCTX]
                            m = mm(ps[:, :], l, r, n == 0, n == 1, after=[freed, after, u_parts], signal=(n == 1))
                        p = slice(64 * par, 64 * par + 64)
                        e = copy("act" if half else "dve",
                                 Vp[p, b, 4 * half:4 * half + 4, :],
                                 ps[p, :].rearrange("p (h d) -> p h d", h=4), after=[m, free_of(b)])
                        bank.free(i, e)
                        ready.append(e)
            return ready

        def store_stack(ps, dst, m, after):
            a = act(dst, ps[:, :], after=[m, after])
            return tt("dve", dst[64:128, :], ps[64:128, :], f(dst[64:128, :]), ALU.subtract, after=[a])

        def cross_tiles(tiles, scale, c_ready, v_ready, masked, finish, parts=(tn_hi, tn_lo)):
            state = {}

            def scores(n):
                b = n // 2
                cs = slice(128 * n, 128 * n + 128)
                j, P, pfreed = slot.take()
                x, _, xfreed = csslot.take()
                subs = []
                for half in range(2):
                    i, ps, freed = bank.take()
                    hs = slice(8 * half, 8 * half + 8)
                    l = (parts[0][:, cs], parts[1][:, cs])
                    r = (C_hi[:, b, hs, :], C_lo[:, b, hs, :])
                    m = mm3(ps[:, :], l, r, after=[freed, c_ready, tn_ready[n // GT]], signal=not masked, more=masked)
                    if masked:
                        mr = maskrow[0:1, NCTX * b:NCTX * b + NCTX].unsqueeze(1).to_broadcast([1, 8, NCTX])
                        m = mm(ps[:, :], ones[:, :], mr, False, True, after=[mrow, ones_set], signal=True)
                    v = ps[:, :].rearrange("p (h k) -> p h k", h=8)
                    k = red(cmx[:, x, hs], v, ALU.max, after=[m, xfreed])
                    k = tt("dve", P[:, 512 * half:512 * half + 512].rearrange("p (h k) -> p h k", h=8), v,
                           cmx[:, x, hs].unsqueeze(2).to_broadcast([128, 8, NCTX]), ALU.subtract, after=[k, pfreed])
                    bank.free(i, k)
                    subs.append(k)
                state[n] = [j, P, x, m]
                a = act(P, P, ACT.Exp, scale=scale, after=[subs])
                P3 = P.rearrange("p (h k) -> p h k", h=NH)
                k = red(csum[:, x, :], P3, ALU.add, after=[a])
                k = recip(crec[:, x, :], csum[:, x, :], after=[k])
                state[n].append(tt("pool", P3, P3, crec[:, x, :].unsqueeze(2).to_broadcast([128, NH, NCTX]),
                                   ALU.mult, after=[k]))
                csslot.free(x, state[n][4])
                return m

            def output(n):
                j, P, x, _, p_ready = state.pop(n)
                y, T, tfreed = ptslot.take()
                ev = []
                for half in range(2):
                    i, ps, freed = bank.take()
                    for c in range(4):
                        m = tr(ps[:, 128 * c:128 * c + 128], P[:, 512 * half + 128 * c:512 * half + 128 * c + 128],
                               after=[freed, p_ready], signal=(c == 3))
                    ev.append(copy("act", T[:, 512 * half:512 * half + 512], ps[:, :],
                                   after=[m, tfreed]))
                    bank.free(i, ev[-1])
                slot.free(j, m)
                i, ps, freed = bank.take()
                for hp in range(NHP):
                    m = mm(ps[:, 0:DM], T[:, 128 * hp:128 * hp + 128], Vp[:, n // 2, hp, :], hp == 0, hp == NHP - 1,
                           after=[freed, ev, v_ready], signal=(hp == NHP - 1))
                ptslot.free(y, m)
                bank.free(i, finish(n, ps[:, 0:DM], m))
                return m

            last = s = None
            for n in list(tiles) + [None]:
                if n is not None:
                    s = scores(n)
                    tn_free[n // GT] = [s]
                if last is not None:
                    o = output(last)
                last = n
            return s, o

        i, ps, freed = bank.take()
        m = mm(ps[:, :], small("wk0T"), ctxT[0:64, :], after=[freed, loaded], signal=True)
        kT0 = stage[:, 2048:2560]
        k = tt("dve", kT0.rearrange("p (b k) -> p b k", b=NB), ps[:, :].rearrange("p (b k) -> p b k", b=NB),
               small("pos0T").unsqueeze(1).to_broadcast([128, NB, NCTX]), ALU.add, after=[m])
        bank.free(i, k)
        y, WM, tfreed = ptslot.take()
        j, WM2, jfreed = slot.take()
        wm_ready = []
        for h in range(H0):
            w = ts("pool", (WM if h < 8 else WM2)[:, 128 * (h % 8):128 * (h % 8) + 128], small("wq0"), hmask[:, h:h + 1], None,
                   ALU.mult, after=[tfreed, jfreed, loaded])
            wm_ready.append(w)
        c_ready = []
        for h in range(H0):
            i, ps, freed = bank.take()
            m = mm(ps[:, :], (WM if h < 8 else WM2)[:, 128 * (h % 8):128 * (h % 8) + 128], kT0,
                   after=[freed, wm_ready[h], k], signal=True)
            v = ps[:, :].rearrange("p (b k) -> p b k", b=NB)
            s = split(v, C_hi[:, :, h, :], C_lo[:, :, h, :], [m])
            bank.free(i, s)
            c_ready = [s]
        ptslot.free(y, m)
        slot.free(j, m)
        h_ready = []
        for par in range(2):
            for half in range(2):
                j, buf, jfreed = slot.take()
                for c in range(4):
                    h = par + 2 * (4 * half + c)
                    w = ts("pool", buf[:, 128 * c:128 * c + 128], small("wo0T"), hmask[:, h:h + 1], None, ALU.mult,
                           after=[jfreed, loaded])
                i, ps, freed = bank.take()
                for twice in range(2):
                    m = mm(ps[64 * twice:64 * twice + 64, :], small("wv0"), buf[:, 0:512], after=[freed, w], signal=True)
                slot.free(j, m)
                k = store_stack(ps, ag_lo[:, 1024 * par + 512 * half:1024 * par + 512 * half + 512], m, [])
                bank.free(i, k)
                h_ready.append(k)
        v_ready = values_through(ag_lo, h_ready, lambda b: xT_read)
        ag_used = [("pe", q.count["pe"])]

        def statistics(srcs, x, eps, after):
            n = len(srcs)
            for c, src in enumerate(srcs):
                k = q.put("dve", bn_call(st[:, x, c, :], src), [after[c]])
            for c in range(n):
                k2 = q.put("dve", aggr_call(mv[:, x, c, :], st[:, x, c, :]), [k])
            v, y, w = ve[:, x, 0, 0:n], ve[:, x, 1, 0:n], ve[:, x, 2, 0:n]
            k = ts("dve", v, mv[:, x, 0:n, 1], eps, None, ALU.add, after=[k2])
            a = act(y, v, ACT.Ln, after=[k])
            a = act(y, y, ACT.Exp, scale=-0.5, after=[a])
            k = tt("dve", w, v, y, ALU.mult, after=[a])
            k = tt("dve", w, w, y, ALU.mult, after=[k])
            k = ts("dve", w, w, -0.5, 1.5, ALU.mult, ALU.add, after=[k])
            return tt("dve", mv[:, x, 0:n, 1], w, y, ALU.mult, after=[k])

        def finish0(n, ps, m):
            b = n // 2
            j, buf, jfreed = slot.take()
            x, _, xfreed = lnslot.take()
            h = buf[:, 0:DM]
            r = stt(h, ps, gate[:, n:n + 1], t[:, n, :], ALU.mult, ALU.add, after=[m, jfreed, gate_ready, t_ready[n]])
            k = statistics([h], x, 1e-5, [[r, xfreed]])
            k = ts("dve", h, h, mv[:, x, 0, 0:1], mv[:, x, 0, 1:2], ALU.subtract, ALU.mult, after=[k])
            lnslot.free(x, k)
            k = tt("pool", h, h, rows[:, ROW["ln_scale"], :], ALU.mult, after=[k, loaded])
            k = tt("pool", h, h, rows[:, ROW["ln_bias"], :], ALU.add, after=[k])
            k = ts("dve", h, h, rmask[:, b:b + 1], None, ALU.mult, after=[k, rm_ready])
            k = stt(t[:, n, :], t[:, n, :], rinv[:, b:b + 1], h, ALU.mult, ALU.add, after=[k])
            slot.free(j, k)
            t_ready[n] = [k]
            return r

        s, o = cross_tiles(range(NT), float(DM // H0) ** -0.5, c_ready, v_ready, False, finish0)
        big_free = [s]
        for g in range(NG):
            tn_free[g] = [s]
            vals_free[g] = [o]

        tT, q1 = vals[:, 0:TOK], vals[:, TOK:2 * TOK]
        for g in range(NG):
            i, ps, freed = bank.take()
            for c in range(GT):
                n = GT * g + c
                m = tr(ps[:, 128 * c:128 * c + 128], t[:, n, :], after=[freed, t_ready[n]], signal=(c == GT - 1))
            e = copy("act", tT[:, GTOK * g:GTOK * g + GTOK], ps[:, :], after=[m, vals_free])
            bank.free(i, e)
            i, ps, freed = bank.take()
            m = mm(ps[:, :], small("wq1"), tT[:, GTOK * g:GTOK * g + GTOK], after=[freed, e], signal=True)
            q1_ready = act(q1[:, GTOK * g:GTOK * g + GTOK], ps[:, :], ACT.Identity, bias=col("l1_bq"), after=[m])
            bank.free(i, q1_ready)
        k1, v1 = vals[:, 2 * TOK:2 * TOK + CK], vals[:, 2 * TOK + CK:2 * TOK + 2 * CK]
        vw = vals[:, 2 * TOK + 2 * CK:2 * TOK + 3 * CK].rearrange("p (a d) -> p a d", a=NB // 2)
        kv_ready = []
        for w, b_, dst in (("wk1", "l1_bk", k1), ("wv1", "l1_bv", v1)):
            i, ps, freed = bank.take()
            m = mm(ps[:, :], small(w), ctxT[0:64, :], after=[freed], signal=True)
            e = act(dst, ps[:, :], ACT.Identity, bias=col(b_), after=[m, vals_free])
            bank.free(i, e)
            kv_ready.append(e)
        i, ps, freed = bank.take()
        for a in range(NB // 2):
            m = mm(ps[:, DM * a:DM * a + DM], v1[:, 128 * a:128 * a + 128], small("wo1"), after=[freed, kv_ready],
                   signal=(a == NB // 2 - 1))
        vw_ready = copy("act", vw, ps[:, :].rearrange("p (a d) -> p a d", a=NB // 2), after=[m])
        bank.free(i, vw_ready)
        zp = vals[:, 3 * TOK:4 * TOK].rearrange("p (n c) -> p n c", n=NT)
        zero = fill("pool", zp, 0.0, after=[vals_free])
        for half in range(2):
            i, ps, freed = bank.take()
            for c in range(8):
                n = 8 * half + c
                m = mm(ps[:, 64 * c:64 * c + 64], q1[:, 128 * n:128 * n + 128], k1[:, NCTX * (n // 2):NCTX * (n // 2) + NCTX],
                       after=[freed, q1_ready, kv_ready], signal=(c == 7))
            j, buf, jfreed = slot.take()
            x, _, xfreed = csslot.take()
            v = ps[:, :].rearrange("p (n k) -> p n k", n=8)
            P3 = buf[:, 0:512].rearrange("p (n k) -> p n k", n=8)
            k = red(cmx[:, x, 0:8], v, ALU.max, after=[m, xfreed])
            k = tt("dve", P3, v, cmx[:, x, 0:8].unsqueeze(2).to_broadcast([128, 8, NCTX]), ALU.subtract, after=[k, jfreed])
            bank.free(i, k)
            k = act(P3, P3, ACT.Exp, scale=float(DM) ** -0.5, after=[k])
            k = red(csum[:, x, 0:8], P3, ALU.add, after=[k])
            k = recip(crec[:, x, 0:8], csum[:, x, 0:8], after=[k])
            k = tt("pool", P3, P3, crec[:, x, 0:8].unsqueeze(2).to_broadcast([128, 8, NCTX]), ALU.mult, after=[k])
            csslot.free(x, k)
            put = []
            for par in range(2):
                src = P3.rearrange("p (a b2 c) k -> p a b2 c k", a=2, b2=2)[:, :, par, :, :]
                dst = zp[:, 8 * half:8 * half + 8, :].rearrange("p (a b2 c) k -> p a b2 c k", a=2, b2=2)[:, :, par, :, 64 * par:64 * par + 64]
                put.append(copy("dve", dst, src, after=[k, zero]))
            slot.free(j, put)
            for a in range(2):
                i, ps, freed = bank.take()
                for c in range(4):
                    n = 8 * half + 4 * a + c
                    m = tr(ps[:, 128 * c:128 * c + 128], zp[:, n, :], after=[freed, put], signal=(c == 3))
                y, T, tfreed = ptslot.take()
                e = copy("act", T[:, 0:512], ps[:, :], after=[m, tfreed])
                bank.free(i, e)
                i, ps, freed = bank.take()
                for c in range(4):
                    n = 8 * half + 4 * a + c
                    m = mm(ps[:, 128 * c:128 * c + 128], T[:, 128 * c:128 * c + 128], vw[:, n // 4, :],
                           after=[freed, e, vw_ready], signal=(c == 3))
                ptslot.free(y, m)
                n = 8 * half + 4 * a
                tv = t[:, n:n + 4, :]
                k = tt("dve", tv, ps[:, :].rearrange("p (n d) -> p n d", n=4), tv, ALU.add, after=[m, t_ready[n:n + 4]])
                bank.free(i, k)
                k = tt("pool", tv, tv, rows[:, ROW["l1_bo"], :].unsqueeze(1).to_broadcast([128, 4, DM]), ALU.add, after=[k])
                for c in range(4):
                    t_ready[n + c] = [k]
        vals_free = [[m]] * 4
        stage_free = [(n, q.count[n]) for n in ("pe", "pool", "dve")]

        def load_bias(l, r, after):
            S["lrows", r] = load(lrows[:, r, :], A["lrows"][l, r:r + 1, :].to_broadcast([128, DM]), f"bias{r}", after)

        def layer_norm(g, gcol, bcol, l, r):
            j, buf, jfreed = slot.take()
            x, _, xfreed = lnslot.take()
            xs = []
            k = statistics([t[:, GT * g + c, :] for c in range(GT)], x, 1e-5,
                           [[xfreed, t_ready[GT * g + c]] for c in range(GT)])
            for c in range(GT):
                n = GT * g + c
                xs.append(ts("dve", buf[:, 128 * c:128 * c + 128], t[:, n, :], mv[:, x, c, 0:1], mv[:, x, c, 1:2],
                             ALU.subtract, ALU.mult, after=[k, jfreed]))
            lnslot.free(x, xs)
            tv = t[:, GT * g:GT * g + GT, :]
            k = tt("pool", tv, tv, lrows[:, r, :].unsqueeze(1).to_broadcast([128, GT, DM]), ALU.add,
                   after=[S["lrows", r], xs])
            for n in range(GT * g, GT * g + GT):
                t_ready[n] = [k]
            if g == NG - 1 and l + 1 < NLAYER:
                load_bias(l + 1, r, k)

            def transposed():
                i, ps, freed = bank.take()
                for c in range(GT):
                    m = tr(ps[:, 128 * c:128 * c + 128], buf[:, 128 * c:128 * c + 128], after=[freed, xs[c]],
                           signal=(c == GT - 1))
                s = slice(GTOK * g, GTOK * g + GTOK)
                full = buf[:, 512:1024]
                a = act(full, ps[:, :], ACT.Identity, bias=bcol, scale=gcol, after=[m, jfreed])
                bank.free(i, a)
                h = act(tn_hi[:, s], full, after=[a, tn_free[g]])
                k = tt("pool", tn_lo[:, s], full, f(tn_hi[:, s]), ALU.subtract, after=[h])
                slot.free(j, [k, h])
                tn_ready[g] = k
            return transposed

        w_hi = big_hi[:, :].rearrange("p (c b h k) -> p c b h k", c=NHP, b=2, h=2)
        w_lo = big_lo[:, :].rearrange("p (c b h k) -> p c b h k", c=NHP, b=2, h=2)
        V = vals[:, 0:4096].rearrange("p (n e) -> p n e", n=GT)
        oT = vals[:, 4096:8192].rearrange("p (b h k) -> p b h k", b=2, h=NHP)
        def load_self(l, after):
            load(stage[:, 0:1024], A["wqT"][l], "self", after)
            load(stage[:, 1024:2048], A["wkT"][l], "self", after)
            return load(stage[:, 2048:3072], A["wv"][l], "self", after)

        def load_cross(l, after):
            load(stage[:, 0:1024], A["cqT"][l], "cross", after)
            load(stage[:, 1024:1536], A["ckT"][l], "cross", after)
            load(stage[:, 1536:2048], A["cvT"][l], "cross", after)
            return load(stage[:, 2048:3072], A["co"][l], "cross", after)

        def value_weights(got, wv_free):
            a = act(wv_hi[:, :], stage[:, 2048:3072], after=[got, wv_free])
            k = tt("pool", wv_lo[:, :], stage[:, 2048:3072], f(wv_hi[:, :]), ALU.subtract, after=[a])
            return [a, k]

        def self_weights(got, ag_free):
            qT = stage[:, 0:1024].rearrange("p (c d) -> p c d", c=NHP)
            kT = stage[:, 1024:2048].rearrange("p (c d) -> p c d", c=NHP)
            ready = []
            for half in range(2):
                for par in range(2):
                    i, ps, freed = bank.take()
                    p = slice(64 * par, 64 * par + 64)
                    for c in range(4):
                        m = mm(ps[:, 128 * c:128 * c + 128], kT[p, 4 * half + c, :], qT[p, 4 * half + c, :],
                               after=[freed, got], signal=(c == 3))
                    at = slice(1024 * half + 512 * par, 1024 * half + 512 * par + 512)
                    s = split(ps[:, :], ag_hi[:, at], ag_lo[:, at], [m, ag_free])
                    bank.free(i, s)
                    ready.append(s)
            return ready, m

        def a_slice(h):
            hp, par = h // 2, h % 2
            at = 1024 * (hp // 4) + 512 * par + 128 * (hp % 4)
            return ag_hi[:, at:at + 128], ag_lo[:, at:at + 128]

        def w_project(g, hp, after):
            s = slice(GTOK * g, GTOK * g + GTOK)
            ready = []
            for par in range(2):
                i, ps, freed = bank.take()
                m = mm3(ps[:, :], a_slice(2 * hp + par), (tn_hi[:, s], tn_lo[:, s]),
                        after=[freed, S["A"], tn_ready[g]], signal=True)
                v = ps[:, :].rearrange("p (b k) -> p b k", b=2)
                k = split(v, w_hi[:, hp, :, par, :], w_lo[:, hp, :, par, :], [m, after])
                bank.free(i, k)
                ready.append(k)
            S["tn_read", g] = m
            return ready

        def v_project(g, half, after):
            for n in range(GT):
                i, ps, freed = bank.take()
                cs = slice(GTOK * g + 128 * n, GTOK * g + 128 * n + 128)
                es = slice(512 * half, 512 * half + 512)
                m = mm3(ps[:, :], (tn_hi[:, cs], tn_lo[:, cs]), (wv_hi[:, es], wv_lo[:, es]),
                        after=[freed, S["Wv"], tn_ready[g]], signal=True)
                e = copy("dve" if n % 2 else "act", V[:, n, es], ps[:, :], after=[m, after])
                bank.free(i, e)
                S["V", half, n] = e
            S["wv_used"] = m
            S["tn_read2", g] = m

        def unit_scores(g, hp, b):
            j, P, pfreed = slot.take()
            x, _, xfreed = smslot.take()
            P4 = P.rearrange("p (a h k) -> p a h k", a=2, h=2)
            ex = []
            for a in range(2):
                n = GT * g + 2 * b + a
                i, ps, freed = bank.take()
                cs = slice(128 * n, 128 * n + 128)
                m = mm3(ps[:, :], (tn_hi[:, cs], tn_lo[:, cs]), (w_hi[:, hp, b, :, :], w_lo[:, hp, b, :, :]),
                        after=[freed, S["w", hp], tn_ready[g]], signal=True)
                for h in range(2):
                    c = 2 * a + h
                    o_, i_, m_, s_, x_ = P4[:, a, h, :], ps[:, 256 * h:256 * h + 256], maskb[:, n, :], rowscale[:, n:n + 1], nmx[:, x, c:c + 1]
                    k = ttr(o_, i_, m_, s_, x_, [m, pfreed, xfreed, mask_ready])
                    e = act(P4[:, a, h, :], P4[:, a, h, :], ACT.Exp, bias=x_, scale=-1.0, accum=den[:, x, c:c + 1], after=[k])
                    ex.append(e)
                bank.free(i, k)
            r = recip(rden[:, x, :], den[:, x, :], after=[ex])
            pn = []
            for a in range(2):
                pn.append(tt("pool", P4[:, a, :, :], P4[:, a, :, :],
                             rden[:, x, 2 * a:2 * a + 2].unsqueeze(2).to_broadcast([128, 2, SEQ]), ALU.mult, after=[r]))
            smslot.free(x, pn)
            S["scores_read"] = m
            return j, P4, pn

        def ttr(o, i, m, s, acc, after):
            return q.put("dve", lambda e: e.tensor_tensor_reduce(o, i, m, s, BIG, ALU.add, ALU.min, acc), after)

        def unit_transpose(u):
            j, P4, pn = u
            y, T, tfreed = ptslot.take()
            ev = []
            for h in range(2):
                i, ps, freed = bank.take()
                for kt in range(2):
                    for a in range(2):
                        m = tr(ps[:, 256 * kt + 128 * a:256 * kt + 128 * a + 128], P4[:, a, h, 128 * kt:128 * kt + 128],
                               after=[freed, pn[a]], signal=(kt == 1 and a == 1))
                ev.append(copy("dve" if h else "act", T[:, 512 * h:512 * h + 512], ps[:, :], after=[m, tfreed]))
                bank.free(i, ev[-1])
            slot.free(j, m)
            return y, T, ev

        def unit_values(g, hp, b, u):
            y, T, ev = u
            i, ps, freed = bank.take()
            for kt in range(2):
                for h in range(2):
                    e = slice(64 * (2 * hp + h), 64 * (2 * hp + h) + 64)
                    m = mm(ps[64 * h:64 * h + 64, 0:SEQ], V[:, 2 * b + kt, e], T[:, 512 * h + 256 * kt:512 * h + 256 * kt + 256],
                           kt == 0, kt == 1, after=[freed, ev[h], S["V", hp // 4, 2 * b + kt]], signal=(kt == 1))
            ptslot.free(y, m)
            S["v_used", hp // 4] = m
            k = copy("act", oT[:, b, hp, :], ps[:, 0:SEQ], after=[m, S["oT_free"]])
            bank.free(i, k)
            S["oT", b, hp] = k

        def out_project(g):
            for b in range(2):
                i, ps, freed = bank.take()
                for a in range(2):
                    for hp in range(NHP):
                        m = mm(ps[:, 128 * a:128 * a + 128], oT[:, b, hp, 128 * a:128 * a + 128], wo[:, hp, :],
                               hp == 0, hp == NHP - 1, after=[freed, S["oT", b, hp], S["Wo"]],
                               signal=(a == 1 and hp == NHP - 1))
                n = GT * g + 2 * b
                tv = t[:, n:n + 2, :]
                k = tt("dve", tv, ps[:, 0:256].rearrange("p (n d) -> p n d", n=2), tv, ALU.add, after=[m, t_ready[n], t_ready[n + 1]])
                bank.free(i, k)
                t_ready[n] = t_ready[n + 1] = [k]
            S["oT_free"] = m

        def norm_later(g, l):
            def first(n):
                rest = layer_norm(g, *norm, l, 1)
                return [(n + 1, lambda n: rest())]
            return first

        got = load_self(0, stage_free)
        S["A"], a_read = self_weights(got, ag_used)
        S["Wv"] = value_weights(got, [])
        staged = [a_read, S["Wv"]]
        S["Wo"] = load(wo[:, :, :], A["wo"][0].rearrange("p (c d) -> p c d", c=NHP), "wo")
        for r in range(3):
            load_bias(0, r, [])
        norm = (col("norm_g"), col("norm_b"))
        for g in range(NG):
            layer_norm(g, *norm, 0, 0)()
        w_free = {hp: big_free for hp in range(NHP)}
        units = [(g, hp, b) for g in range(NG) for hp in range(NHP) for b in range(2)]
        for l in range(NLAYER):
            got_cross = load_cross(l, staged)
            S["oT_free"] = vals_free[2:4]
            for hp in range(NHP):
                S["w", hp] = w_project(0, hp, w_free[hp])
            v_project(0, 0, vals_free[0:2])
            v_project(0, 1, vals_free[0:2])
            scored, due = {}, []
            for n in range(len(units) + 2):
                moved = None
                if n >= 2:
                    moved = unit_transpose(scored.pop(n - 2))
                for d in [d for d in due if d[0] <= n]:
                    due.remove(d)
                    due += d[1](n) or []
                if n < len(units):
                    g, hp, b = units[n]
                    scored[n] = unit_scores(g, hp, b)
                    if b == 1:
                        w_free[hp] = [S["scores_read"]]
                        S["tn_units", g] = S["scores_read"]
                        if g + 1 < NG:
                            S["w", hp] = w_project(g + 1, hp, w_free[hp])
                if n >= 2:
                    g, hp, b = units[n - 2]
                    unit_values(g, hp, b, moved)
                    if b == 1 and hp == 3 and g + 1 < NG:
                        v_project(g + 1, 0, [S["v_used", 0]])
                    if b == 1 and hp == NHP - 1:
                        if g + 1 < NG:
                            v_project(g + 1, 1, [S["v_used", 1]])
                        out_project(g)
                        tn_free[g] = [S["tn_units", g], S["tn_read", g], S["tn_read2", g]]
                        if g + 1 < NG:
                            due.append((n + 1, norm_later(g, l)))
            vals_free = [[S["v_used", 0], S["v_used", 1], S["oT_free"]]] * 4
            ag_free = [S["tn_read", NG - 1]]
            qT = stage[:, 0:1024].rearrange("p (c d) -> p c d", c=NHP)
            kT = stage[:, 1024:1536].rearrange("p (c d) -> p c d", c=NHP)
            vT = stage[:, 1536:2048].rearrange("p (c d) -> p c d", c=NHP)
            co = stage[:, 2048:3072].rearrange("p (c d) -> p c d", c=NHP)
            done = {}
            ln_rest = layer_norm(NG - 1, *norm, l, 1)
            for what, lhs, rhs, dst in (("G", kT, qT, ag_hi), ("H", vT, co, ag_lo)):
                done[what] = []
                for par in range(2):
                    for half in range(2):
                        i, ps, freed = bank.take()
                        p = slice(64 * par, 64 * par + 64)
                        for c in range(4):
                            for o in range(2):
                                m = mm(ps[64 * o:64 * o + 64, 128 * c:128 * c + 128], lhs[p, 4 * half + c, :],
                                       rhs[p, 4 * half + c, :], after=[freed, got_cross], signal=(c == 3 and o == 1))
                        at = slice(1024 * par + 512 * half, 1024 * par + 512 * half + 512)
                        k = store_stack(ps, dst[:, at], m, ag_free)
                        bank.free(i, k)
                        done[what].append(k)
            ln_rest()
            staged = [m]
            if l + 1 < NLAYER:
                got = load_self(l + 1, staged)
            c_ready = []
            for h in range(NH):
                par, hp = h % 2, h // 2
                i, ps, freed = bank.take()
                G = ag_hi[:, 1024 * par + 128 * hp:1024 * par + 128 * hp + 128]
                mm(ps[:, :], G, mHH[:, :], True, False, after=[freed, done["G"], m_parts])
                m = mm(ps[:, :], G, mLL[:, :], False, True, signal=True)
                v = ps[:, :].rearrange("p (b k) -> p b k", b=NB)
                k = split(v, C_hi[:, :, h, :], C_lo[:, :, h, :], [m, list(w_free.values())])
                bank.free(i, k)
                c_ready = [k]
            v_ready = values_through(ag_lo, done["H"], lambda b: vals_free[b // 2])
            ag_free = [("pe", q.count["pe"])]
            if l + 1 < NLAYER:
                S["A"], a_read = self_weights(got, ag_free)
            j, buf, jfreed = slot.take()
            got1 = load(buf[:, 0:FF], A["w1"][l], "w1", after=[jfreed])
            got2 = load(w2, A["w2"][l].rearrange("p (c d) -> p c d", c=4), "w2", after=[S["oT_free"]])
            a = act(w1_hi, buf[:, 0:FF], after=[got1, S["wv_used"]])
            w1_ready = tt("pool", w1_lo, buf[:, 0:FF], f(w1_hi), ALU.subtract, after=[a])
            slot.free(j, [w1_ready, a])

            def finish2(n, ps, m):
                k = tt("dve", t[:, n, :], ps, t[:, n, :], ALU.add, after=[m, t_ready[n]])
                t_ready[n] = [k]
                return k

            hT = vals[:, :].rearrange("p (g c k) -> p g c k", g=NG, c=4)

            def feed_forward(g, free):
                s = slice(GTOK * g, GTOK * g + GTOK)
                ev = []
                for c in range(4):
                    i, ps, freed = bank.take()
                    cs = slice(128 * c, 128 * c + 128)
                    m = mm3(ps[:, :], (w1_hi[:, cs], w1_lo[:, cs]), (tn_hi[:, s], tn_lo[:, s]),
                            after=[freed, w1_ready, tn_ready[g]], signal=True)
                    bc = cols[:, FFB + 4 * l + c:FFB + 4 * l + c + 1]
                    ev.append(act(hT[:, g, c, :], ps[:, :], ACT.Relu, bias=bc, after=[m, free]))
                    bank.free(i, ev[-1])
                tn_free[g] = S["w1_used"] = [m]
                i, ps, freed = bank.take()
                for a in range(GT):
                    for c in range(4):
                        m = mm(ps[:, 128 * a:128 * a + 128], hT[:, g, c, 128 * a:128 * a + 128], w2[:, c, :],
                               c == 0, c == 3, after=[freed, ev[c], got2], signal=(a == GT - 1 and c == 3))
                tv = t[:, GT * g:GT * g + GT, :]
                k = tt("dve", tv, ps[:, :].rearrange("p (n d) -> p n d", n=GT), tv, ALU.add,
                       after=[m, t_ready[GT * g:GT * g + GT]])
                bank.free(i, k)
                for n in range(GT * g, GT * g + GT):
                    t_ready[n] = [k]
                vals_free[g] = [m]
                S["w2_used"] = [m]

            vals_free = [[]] * 4
            vals_free = list(vals_free)
            for g in range(NG + 1):
                if g < NG:
                    s, o = cross_tiles(range(GT * g, GT * g + GT), 0.125, c_ready, v_ready, True, finish2)
                    tn_free[g] = [s]
                    S["vp", g] = o
                    S["c_used"] = s
                    rest = layer_norm(g, cols[:, PRE_G + l:PRE_G + l + 1], cols[:, PRE_B + l:PRE_B + l + 1], l, 2)
                if g >= 1:
                    feed_forward(g - 1, [S["vp", g - 1]])
                if g < NG:
                    rest()
                if g >= 1 and l + 1 < NLAYER:
                    layer_norm(g - 1, *norm, l + 1, 0)()
            w_free = {hp: [S["c_used"]] for hp in range(NHP)}
            if l + 1 < NLAYER:
                S["Wv"] = value_weights(got, S["w1_used"])
                staged = [a_read, S["Wv"]]
                S["Wo"] = load(wo[:, :, :], A["wo"][l + 1].rearrange("p (c d) -> p c d", c=NHP), "wo", S["w2_used"])

        load(rows[:, :, :], A["rows3"].rearrange("(o r) d -> o r d", o=1).to_broadcast([128, len(ROWS3), DM]), "last")
        load(ctxT[0:64, :], A["ctxT"], "last", staged)
        got = load(stage[:, 0:n_small3], A["small3"], "last", staged)
        qT3, kT3 = vals[:, 0:TOK], vals[:, 3 * TOK:3 * TOK + CK]
        tT = vals[:, TOK:2 * TOK]
        v3 = vals[:, 3 * TOK + CK:3 * TOK + 2 * CK].rearrange("p (a d) -> p a d", a=NB // 2)
        wT = vals[:, 2 * TOK:2 * TOK + 4 * SEQ].rearrange("p (a k) -> p a k", a=NB // 2)
        for g in range(NG):
            i, ps, freed = bank.take()
            for c in range(GT):
                n = GT * g + c
                m = tr(ps[:, 128 * c:128 * c + 128], t[:, n, :], after=[freed, t_ready[n]], signal=(c == GT - 1))
            e = copy("act", tT[:, GTOK * g:GTOK * g + GTOK], ps[:, :], after=[m, vals_free])
            bank.free(i, e)
            i, ps, freed = bank.take()
            m = mm(ps[:, :], small("wq3", so3), tT[:, GTOK * g:GTOK * g + GTOK], after=[freed, e, got], signal=True)
            q3_ready = act(qT3[:, GTOK * g:GTOK * g + GTOK], ps[:, :], ACT.Identity, bias=col("l3_bq"), after=[m])
            bank.free(i, q3_ready)
        i, ps, freed = bank.take()
        m = mm(ps[:, :], small("wk3", so3), ctxT[0:64, :], after=[freed, got], signal=True)
        k3_ready = act(kT3, ps[:, :], ACT.Identity, bias=col("l3_bk"), after=[m, vals_free])
        bank.free(i, k3_ready)
        i, ps, freed = bank.take()
        for a in range(NB // 2):
            m = mm(ps[:, DM * a:DM * a + DM], ctxT[0:64, 128 * a:128 * a + 128], small("wv3", so3), after=[freed, got],
                   signal=(a == NB // 2 - 1))
        v3_ready = tt("dve", v3, ps[:, :].rearrange("p (a d) -> p a d", a=NB // 2),
                      rows[:, ROW["l3_bv"], :].unsqueeze(1).to_broadcast([128, NB // 2, DM]), ALU.add, after=[m, vals_free, got])
        bank.free(i, v3_ready)
        stores = []
        out_v = out.rearrange("(n p) d -> p n d", p=128)
        for a in range(NB // 2):
            i, ps, freed = bank.take()
            for c in range(2):
                b = 2 * a + c
                m = mm(ps[64 * c:64 * c + 64, 0:SEQ], kT3[:, NCTX * b:NCTX * b + NCTX], qT3[:, SEQ * b:SEQ * b + SEQ],
                       after=[freed, q3_ready, k3_ready], signal=(c == 1))
            x, _, xfreed = csslot.take()
            k = red(cmx[:, x, 0:1], ps[:, 0:SEQ], ALU.max, after=[m, xfreed])
            k = ts("dve", cmx[:, x, 1:2], cmx[:, x, 0:1], -float(DM) ** -0.5, None, ALU.mult, after=[k])
            e = act(wT[:, a, :], ps[:, 0:SEQ], ACT.Exp, bias=cmx[:, x, 1:2], scale=float(DM) ** -0.5,
                    accum=csum[:, x, 0:1], after=[k])
            bank.free(i, e)
            k = recip(crec[:, x, 0:1], csum[:, x, 0:1], after=[e])
            k = ts("dve", v3[:, a, :], v3[:, a, :], crec[:, x, 0:1], None, ALU.mult, after=[k, v3_ready])
            csslot.free(x, k)
            j, buf, jfreed = slot.take()
            x, _, xfreed = lnslot.take()
            xs, rs = [], []
            for c in range(4):
                n = GT * a + c
                p = slice(64 * (c // 2), 64 * (c // 2) + 64)
                i, ps, freed = bank.take()
                m = mm(ps[:, 0:DM], wT[p, a, 128 * (c % 2):128 * (c % 2) + 128], v3[p, a, :], after=[freed, k, e],
                       signal=True)
                h = buf[:, DM * c:DM * c + DM]
                r = tt("dve", h, ps[:, 0:DM], t[:, n, :], ALU.add, after=[m, jfreed, t_ready[n]])
                bank.free(i, r)
                rs.append([r, xfreed])
            k = statistics([buf[:, DM * c:DM * c + DM] for c in range(4)], x, 1e-6, rs)
            for c in range(4):
                h = buf[:, DM * c:DM * c + DM]
                xs.append(ts("dve", h, h, mv[:, x, c, 0:1], mv[:, x, c, 1:2], ALU.subtract, ALU.mult, after=[k]))
            lnslot.free(x, xs)
            b3 = buf[:, 0:GT * DM].rearrange("p (n d) -> p n d", n=GT)
            k = tt("pool", b3, b3, rows[:, ROW["l3_gamma"], :].unsqueeze(1).to_broadcast([128, GT, DM]), ALU.mult, after=[xs])
            k = tt("pool", b3, b3, rows[:, ROW["l3_beta"], :].unsqueeze(1).to_broadcast([128, GT, DM]), ALU.add, after=[k])
            s = q.put("sp", store_call(out_v[:, GT * a:GT * a + GT, :], b3), [k], by=16, sem=f"store{a}")
            slot.free(j, s)
            stores.append(s)

        sems = {n: ctx.enter_context(nc.semaphore("s_" + n)) for n in q.count}
        block = ctx.enter_context(nc.Block())

        @block.tensor
        def _(e):
            q.run("pe", e, sems)

        @block.scalar
        def _(e):
            q.run("act", e, sems)

        @block.vector
        def _(e):
            q.run("dve", e, sems)

        @block.gpsimd
        def _(e):
            q.run("pool", e, sems)

        @block.sync
        def _(e):
            q.run("sp", e, sems)
            for s, v in stores:
                e.wait_ge(sems[s], v)


def bn_call(o, i):
    return lambda e: e.bn_stats(o, i)


def aggr_call(o, i):
    return lambda e: e.bn_aggr(o, i)


def store_call(o, i):
    return lambda e: e.dma_start(o, i)


def layout(inputs):
    g = {k: np.asarray(v) for k, v in inputs.items()}

    def c(a):
        return np.ascontiguousarray(a)

    def pack(parts, values):
        at, n = offsets(parts)
        a = np.zeros((128, n), np.float32)
        for name, rows, w in parts:
            o = at[name][0]
            a[0:rows, o:o + w] = values[name]
        return a

    def pairs(w):
        L, e, n = w.shape
        return c(w.reshape(L, e // 128, 128, n).transpose(0, 2, 1, 3).reshape(L, 128, e // 128 * n))

    E = NH * HD
    x = g["x"].reshape(TOK, DM)
    g1 = g["L0_xattn_gate_w1"]
    kv, ckv = g["L2_xattn_sa_kv"], g["L2_xattn_ca_kv"]
    A = {
        "x": c(x), "xT": c(x.T), "ctxT": c(g["ctx_512"].reshape(CK, DC).T),
        "mask": c(g["mask_BxSxS_ik0"].reshape(TOK, SEQ)), "mask2": c(g["mask_Bx1xS2_if1"].reshape(CK)),
        "small": pack(SMALL, {
            "wq0": g["L0_xattn_Wq"], "wk0T": g["L0_xattn_Wk"].T, "wv0": g["L0_xattn_Wv"], "wo0T": g["L0_xattn_Wo"].T,
            "pos0T": g["L0_xattn_mem_pos_embed"][0].T, "g1x": g1[:, :DM].T, "g1p": g1[:, DM:].T,
            "g2": g["L0_xattn_gate_w2"].T, "entw": g["L0_xattn_ent_w"].T,
            "wq1": g["L1_xattn_Wq"], "wk1": g["L1_xattn_Wk"], "wv1": g["L1_xattn_Wv"], "wo1": g["L1_xattn_Wo"]}),
        "small3": pack(SMALL3, {"wq3": g["L3_xattn_Wq"], "wk3": g["L3_xattn_Wk"], "wv3": g["L3_xattn_Wv"]}),
        "wqT": pairs(g["L2_xattn_sa_q"].transpose(0, 2, 1)), "wkT": pairs(kv[:, :, :E].transpose(0, 2, 1)),
        "wv": c(kv[:, :, E:]), "wo": pairs(g["L2_xattn_sa_ow"]),
        "cqT": pairs(g["L2_xattn_ca_q"].transpose(0, 2, 1)), "ckT": pairs(ckv[:, :, :E].transpose(0, 2, 1)),
        "cvT": pairs(ckv[:, :, E:].transpose(0, 2, 1)), "co": pairs(g["L2_xattn_ca_ow"]),
        "w1": c(g["L2_xattn_ff_w1"]), "w2": pairs(g["L2_xattn_ff_w2"]),
        "lrows": c(np.stack([g["L2_xattn_sa_ob"], g["L2_xattn_ca_ob"], g["L2_xattn_ff_b2"]], 1)),
        "rows": c(np.stack([g["L0_xattn_ln_scale"], g["L0_xattn_ln_bias"], g["L1_xattn_bo"]])),
        "rows3": c(np.stack([g["L3_xattn_bv"], g["L3_xattn_gamma"], g["L3_xattn_beta"]])),
        "ident": np.eye(128, dtype=np.float32),
        "hmask": c(np.repeat(np.eye(H0, dtype=np.float32), DM // H0, 0)),
    }
    cols = np.zeros((128, NCOL), np.float32)
    for name, v in (("gate_b1", g["L0_xattn_gate_b1"]), ("gate_b2", np.broadcast_to(g["L0_xattn_gate_b2"], 128)),
                    ("ent_b", np.broadcast_to(g["L0_xattn_ent_b"], 128)), ("l1_bq", g["L1_xattn_bq"]),
                    ("l1_bk", g["L1_xattn_bk"]), ("l1_bv", g["L1_xattn_bv"]), ("l3_bq", g["L3_xattn_bq"]),
                    ("l3_bk", g["L3_xattn_bk"]), ("norm_g", g["L2_xattn_norm_g"]), ("norm_b", g["L2_xattn_norm_b"])):
        cols[0:len(v), COL[name]] = v
    cols[:, PRE_G:PRE_G + NLAYER] = g["L2_xattn_pre_g"].T
    cols[:, PRE_B:PRE_B + NLAYER] = g["L2_xattn_pre_b"].T
    cols[:, FFB:] = g["L2_xattn_ff_b1"].reshape(NLAYER * 4, 128).T
    A["cols"] = cols
    return A


def kernel(**inputs):
    import concourse.bacc as bacc
    from concourse.bass_utils import run_bass_kernel_spmd

    nc = bacc.Bacc("TRN2", target_bir_lowering=False, num_devices=1)
    arrays = layout(inputs)
    aps = {n: nc.dram_tensor("in_" + n, a.shape, mybir.dt.from_np(a.dtype), kind="ExternalInput").ap()
           for n, a in arrays.items()}
    out = nc.dram_tensor("out", (TOK, DM), F32, kind="ExternalOutput").ap()
    decoder_kernel(nc, aps, out)
    r = run_bass_kernel_spmd(nc, [{"in_" + n: a for n, a in arrays.items()}], core_ids=[0])
    return r.results[0]["out"].reshape(NB, SEQ, DM)
```

```python
from contextlib import ExitStack

import numpy as np
import concourse.bass as bass
from concourse import mybir

F32 = mybir.dt.float32
F32R = mybir.dt.float32r
BF16 = mybir.dt.bfloat16
I32 = mybir.dt.int32
ALU = mybir.AluOpType
ACT = mybir.ActivationFunctionType
AX = mybir.AxisListType

NB, SEQ, DM = 8, 256, 128
NCTX, DC = 64, 64
TOK = NB * SEQ
NT = TOK // 128
NLAYER, NH, HD, FF = 6, 16, 64, 512
NHP = NH // 2
CK = NB * NCTX
H0 = 16
NG, GT = 4, 4
GTOK = GT * 128
NEG = -float(2 ** 33)
BIG = 3.0e38

COLS = ["gate_b1", "gate_b2", "ent_b", "l1_bq", "l1_bk", "l1_bv", "l3_bq", "l3_bk", "norm_g", "norm_b"]
COL = {n: i for i, n in enumerate(COLS)}
PRE_G, PRE_B, FFB = len(COLS), len(COLS) + NLAYER, len(COLS) + 2 * NLAYER
NCOL = FFB + NLAYER * 4
ROWS = ["ln_scale", "ln_bias", "l1_bo"]
ROWS3 = ["l3_bv", "l3_gamma", "l3_beta"]
ROW = {n: i for r in (ROWS, ROWS3) for i, n in enumerate(r)}
SMALL = [("wq0", 128, 128), ("wk0T", 64, 128), ("wv0", 128, 64), ("wo0T", 128, 128), ("pos0T", 128, 64),
         ("g1x", 128, 64), ("g1p", 64, 64), ("g2", 64, 1), ("entw", 128, 1),
         ("wq1", 128, 128), ("wk1", 64, 128), ("wv1", 64, 128), ("wo1", 128, 128)]
SMALL3 = [("wq3", 128, 128), ("wk3", 64, 128), ("wv3", 64, 128)]


def offsets(parts):
    at, out = 0, {}
    for name, rows, n in parts:
        out[name] = (at, rows, n)
        at += n
    return out, at


class Queues:

    def __init__(self, names):
        self.work = {n: [] for n in names}
        self.count = {}
        self.waited = {n: {} for n in names}

    def put(self, engine, call, after=(), signal=True, by=1, sem=None):
        waits = []
        for s, v in flat(after):
            if v > self.waited[engine].get(s, 0):
                self.waited[engine][s] = v
                waits = [w for w in waits if w[0] != s] + [(s, v)]
        sem = sem or engine
        if signal:
            self.count[sem] = self.count.get(sem, 0) + by
        self.work[engine].append((waits, call, sem if signal else None, by))
        return (sem, self.count.get(sem, 0))

    def run(self, engine, handle, sems):
        for waits, call, sem, by in self.work[engine]:
            for s, v in waits:
                handle.wait_ge(sems[s], v)
            ins = call(handle)
            if sem:
                ins.then_inc(sems[sem], by)


def flat(after):
    if isinstance(after, tuple) and len(after) == 2 and isinstance(after[0], str):
        return [after]
    out = []
    for a in after:
        out += flat(a)
    return out


class Ring:

    def __init__(self, views):
        self.views, self.at = views, 0
        self.freed, self.held = [[] for _ in views], [False] * len(views)

    def take(self):
        if all(self.held):
            raise ValueError("every buffer is held")
        while self.held[self.at]:
            self.at = (self.at + 1) % len(self.views)
        i = self.at
        self.held[i] = True
        self.at = (i + 1) % len(self.views)
        return i, self.views[i], self.freed[i]

    def free(self, i, after):
        self.freed[i], self.held[i] = flat(after), False


class Background:

    def __init__(self):
        self.chains = []

    def start(self, chain):
        self.chains.append(chain)

    def tick(self, times=1):
        for _ in range(times):
            for chain in list(self.chains):
                try:
                    next(chain)
                except StopIteration:
                    self.chains.remove(chain)

    def drain(self):
        while self.chains:
            self.tick()


def decoder_kernel(nc, A, out):
    q = Queues(["pe", "act", "dve", "pool", "sp"])
    ctx = ExitStack()
    with ctx:
        def sb(name, shape, dt=F32):
            return ctx.enter_context(nc.sbuf_tensor(name, shape, dt))

        def mm(o, l, r, start=True, stop=True, after=(), signal=False):
            return q.put("pe", lambda e: e.matmul(o, l, r, start=start, stop=stop), after, signal)

        def mm3(o, l, r, after=(), signal=False, more=False):
            mm(o, l[0], r[0], True, False, after)
            mm(o, l[0], r[1], False, False)
            return mm(o, l[1], r[0], False, not more, (), signal)

        def tr(o, i, after=(), signal=False):
            return q.put("pe", lambda e: e.transpose(o, i, ident[:, :]), after, signal)

        def act(o, i, f=ACT.Copy, bias=0.0, scale=1.0, accum=None, after=()):
            if f == ACT.Copy:
                return q.put("act", lambda e: e.copy(o, i), after)
            if accum is None:
                return q.put("act", lambda e: e.activation(o, i, f, bias=bias, scale=scale), after)
            return q.put("act", lambda e: e.activation(o, i, f, bias=bias, scale=scale, accum_out=accum), after)

        def copy(eng, o, i, after=()):
            if eng == "act":
                return act(o, i, after=after)
            return q.put(eng, lambda e: e.tensor_copy(o, i), after)

        def tt(eng, o, a, b, op, after=()):
            return q.put(eng, lambda e: e.tensor_tensor(o, a, b, op), after)

        def ts(eng, o, a, s1, s2, op0, op1=None, after=()):
            if op1 is None:
                return q.put(eng, lambda e: e.tensor_scalar(o, a, s1, None, op0), after)
            return q.put(eng, lambda e: e.tensor_scalar(o, a, s1, s2, op0, op1), after)

        def stt(o, a, s, b, op0, op1, after=()):
            return q.put("dve", lambda e: e.scalar_tensor_tensor(out=o, in0=a, scalar=s, in1=b, op0=op0, op1=op1), after)

        def red(o, i, op, after=()):
            return q.put("dve", lambda e: e.tensor_reduce(o, i, AX.X, op), after)

        def recip(o, i, after=()):
            return q.put("dve", lambda e: e.reciprocal(o, i), after)

        def fill(eng, o, v, after=()):
            return q.put(eng, lambda e: e.memset(o, v), after)

        def load(o, i, group, after=()):
            return q.put("sp", lambda e: e.dma_start(o, i), after, by=16, sem="ld_" + group)

        def tables(after=()):
            q.put("act", lambda e: e.preload_act_table_set("natural_log_exp_and_others"), after, signal=False)

        t = sb("t", [128, NT, DM])
        tn_hi = sb("tn_hi", [128, TOK], F32R)
        tn_lo = sb("tn_lo", [128, TOK], F32R)
        maskb = sb("maskb", [128, NT, SEQ], BF16)
        big_hi = sb("big_hi", [128, 8192], F32R)
        big_lo = sb("big_lo", [128, 8192], F32R)
        vals = sb("vals", [128, 8192])
        ag_hi = sb("ag_hi", [128, 2048], F32R)
        ag_lo = sb("ag_lo", [128, 2048], F32R)
        wv_hi = sb("wv_hi", [128, 1024], F32R)
        wv_lo = sb("wv_lo", [128, 1024], F32R)
        wo = sb("wo", [128, NHP, DM])
        stage = sb("stage", [128, 3072])
        uHH = sb("uHH", [128, CK + NCTX], F32R)
        uLL = sb("uLL", [128, CK + NCTX], F32R)
        mHH = sb("mHH", [128, CK], F32R)
        mLL = sb("mLL", [128, CK], F32R)
        work = sb("work", [128, 3, 1024])
        lnbuf = sb("lnbuf", [128, 2, 512])
        pt = sb("pt", [128, 2, 1024])
        ident = sb("ident", [128, 128])
        cols = sb("cols", [128, NCOL])
        rows = sb("rows", [128, len(ROWS), DM])
        lrows = sb("lrows", [128, 3, DM])
        rowscale = sb("rowscale", [128, NT])
        maskrow = sb("maskrow", [128, CK], BF16)
        ones = sb("ones", [128, 128], BF16)
        hmask = sb("hmask", [128, H0])
        st = sb("st", [128, 3, GT, 6])
        mv = sb("mv", [128, 3, GT, 2])
        ve = sb("ve", [128, 3, 3, GT])
        nmx = sb("nmx", [128, 4, 4])
        den = sb("den", [128, 4, 4])
        rden = sb("rden", [128, 4, 4])
        cmx = sb("cmx", [128, 4, 16])
        csum = sb("csum", [128, 4, 16])
        crec = sb("crec", [128, 4, 16])
        gate = sb("gate", [128, NT])
        rmask = sb("rmask", [128, NB])
        rinv = sb("rinv", [128, NB])
        psums = [ctx.enter_context(nc.psum_tensor(f"ps{i}", [128, 512], F32)) for i in range(8)]
        bank = Ring(psums)
        slot = Ring([work[:, i, :] for i in range(3)])
        lnslot = Ring([lnbuf[:, i, :] for i in range(2)])
        ptslot = Ring([pt[:, i, :] for i in range(2)])
        smslot = Ring(list(range(4)))
        csslot = Ring(list(range(4)))
        stslot = Ring(list(range(3)))
        vals_free = [[] for _ in range(4)]
        tn_free = [[] for _ in range(NG)]
        tn_ready = [None] * NG
        t_ready = [[] for _ in range(NT)]
        S = {}
        back = Background()

        def f(ap):
            return ap.bitcast(F32)

        def col(name):
            return cols[:, COL[name]:COL[name] + 1]

        def split(i, hi, lo, after):
            a = act(hi, i, after=after)
            return tt("dve", lo, i, f(hi), ALU.subtract, after=[a])

        def split_sb(i, hi, lo, after, wr=()):
            a = act(hi, i, after=[after, wr])
            return [a, tt("pool", lo, i, f(hi), ALU.subtract, after=[a])]

        so, n_small = offsets(SMALL)
        so3, n_small3 = offsets(SMALL3)
        assert n_small <= 1536
        ctxT = stage[:, 2560:3072]
        wv_raw0 = stage[:, 1536:2560]

        def small(name, o=so):
            at, r, n = o[name]
            return stage[0:r, at:at + n]

        xT = vals[:, 0:TOK]
        kT0, v1 = vals[:, TOK:TOK + CK], vals[:, TOK + CK:TOK + 2 * CK]
        k1, vw = wo[:, 4:8, :], wo[:, 0:4, :]
        loaded_xT = load(xT, A["xT"], "xT")
        load(stage[:, 0:n_small], A["small"], "in")
        load(ctxT[0:64, :], A["ctxT"], "in")
        load(ctxT[64:128, :], A["ctxT"], "in")
        loaded = load(hmask[:, :], A["hmask"], "in")
        loaded_id = load(ident[:, :], A["ident"], "id")
        got_a = load(pt[:, 0, :], A["wqT"][0], "self")
        got_a = load(pt[:, 1, :], A["wkT"][0], "self")
        loaded_cols = load(cols[:, :], A["cols"], "cols")
        mi = lnbuf[:, 0, :].bitcast(I32)
        loaded_m2 = load(mi, A["mask2"].rearrange("(o k) -> o k", o=1).to_broadcast([128, CK]), "m2")
        load(wv_raw0, A["wv"][0], "wv0")
        loaded_x = load(t[:, :, :], A["x"].rearrange("(n p) d -> p n d", p=128), "x")
        loaded_rows = load(rows[:, :, :], A["rows"].rearrange("(o r) d -> o r d", o=1).to_broadcast([128, len(ROWS), DM]), "rows")
        for n in range(NT):
            t_ready[n] = [loaded_x]
        tables()
        ones_set = fill("pool", ones[:, :], 1.0)
        entw = work[:, 0, 0:NB * NB].rearrange("p (b c) -> p b c", b=NB)
        entw_zero = fill("pool", entw, 0.0)
        mrow_zero = fill("pool", maskrow[:, :], 0.0)

        i, ps, freed = bank.take()
        m = mm(ps[:, :], small("wk0T"), ctxT[0:64, :], after=[freed, loaded], signal=True)
        kT0_ready = tt("dve", kT0.rearrange("p (b k) -> p b k", b=NB), ps[:, :].rearrange("p (b k) -> p b k", b=NB),
                       small("pos0T").unsqueeze(1).to_broadcast([128, NB, NCTX]), ALU.add, after=[m])
        bank.free(i, kT0_ready)
        k1f = k1.rearrange("p a d -> p (a d)")
        for w, b_, dst in (("wk1", "l1_bk", k1f), ("wv1", "l1_bv", v1)):
            i, ps, freed = bank.take()
            m = mm(ps[:, :], small(w), ctxT[0:64, :], after=[freed], signal=True)
            kv1_ready = act(dst, ps[:, :], ACT.Identity, bias=col(b_), after=[m, loaded_cols])
            bank.free(i, kv1_ready)
        i, ps, freed = bank.take()
        for a in range(NB // 2):
            v1_read = mm(ps[:, DM * a:DM * a + DM], v1[:, 128 * a:128 * a + 128], small("wo1"), after=[freed, kv1_ready],
                         signal=(a == NB // 2 - 1))
        vw_ready = copy("act", vw, ps[:, :].rearrange("p (a d) -> p a d", a=NB // 2), after=[v1_read])
        bank.free(i, vw_ready)

        for g in range(NG):
            s = slice(GTOK * g, GTOK * g + GTOK)
            tn_ready[g] = split_sb(xT[:, s], tn_hi[:, s], tn_lo[:, s], loaded_xT)
        u_parts = []
        for dst, src in ((slice(0, CK), slice(0, CK)), (slice(CK, CK + NCTX), slice(0, NCTX))):
            u_parts.append(split_sb(ctxT[:, src], uHH[:, dst], uLL[:, dst], loaded))

        for b in range(NB):
            z2 = copy("dve", entw[:, b, b:b + 1], small("entw"), after=[entw_zero, loaded])
        i, ps, freed = bank.take()
        for b in range(NB):
            last = mm(ps[0:NB, 0:SEQ], entw[:, b, :], xT[:, SEQ * b:SEQ * b + SEQ], b == 0, b == NB - 1,
                      after=[freed, z2, loaded_xT], signal=(b == NB - 1))
        e_bank = i

        def entropy_gate(buf):
            e_l, e_p, e_g = buf[0:NB, 128:384], buf[0:NB, 384:640], buf[0:NB, 640:896]
            e_s, e_1 = buf[0:NB, 64:96], buf[0:NB, 896:1024]
            o8 = fill("pool", e_1, 1.0)
            k = ts("dve", e_l, psums[e_bank][0:NB, 0:SEQ], cols[0:NB, COL["ent_b"]:COL["ent_b"] + 1], None, ALU.add,
                   after=[last, loaded_cols])
            bank.free(e_bank, k)
            k = red(e_s[:, 0:1], e_l, ALU.max, after=[k])
            k = ts("dve", e_l, e_l, e_s[:, 0:1], None, ALU.subtract, after=[k])
            k = act(e_p, e_l, ACT.Exp, accum=e_s[:, 1:2], after=[k])
            yield
            k = recip(e_s[:, 2:3], e_s[:, 1:2], after=[k])
            k = ts("dve", e_p, e_p, e_s[:, 2:3], None, ALU.mult, after=[k])
            k = ts("dve", e_l, e_p, 1e-9, None, ALU.add, after=[k])
            k = act(e_g, e_l, ACT.Ln, after=[k])
            yield
            k = tt("dve", e_g, e_g, e_p, ALU.mult, after=[k])
            k = red(e_s[:, 3:4], e_g, ALU.add, after=[k])
            k = ts("dve", e_s[:, 4:5], e_s[:, 3:4], -1.0, None, ALU.is_lt, after=[k])
            k = ts("dve", e_s[:, 8:16], ident[0:NB, 0:NB], e_s[:, 4:5], None, ALU.mult, after=[k, loaded_id])
            yield
            i, ps, freed = bank.take()
            k = mm(ps[:, 0:NB], e_1, e_s[:, 8:16], after=[freed, k, o8], signal=True)
            k = copy("dve", rmask[:, :], ps[:, 0:NB], after=[k])
            bank.free(i, k)
            S["rmask"] = ts("dve", rinv[:, :], rmask[:, :], -1.0, 1.0, ALU.mult, ALU.add, after=[k])

        def masked_heads(j, buf, src, heads):
            for c, h in enumerate(heads):
                k = ts("pool" if c % 4 == 3 else "dve", buf[:, 128 * c:128 * c + 128], small(src), hmask[:, h:h + 1],
                       None, ALU.mult, after=[slot.freed[j], loaded])
                S["mh", c] = k
            return [S["mh", c] for c in range(len(heads))]

        def store_stack(ps, dst, m, after):
            a = act(dst, ps[:, :], after=[m, after])
            return tt("dve", dst[64:128, :], ps[64:128, :], f(dst[64:128, :]), ALU.subtract, after=[a])

        C_hi = big_hi[:, :].rearrange("p (b h k) -> p b h k", b=NB, h=NH)
        C_lo = big_lo[:, :].rearrange("p (b h k) -> p b h k", b=NB, h=NH)
        Vp = vals[:, :].rearrange("p (b h d) -> p b h d", b=NB, h=NHP)

        j0, buf0, _ = slot.take()
        back.start(entropy_gate(buf0))
        back.tick()
        c_ready = []
        for half in range(2):
            j, WM, _ = slot.take()
            wm = masked_heads(j, WM, "wq0", range(8 * half, 8 * half + 8))
            for c in range(8):
                i, ps, freed = bank.take()
                m = mm(ps[:, :], WM[:, 128 * c:128 * c + 128], kT0, after=[freed, wm[c], kT0_ready], signal=True)
                k = split(ps[:, :].rearrange("p (b k) -> p b k", b=NB), C_hi[:, :, 8 * half + c, :],
                          C_lo[:, :, 8 * half + c, :], [m])
                bank.free(i, k)
                c_ready = [k]
            slot.free(j, m)
            back.tick()
        kT0_read = m
        h_ready = []
        H_first = (wv_hi, wv_lo)
        for par in range(2):
            j, WM, _ = slot.take()
            wm = masked_heads(j, WM, "wo0T", range(par, 16, 2))
            for half in range(2):
                i, ps, freed = bank.take()
                for twice in range(2):
                    m = mm(ps[64 * twice:64 * twice + 64, :], small("wv0"), WM[:, 512 * half:512 * half + 512],
                           after=[freed, wm], signal=True)
                k = store_stack(ps, H_first[par][:, 512 * half:512 * half + 512], m, [])
                bank.free(i, k)
                h_ready.append(k)
            slot.free(j, m)
        back.tick()

        def self_weights(qT, kT, got, ag_free):
            ready = []
            for half in range(2):
                for par in range(2):
                    i, ps, freed = bank.take()
                    p = slice(64 * par, 64 * par + 64)
                    for c in range(4):
                        hp = 4 * half + c
                        m = mm(ps[:, 128 * c:128 * c + 128], kT[p, 128 * hp:128 * hp + 128], qT[p, 128 * hp:128 * hp + 128],
                               after=[freed, got], signal=(c == 3))
                    at = slice(1024 * half + 512 * par, 1024 * half + 512 * par + 512)
                    k = split(ps[:, :], ag_hi[:, at], ag_lo[:, at], [m, ag_free])
                    bank.free(i, k)
                    ready.append(k)
            S["A"] = ready
            return m

        a_read = self_weights(pt[:, 0, :], pt[:, 1, :], got_a, [])
        ptslot.free(0, a_read)
        ptslot.free(1, a_read)

        pooled, gbias = buf0[0:64, 96:96 + NB], buf0[0:64, 104:104 + NB]
        k = red(pooled, ctxT[0:64, :].rearrange("c (b k) -> c b k", b=NB), ALU.add, after=[loaded])
        k = ts("dve", pooled, pooled, 1.0 / NCTX, None, ALU.mult, after=[k])
        i, ps, freed = bank.take()
        k = mm(ps[0:64, 0:NB], small("g1p"), pooled, after=[freed, k], signal=True)
        k = ts("dve", gbias, ps[0:64, 0:NB], cols[0:64, COL["gate_b1"]:COL["gate_b1"] + 1], None, ALU.add,
               after=[k, loaded_cols])
        bank.free(i, k)
        gi, gps, gfreed = bank.take()
        j, zs, jfreed = slot.take()
        j2, sg, jfreed2 = slot.take()
        gate_reads = []
        for g in range(NG):
            i, ps, freed = bank.take()
            m = mm(ps[0:64, :], small("g1x"), xT[:, GTOK * g:GTOK * g + GTOK], after=[freed, loaded_xT], signal=True)
            at = 512 * (g % 2)
            for b in range(2):
                za = ts("dve", zs[0:64, at + SEQ * b:at + SEQ * b + SEQ], ps[0:64, SEQ * b:SEQ * b + SEQ],
                        gbias[:, 2 * g + b:2 * g + b + 1], None, ALU.add,
                        after=[m, k, jfreed, gate_reads[g - 2] if g >= 2 else []])
            bank.free(i, za)
            z2, s2 = zs[0:64, at:at + GTOK], sg[0:64, at:at + GTOK]
            a = act(s2, z2, ACT.Sigmoid, after=[za, jfreed2])
            h = tt("dve", z2, z2, s2, ALU.mult, after=[a])
            for n in range(GT):
                last_g = mm(gps[:, GT * g + n:GT * g + n + 1], z2[:, 128 * n:128 * n + 128], small("g2"),
                            after=[h, gfreed], signal=(n == GT - 1))
            gate_reads.append(last_g)
        gate_ready = act(gate[:, :], gps[:, 0:NT], ACT.Sigmoid, bias=col("gate_b2"), after=[last_g])
        tables()
        bank.free(gi, gate_ready)
        slot.free(j, last_g)
        slot.free(j2, h)
        back.drain()
        slot.free(j0, [za, S["rmask"]])
        xT_read = [last_g, last, flat(tn_ready), kT0_read, v1_read]

        m01 = ts("dve", lnbuf[:, 1, :], mi, 0.0, None, ALU.not_equal, after=[loaded_m2])
        mrow = ts("dve", maskrow[0:1, :], mi[0:1, :], 0.0, NEG, ALU.is_equal, ALU.mult, after=[loaded_m2, mrow_zero])
        cm = tt("dve", lnbuf[:, 0, :], ctxT, lnbuf[:, 1, :], ALU.mult, after=[m01, mrow, loaded])
        m_parts = split_sb(lnbuf[:, 0, :], mHH[:, :], mLL[:, :], cm)
        lnslot.free(0, m_parts)
        lnslot.free(1, cm)

        def self_mask():
            mask_v = A["mask"].rearrange("(n p) k -> p n k", p=128)
            for n in range(0, NT, 2):
                i, buf, freed = lnslot.take()
                raw = buf.bitcast(I32).rearrange("p (n k) -> p n k", n=2)
                ld = load(raw, mask_v[:, n:n + 2, :], f"mask{i}", after=freed)
                yield
                k = ts("dve", maskb[:, n:n + 2, :], raw, 0.0, NEG, ALU.is_equal, ALU.mult, after=[ld])
                lnslot.free(i, k)
                k = red(rowscale[:, n:n + 2], maskb[:, n:n + 2, :], ALU.max, after=[k])
                S["mask"] = ts("dve", rowscale[:, n:n + 2], rowscale[:, n:n + 2], 0.0, -0.125, ALU.is_equal, ALU.mult,
                               after=[k])

        def values_through(H, after, free_of):
            ready = {}
            for b in range(NB):
                for par in range(2):
                    for half in range(2):
                        i, ps, freed = bank.take()
                        r = H[par][:, 512 * half:512 * half + 512]
                        at = NCTX * ((b - par) % NB)
                        for n, part in enumerate((uHH, uLL)):
                            m = mm(ps[:, :], part[:, at:at + 2 * NCTX], r, n == 0, n == 1,
                                   after=[freed, after, u_parts], signal=(n == 1))
                        p = slice(64 * par, 64 * par + 64)
                        e = copy("act" if half else "dve", Vp[p, b, 4 * half:4 * half + 4, :],
                                 ps[p, :].rearrange("p (h d) -> p h d", h=4), after=[m, free_of(b)])
                        bank.free(i, e)
                        ready.setdefault(b, []).append(e)
                if b % 2:
                    back.tick()
            S["H_read"] = m
            return ready

        back.start(self_mask())
        v_ready = values_through(H_first, h_ready, lambda b: xT_read)
        S["Wv"] = split_sb(wv_raw0, wv_hi[:, :], wv_lo[:, :], ("ld_wv0", 16), S["H_read"])

        def cross_tiles(scale, c_ready, v_ready, masked, finish, chain):
            state = {}

            def scores(n):
                b = n // 2
                cs = slice(128 * n, 128 * n + 128)
                j, P, pfreed = slot.take()
                x, _, xfreed = csslot.take()
                subs = []
                for half in range(2):
                    i, ps, freed = bank.take()
                    hs = slice(8 * half, 8 * half + 8)
                    m = mm3(ps[:, :], (tn_hi[:, cs], tn_lo[:, cs]), (C_hi[:, b, hs, :], C_lo[:, b, hs, :]),
                            after=[freed, c_ready, tn_ready[n // GT]], signal=not masked, more=masked)
                    if masked:
                        mr = maskrow[:, NCTX * b:NCTX * b + NCTX].unsqueeze(1).to_broadcast([128, 8, NCTX])
                        m = mm(ps[:, :], ones[:, :], mr, False, True, after=[mrow, ones_set], signal=True)
                    v = ps[:, :].rearrange("p (h k) -> p h k", h=8)
                    k = red(cmx[:, x, hs], v, ALU.max, after=[m, xfreed])
                    k = tt("dve", P[:, 512 * half:512 * half + 512].rearrange("p (h k) -> p h k", h=8), v,
                           cmx[:, x, hs].unsqueeze(2).to_broadcast([128, 8, NCTX]), ALU.subtract, after=[k, pfreed])
                    bank.free(i, k)
                    subs.append(k)
                tn_free[n // GT] = [m]
                S["c_used"] = m
                state[n] = [j, P, x, act(P, P, ACT.Exp, scale=scale, after=[subs])]

            def normal(n):
                j, P, x, a = state[n]
                P3 = P.rearrange("p (h k) -> p h k", h=NH)
                k = red(csum[:, x, :], P3, ALU.add, after=[a])
                k = recip(crec[:, x, :], csum[:, x, :], after=[k])
                k = tt("pool", P3, P3, crec[:, x, :].unsqueeze(2).to_broadcast([128, NH, NCTX]), ALU.mult, after=[k])
                csslot.free(x, k)
                state[n] = [j, P, k]

            def turn(n):
                j, P, p_ready = state[n]
                y, T, tfreed = ptslot.take()
                ev = []
                for half in range(2):
                    i, ps, freed = bank.take()
                    for c in range(4):
                        m = tr(ps[:, 128 * c:128 * c + 128], P[:, 512 * half + 128 * c:512 * half + 128 * c + 128],
                               after=[freed, p_ready], signal=(c == 3))
                    ev.append(copy("act", T[:, 512 * half:512 * half + 512], ps[:, :], after=[m, tfreed]))
                    bank.free(i, ev[-1])
                slot.free(j, m)
                state[n] = [y, T, ev]

            def output(n):
                y, T, ev = state.pop(n)
                i, ps, freed = bank.take()
                for hp in range(NHP):
                    m = mm(ps[:, 0:DM], T[:, 128 * hp:128 * hp + 128], Vp[:, n // 2, hp, :], hp == 0, hp == NHP - 1,
                           after=[freed, ev[hp // 4], v_ready[n // 2]], signal=(hp == NHP - 1))
                ptslot.free(y, m)
                vals_free[n // GT] = [m]
                bank.free(i, finish(n, ps[:, 0:DM], m))

            for n in range(NT + 3):
                if n < NT:
                    scores(n)
                if 1 <= n <= NT:
                    normal(n - 1)
                back.tick()
                if n >= 3:
                    output(n - 3)
                    if (n - 3) % GT == GT - 1:
                        back.start(chain((n - 3) // GT))
                if 2 <= n < NT + 2:
                    turn(n - 2)
                back.tick()

        def statistics(srcs, eps, after):
            x, _, xfreed = stslot.take()
            n = len(srcs)
            for c, src in enumerate(srcs):
                k = q.put("dve", bn_call(st[:, x, c, :], src), [after[c], xfreed])
            for c in range(n):
                k2 = q.put("dve", aggr_call(mv[:, x, c, :], st[:, x, c, :]), [k])
            v, y, w = ve[:, x, 0, 0:n], ve[:, x, 1, 0:n], ve[:, x, 2, 0:n]
            k = ts("dve", v, mv[:, x, 0:n, 1], eps, None, ALU.add, after=[k2])
            a = act(y, v, ACT.Ln, after=[k])
            a = act(y, y, ACT.Exp, scale=-0.5, after=[a])

            def newton():
                k = tt("dve", w, v, y, ALU.mult, after=[a])
                k = tt("dve", w, w, y, ALU.mult, after=[k])
                k = ts("dve", w, w, -0.5, 1.5, ALU.mult, ALU.add, after=[k])
                return tt("dve", mv[:, x, 0:n, 1], w, y, ALU.mult, after=[k])
            return x, newton

        def load_bias(l, r, after):
            S["lrows", r] = load(lrows[:, r, :], A["lrows"][l, r:r + 1, :].to_broadcast([128, DM]), f"bias{r}", after)

        def layer_norm(g, gcol, bcol, l, r, keep=False):
            j, buf, jfreed = lnslot.take()
            x, newton = statistics([t[:, GT * g + c, :] for c in range(GT)], 1e-5,
                                   [t_ready[GT * g + c] for c in range(GT)])
            yield
            k = newton()
            xs = []
            for c in range(GT):
                xs.append(ts("dve", buf[:, 128 * c:128 * c + 128], t[:, GT * g + c, :], mv[:, x, c, 0:1],
                             mv[:, x, c, 1:2], ALU.subtract, ALU.mult, after=[k, jfreed]))
            stslot.free(x, xs)
            tv = t[:, GT * g:GT * g + GT, :]
            k = tt("pool", tv, tv, lrows[:, r, :].unsqueeze(1).to_broadcast([128, GT, DM]), ALU.add,
                   after=[S["lrows", r], xs])
            for n in range(GT * g, GT * g + GT):
                t_ready[n] = [k]
            if g == NG - 1 and l + 1 < NLAYER:
                load_bias(l + 1, r, k)
            yield
            i, ps, freed = bank.take()
            for c in range(GT):
                m = tr(ps[:, 128 * c:128 * c + 128], buf[:, 128 * c:128 * c + 128], after=[freed, xs[c]],
                       signal=(c == GT - 1))
            a = act(buf, ps[:, :], ACT.Identity, bias=bcol, scale=gcol, after=[m])
            bank.free(i, a)
            if keep:
                S["kept", g] = (j, buf, a)
            else:
                s = slice(GTOK * g, GTOK * g + GTOK)
                tn_ready[g] = split_sb(buf, tn_hi[:, s], tn_lo[:, s], a, tn_free[g])
                lnslot.free(j, tn_ready[g])
            yield

        norm = (col("norm_g"), col("norm_b"))

        def finish0(n, ps, m):
            if n % GT == 0:
                S["h"] = lnslot.take()
                S["h_done"] = []
            _, buf, freed = S["h"]
            c = n % GT
            k = stt(buf[:, 128 * c:128 * c + 128], ps, gate[:, n:n + 1], t[:, n, :], ALU.mult, ALU.add,
                    after=[m, freed, gate_ready, t_ready[n]])
            S["h_done"].append(k)
            if c == GT - 1:
                S["h_of", n // GT] = (S["h"], S["h_done"])
            return k

        def first_and_second(g):
            (j, buf, _), done = S["h_of", g]
            x, newton = statistics([buf[:, 128 * c:128 * c + 128] for c in range(GT)], 1e-5, [[k] for k in done])
            yield
            k = newton()
            for c in range(GT):
                h = buf[:, 128 * c:128 * c + 128]
                kx = ts("dve", h, h, mv[:, x, c, 0:1], mv[:, x, c, 1:2], ALU.subtract, ALU.mult, after=[k])
            stslot.free(x, kx)
            h3 = buf.rearrange("p (n d) -> p n d", n=GT)
            k = tt("pool", h3, h3, rows[:, ROW["ln_scale"], :].unsqueeze(1).to_broadcast([128, GT, DM]), ALU.mult,
                   after=[kx, loaded_rows])
            k = tt("pool", h3, h3, rows[:, ROW["ln_bias"], :].unsqueeze(1).to_broadcast([128, GT, DM]), ALU.add, after=[k])
            yield
            for b in range(2):
                hb = buf[:, SEQ * b:SEQ * b + SEQ].rearrange("p (n d) -> p n d", n=2)
                tv = t[:, GT * g + 2 * b:GT * g + 2 * b + 2, :]
                e = 2 * g + b
                k2 = ts("dve", hb, hb, rmask[:, e:e + 1], None, ALU.mult, after=[k, S["rmask"]])
                k2 = stt(tv, tv, rinv[:, e:e + 1], hb, ALU.mult, ALU.add, after=[k2])
            lnslot.free(j, k2)
            at = 2048 * g
            tT, q1 = vals[:, at:at + 512], vals[:, at + 512:at + 1024]
            zp = vals[:, at + 1024:at + 1536].rearrange("p (n c) -> p n c", n=GT)
            P3 = vals[:, at + 1536:at + 1792].rearrange("p (n k) -> p n k", n=GT)
            zero = fill("pool", zp, 0.0, after=vals_free[g])
            yield
            i, ps, freed = bank.take()
            for c in range(GT):
                m = tr(ps[:, 128 * c:128 * c + 128], t[:, GT * g + c, :], after=[freed, k2], signal=(c == GT - 1))
            e = copy("act", tT, ps[:, :], after=[m, vals_free[g]])
            bank.free(i, e)
            yield
            i, ps, freed = bank.take()
            m = mm(ps[:, :], small("wq1"), tT, after=[freed, e], signal=True)
            a = act(q1, ps[:, :], ACT.Identity, bias=col("l1_bq"), after=[m, vals_free[g]])
            bank.free(i, a)
            yield
            i, ps, freed = bank.take()
            for c in range(GT):
                b = 2 * g + c // 2
                m = mm(ps[:, 64 * c:64 * c + 64], q1[:, 128 * c:128 * c + 128], k1f[:, NCTX * b:NCTX * b + NCTX],
                       after=[freed, a, kv1_ready], signal=(c == GT - 1))
            yield
            x, _, xfreed = csslot.take()
            v = ps[:, 0:256].rearrange("p (n k) -> p n k", n=GT)
            k = red(cmx[:, x, 0:GT], v, ALU.max, after=[m, xfreed])
            k = tt("dve", P3, v, cmx[:, x, 0:GT].unsqueeze(2).to_broadcast([128, GT, NCTX]), ALU.subtract,
                   after=[k, vals_free[g]])
            bank.free(i, k)
            a = act(P3, P3, ACT.Exp, scale=float(DM) ** -0.5, after=[k])
            yield
            k = red(csum[:, x, 0:GT], P3, ALU.add, after=[a])
            k = recip(crec[:, x, 0:GT], csum[:, x, 0:GT], after=[k])
            for par in range(2):
                n2 = slice(2 * par, 2 * par + 2)
                kz = tt("dve", zp[:, n2, 64 * par:64 * par + 64], P3[:, n2, :],
                        crec[:, x, n2].unsqueeze(2).to_broadcast([128, 2, NCTX]), ALU.mult, after=[k, zero])
            csslot.free(x, kz)
            yield
            i, ps, freed = bank.take()
            for c in range(GT):
                m = tr(ps[:, 128 * c:128 * c + 128], zp[:, c, :], after=[freed, kz], signal=(c == GT - 1))
            e = copy("act", tT, ps[:, :], after=[m])
            bank.free(i, e)
            yield
            i, ps, freed = bank.take()
            for c in range(GT):
                m = mm(ps[:, 128 * c:128 * c + 128], tT[:, 128 * c:128 * c + 128], vw[:, g, :],
                       after=[freed, e, vw_ready], signal=(c == GT - 1))
            vals_free[g] = [m]
            S["stage_read"] = m
            yield
            tv = t[:, GT * g:GT * g + GT, :]
            k = tt("dve", tv, ps[:, :].rearrange("p (n d) -> p n d", n=GT), tv, ALU.add, after=[m])
            bank.free(i, k)
            k = tt("pool", tv, tv, rows[:, ROW["l1_bo"], :].unsqueeze(1).to_broadcast([128, GT, DM]), ALU.add, after=[k])
            for c in range(GT):
                t_ready[GT * g + c] = [k]
            yield
            yield from layer_norm(g, *norm, 0, 0)

        for r in range(3):
            load_bias(0, r, [])
        back.drain()
        cross_tiles(float(DM // H0) ** -0.5, c_ready, v_ready, False, finish0, first_and_second)

        w_hi = big_hi[:, :].rearrange("p (c b h k) -> p c b h k", c=NHP, b=2, h=2)
        w_lo = big_lo[:, :].rearrange("p (c b h k) -> p c b h k", c=NHP, b=2, h=2)
        V = vals[:, 0:4096].rearrange("p (n e) -> p n e", n=GT)
        oT = vals[:, 4096:8192].rearrange("p (b h k) -> p b h k", b=2, h=NHP)
        hT = vals[:, :].rearrange("p (g c k) -> p g c k", g=NG, c=4)
        w1, w2 = stage[:, 0:512], stage[:, 512:1024]

        def load_self(l, after):
            load(stage[:, 0:1024], A["wqT"][l], "self", after)
            load(stage[:, 1024:2048], A["wkT"][l], "self", after)
            return load(stage[:, 2048:3072], A["wv"][l], "self", after)

        def load_cross(l, after):
            load(stage[:, 0:1024], A["cqT"][l], "cross", after)
            load(stage[:, 1024:1536], A["ckT"][l], "cross", after)
            load(stage[:, 1536:2048], A["cvT"][l], "cross", after)
            return load(stage[:, 2048:3072], A["co"][l], "cross", after)

        def a_slice(h):
            hp, par = h // 2, h % 2
            at = 1024 * (hp // 4) + 512 * par + 128 * (hp % 4)
            return ag_hi[:, at:at + 128], ag_lo[:, at:at + 128]

        def w_project(g, hp, after):
            s = slice(GTOK * g, GTOK * g + GTOK)
            ready = []
            for par in range(2):
                i, ps, freed = bank.take()
                m = mm3(ps[:, :], a_slice(2 * hp + par), (tn_hi[:, s], tn_lo[:, s]),
                        after=[freed, S["A"], tn_ready[g]], signal=True)
                v = ps[:, :].rearrange("p (b k) -> p b k", b=2)
                k = split(v, w_hi[:, hp, :, par, :], w_lo[:, hp, :, par, :], [m, after])
                bank.free(i, k)
                ready.append(k)
            S["w", hp] = ready
            S["A_read"] = m

        def v_project(g, half, n, after):
            i, ps, freed = bank.take()
            cs = slice(GTOK * g + 128 * n, GTOK * g + 128 * n + 128)
            es = slice(512 * half, 512 * half + 512)
            m = mm3(ps[:, :], (tn_hi[:, cs], tn_lo[:, cs]), (wv_hi[:, es], wv_lo[:, es]),
                    after=[freed, S["Wv"], tn_ready[g]], signal=True)
            S["V", half, n] = copy("dve" if n % 2 else "act", V[:, n, es], ps[:, :], after=[m, after])
            bank.free(i, S["V", half, n])
            S["wv_read"] = m

        def ttr(o, i, m, s, acc, after):
            return q.put("dve", lambda e: e.tensor_tensor_reduce(o, i, m, s, BIG, ALU.add, ALU.min, acc), after)

        def unit_scores(g, hp, b):
            j, P, pfreed = slot.take()
            x, _, xfreed = smslot.take()
            P4 = P.rearrange("p (a h k) -> p a h k", a=2, h=2)
            ex = []
            for a in range(2):
                n = GT * g + 2 * b + a
                i, ps, freed = bank.take()
                cs = slice(128 * n, 128 * n + 128)
                m = mm3(ps[:, :], (tn_hi[:, cs], tn_lo[:, cs]), (w_hi[:, hp, b, :, :], w_lo[:, hp, b, :, :]),
                        after=[freed, S["w", hp], tn_ready[g]], signal=True)
                for h in range(2):
                    c = 2 * a + h
                    k = ttr(P4[:, a, h, :], ps[:, 256 * h:256 * h + 256], maskb[:, n, :], rowscale[:, n:n + 1],
                            nmx[:, x, c:c + 1], [m, pfreed, xfreed, S["mask"]])
                    ex.append(act(P4[:, a, h, :], P4[:, a, h, :], ACT.Exp, bias=nmx[:, x, c:c + 1], scale=-1.0,
                                  accum=den[:, x, c:c + 1], after=[k]))
                bank.free(i, k)
            S["scores_read"] = m
            return j, P4, x, ex

        def unit_normal(u):
            j, P4, x, ex = u
            pn = []
            r = recip(rden[:, x, :], den[:, x, :], after=[ex])
            for a in range(2):
                pn.append(tt("pool", P4[:, a, :, :], P4[:, a, :, :],
                             rden[:, x, 2 * a:2 * a + 2].unsqueeze(2).to_broadcast([128, 2, SEQ]), ALU.mult, after=[r]))
            smslot.free(x, pn)
            return j, P4, pn

        def unit_turn(u):
            j, P4, pn = u
            y, T, tfreed = ptslot.take()
            ev = []
            for h in range(2):
                i, ps, freed = bank.take()
                for a in range(2):
                    for kt in range(2):
                        m = tr(ps[:, 256 * kt + 128 * a:256 * kt + 128 * a + 128], P4[:, a, h, 128 * kt:128 * kt + 128],
                               after=[freed, pn[a]], signal=(kt == 1 and a == 1))
                ev.append(copy("dve" if h else "act", T[:, 512 * h:512 * h + 512], ps[:, :], after=[m, tfreed]))
                bank.free(i, ev[-1])
            slot.free(j, m)
            return y, T, ev

        def unit_values(g, hp, b, u):
            y, T, ev = u
            i, ps, freed = bank.take()
            for kt in range(2):
                for h in range(2):
                    e = slice(64 * (2 * hp + h), 64 * (2 * hp + h) + 64)
                    m = mm(ps[64 * h:64 * h + 64, 0:SEQ], V[:, 2 * b + kt, e], T[:, 512 * h + 256 * kt:512 * h + 256 * kt + 256],
                           kt == 0, kt == 1, after=[freed, ev[h], S["V", hp // 4, 2 * b + kt]], signal=(kt == 1))
            ptslot.free(y, m)
            S["v_used", hp // 4] = m
            S["oT", b, hp] = copy("act", oT[:, b, hp, :], ps[:, 0:SEQ], after=[m, S["oT_free", b]])
            bank.free(i, S["oT", b, hp])

        def out_project(g, b):
            i, ps, freed = bank.take()
            for a in range(2):
                for hp in range(NHP):
                    m = mm(ps[:, 128 * a:128 * a + 128], oT[:, b, hp, 128 * a:128 * a + 128], wo[:, hp, :],
                           hp == 0, hp == NHP - 1, after=[freed, S["oT", b, hp], S["Wo"]],
                           signal=(a == 1 and hp == NHP - 1))
            n = GT * g + 2 * b
            tv = t[:, n:n + 2, :]
            k = tt("dve", tv, ps[:, 0:256].rearrange("p (n d) -> p n d", n=2), tv, ALU.add,
                   after=[m, t_ready[n], t_ready[n + 1]])
            bank.free(i, k)
            t_ready[n] = t_ready[n + 1] = [k]
            S["oT_free", b] = m

        def finish2(n, ps, m):
            k = tt("dve", t[:, n, :], ps, t[:, n, :], ALU.add, after=[m, t_ready[n]])
            t_ready[n] = [k]
            return k

        def feed_forward(l, g):
            j, xn, x_ready = S["kept", g]
            ev = []
            for c in range(4):
                i, ps, freed = bank.take()
                m = mm(ps[:, :], w1[:, 128 * c:128 * c + 128], xn, after=[freed, S["w12"], x_ready], signal=True)
                bc = cols[:, FFB + 4 * l + c:FFB + 4 * l + c + 1]
                ev.append(act(hT[:, g, c, :], ps[:, :], ACT.Relu, bias=bc, after=[m, vals_free[g]]))
                bank.free(i, ev[-1])
                if c == 1:
                    yield
            lnslot.free(j, m)
            yield
            i, ps, freed = bank.take()
            for a in range(GT):
                for c in range(4):
                    m = mm(ps[:, 128 * a:128 * a + 128], hT[:, g, c, 128 * a:128 * a + 128], w2[:, 128 * c:128 * c + 128],
                           c == 0, c == 3, after=[freed, ev[c], S["w12"]], signal=(a == GT - 1 and c == 3))
            tv = t[:, GT * g:GT * g + GT, :]
            k = tt("dve", tv, ps[:, :].rearrange("p (n d) -> p n d", n=GT), tv, ALU.add,
                   after=[m, t_ready[GT * g:GT * g + GT]])
            bank.free(i, k)
            for n in range(GT * g, GT * g + GT):
                t_ready[n] = [k]
            vals_free[g] = [m]
            S["stage_read"] = m
            yield

        def after_cross(l):
            def chain(g):
                yield from layer_norm(g, cols[:, PRE_G + l:PRE_G + l + 1], cols[:, PRE_B + l:PRE_B + l + 1], l, 2, True)
                yield from feed_forward(l, g)
                if l + 1 < NLAYER:
                    yield from layer_norm(g, *norm, l + 1, 0)
            return chain

        w_free = {hp: [S["c_used"]] for hp in range(NHP)}
        staged = [S["Wv"], S["rmask"], c_ready, v1_read, xT_read]
        units = [(g, hp, b) for g in range(NG) for hp in range(NHP) for b in range(2)]
        wo_read = []
        for l in range(NLAYER):
            v_free = [vals_free[0], vals_free[1]]
            w_project(0, 0, w_free[0])
            w_project(0, 1, w_free[1])
            scored, turned = {}, {}
            for n in range(len(units) + 3):
                g, hp, b = units[n] if n < len(units) else (NG, 0, 0)
                s = n % 16
                if g < NG:
                    scored[n] = unit_scores(g, hp, b)
                if n == 3:
                    back.drain()
                    S["Wo"] = load(wo[:, :, :], A["wo"][l].rearrange("p (c d) -> p c d", c=NHP), "wo",
                                   [S["stage_read"], wo_read])
                    S["oT_free", 0], S["oT_free", 1] = vals_free[2], vals_free[3]
                    got_cross = load_cross(l, [staged, S["stage_read"]])
                if n >= 3:
                    unit_values(*units[n - 3], turned.pop(n - 3))
                if g < NG and b == 1:
                    w_free[hp] = [S["scores_read"]]
                    S["tn_units", g] = S["scores_read"]
                    if g + 1 < NG:
                        w_project(g + 1, hp, w_free[hp])
                elif g == 0 and hp + 2 < NHP:
                    w_project(0, hp + 2, w_free[hp + 2])
                if g == 0 and s < 2:
                    for kt in (2 * s, 2 * s + 1):
                        v_project(0, 0, kt, v_free)
                if 2 <= s < 6 and g < NG:
                    v_project(g, 1, s - 2, [v_free, S["v_used", 1] if g else []])
                if 10 <= s < 14 and g + 1 < NG:
                    v_project(g + 1, 0, s - 10, [S["v_used", 0]])
                if 1 <= g < NG and s in (2, 3):
                    out_project(g - 1, s - 2)
                    if s == 3:
                        tn_free[g - 1] = [S["tn_units", g - 1], S["A_read"], S["wv_read"]]
                        back.start(layer_norm(g - 1, *norm, l, 1))
                back.tick()
                if n >= 1 and n - 1 in scored:
                    scored[n - 1] = unit_normal(scored[n - 1])
                if n >= 2 and n - 2 in scored:
                    turned[n - 2] = unit_turn(scored.pop(n - 2))
                back.tick()
            out_project(NG - 1, 0)
            out_project(NG - 1, 1)
            tn_free[NG - 1] = [S["tn_units", NG - 1], S["A_read"], S["wv_read"]]
            back.start(layer_norm(NG - 1, *norm, l, 1))
            back.tick()
            wo_read = [S["oT_free", 0], S["oT_free", 1]]
            self_read = [S["v_used", 0], S["v_used", 1], wo_read]

            qT, kT, vT, co = stage[:, 0:1024], stage[:, 1024:1536], stage[:, 1536:2048], stage[:, 2048:3072]
            done = {}
            for what, lhs, rhs, dst in (("G", kT, qT, ag_hi), ("H", vT, co, ag_lo)):
                done[what] = []
                for par in range(2):
                    for half in range(2):
                        i, ps, freed = bank.take()
                        p = slice(64 * par, 64 * par + 64)
                        for c in range(4):
                            hp = 4 * half + c
                            for o in range(2):
                                m = mm(ps[64 * o:64 * o + 64, 128 * c:128 * c + 128], lhs[p, 64 * hp:64 * hp + 64],
                                       rhs[p, 128 * hp:128 * hp + 128], after=[freed, got_cross],
                                       signal=(c == 3 and o == 1))
                        at = slice(1024 * par + 512 * half, 1024 * par + 512 * half + 512)
                        k = store_stack(ps, dst[:, at], m, [S["A_read"]])
                        bank.free(i, k)
                        done[what].append(k)
                back.tick()
            if l + 1 < NLAYER:
                got = load_self(l + 1, m)
            for h in range(NH):
                par, hp = h % 2, h // 2
                i, ps, freed = bank.take()
                G = ag_hi[:, 1024 * par + 128 * hp:1024 * par + 128 * hp + 128]
                mm(ps[:, :], G, mHH[:, :], True, False, after=[freed, done["G"], m_parts])
                m = mm(ps[:, :], G, mLL[:, :], False, True, signal=True)
                v = ps[:, :].rearrange("p (b k) -> p b k", b=NB)
                k = split(v, C_hi[:, :, h, :], C_lo[:, :, h, :], [m, list(w_free.values())])
                bank.free(i, k)
                c_ready = [k]
                if h % 4 == 3:
                    back.tick()
            v_ready = values_through((ag_lo[:, 0:1024], ag_lo[:, 1024:2048]), done["H"], lambda b: self_read)
            staged = [S["H_read"]]
            if l + 1 < NLAYER:
                staged = [self_weights(stage[:, 0:1024], stage[:, 1024:2048], got, [S["H_read"]])]
                S["Wv"] = split_sb(stage[:, 2048:3072], wv_hi[:, :], wv_lo[:, :], got, S["wv_read"])
            load(w1, A["w1"][l], "w12", staged)
            S["w12"] = load(w2, A["w2"][l], "w12", staged)
            cross_tiles(0.125, c_ready, v_ready, True, finish2, after_cross(l))
            w_free = {hp: [S["c_used"]] for hp in range(NHP)}
            staged = S["Wv"]
        back.drain()
        staged = [staged, S["stage_read"]]

        load(rows[:, :, :], A["rows3"].rearrange("(o r) d -> o r d", o=1).to_broadcast([128, len(ROWS3), DM]), "last")
        load(ctxT[0:64, :], A["ctxT"], "last", staged)
        got = load(stage[:, 0:n_small3], A["small3"], "last", staged)
        qT3, tT, kT3 = vals[:, 0:TOK], vals[:, TOK:2 * TOK], vals[:, 3 * TOK:3 * TOK + CK]
        v3 = vals[:, 3 * TOK + CK:3 * TOK + 2 * CK].rearrange("p (a d) -> p a d", a=NB // 2)
        wT = vals[:, 2 * TOK:2 * TOK + 4 * SEQ].rearrange("p (a k) -> p a k", a=NB // 2)
        i, ps, freed = bank.take()
        m = mm(ps[:, :], small("wk3", so3), ctxT[0:64, :], after=[freed, got], signal=True)
        k3_ready = act(kT3, ps[:, :], ACT.Identity, bias=col("l3_bk"), after=[m, vals_free])
        bank.free(i, k3_ready)
        i, ps, freed = bank.take()
        for a in range(NB // 2):
            m = mm(ps[:, DM * a:DM * a + DM], ctxT[0:64, 128 * a:128 * a + 128], small("wv3", so3), after=[freed, got],
                   signal=(a == NB // 2 - 1))
        v3_ready = tt("dve", v3, ps[:, :].rearrange("p (a d) -> p a d", a=NB // 2),
                      rows[:, ROW["l3_bv"], :].unsqueeze(1).to_broadcast([128, NB // 2, DM]), ALU.add,
                      after=[m, vals_free, got])
        bank.free(i, v3_ready)
        stores = []
        out_v = out.rearrange("(n p) d -> p n d", p=128)

        def last_block(a):
            i, ps, freed = bank.take()
            for c in range(GT):
                m = tr(ps[:, 128 * c:128 * c + 128], t[:, GT * a + c, :], after=[freed, t_ready[GT * a + c]],
                       signal=(c == GT - 1))
            s = slice(GTOK * a, GTOK * a + GTOK)
            e = copy("act", tT[:, s], ps[:, :], after=[m, vals_free])
            bank.free(i, e)
            yield
            i, ps, freed = bank.take()
            m = mm(ps[:, :], small("wq3", so3), tT[:, s], after=[freed, e, got], signal=True)
            q_ready = act(qT3[:, s], ps[:, :], ACT.Identity, bias=col("l3_bq"), after=[m])
            bank.free(i, q_ready)
            yield
            i, ps, freed = bank.take()
            for c in range(2):
                b = 2 * a + c
                m = mm(ps[64 * c:64 * c + 64, 0:SEQ], kT3[:, NCTX * b:NCTX * b + NCTX], qT3[:, SEQ * b:SEQ * b + SEQ],
                       after=[freed, q_ready, k3_ready], signal=(c == 1))
            x, _, xfreed = csslot.take()
            k = red(cmx[:, x, 0:1], ps[:, 0:SEQ], ALU.max, after=[m, xfreed])
            k = ts("dve", cmx[:, x, 1:2], cmx[:, x, 0:1], -float(DM) ** -0.5, None, ALU.mult, after=[k])
            e = act(wT[:, a, :], ps[:, 0:SEQ], ACT.Exp, bias=cmx[:, x, 1:2], scale=float(DM) ** -0.5,
                    accum=csum[:, x, 0:1], after=[k, vals_free])
            bank.free(i, e)
            yield
            k = recip(crec[:, x, 0:1], csum[:, x, 0:1], after=[e])
            k = ts("dve", v3[:, a, :], v3[:, a, :], crec[:, x, 0:1], None, ALU.mult, after=[k, v3_ready])
            csslot.free(x, k)
            yield
            i, ps, freed = bank.take()
            i2, ps2, freed2 = bank.take()
            for c in range(GT):
                p = slice(64 * (c // 2), 64 * (c // 2) + 64)
                o = (ps if c < 2 else ps2)[:, DM * (c % 2):DM * (c % 2) + DM]
                m = mm(o, wT[p, a, 128 * (c % 2):128 * (c % 2) + 128], v3[p, a, :], after=[freed, freed2, k, e],
                       signal=(c % 2 == 1))
            yield
            j, buf, jfreed = lnslot.take()
            b3 = buf.rearrange("p (n d) -> p n d", n=GT)
            for c, o in enumerate((ps, ps2)):
                r = tt("dve", b3[:, 2 * c:2 * c + 2, :], o[:, 0:256].rearrange("p (n d) -> p n d", n=2),
                       t[:, GT * a + 2 * c:GT * a + 2 * c + 2, :], ALU.add, after=[m, jfreed, t_ready[GT * a]])
            bank.free(i, r)
            bank.free(i2, r)
            x, newton = statistics([buf[:, DM * c:DM * c + DM] for c in range(GT)], 1e-6, [[r]] * GT)
            yield
            k = newton()
            for c in range(GT):
                h = buf[:, DM * c:DM * c + DM]
                kx = ts("dve", h, h, mv[:, x, c, 0:1], mv[:, x, c, 1:2], ALU.subtract, ALU.mult, after=[k])
            stslot.free(x, kx)
            k = tt("dve", b3, b3, rows[:, ROW["l3_gamma"], :].unsqueeze(1).to_broadcast([128, GT, DM]), ALU.mult, after=[kx])
            k = tt("dve", b3, b3, rows[:, ROW["l3_beta"], :].unsqueeze(1).to_broadcast([128, GT, DM]), ALU.add, after=[k])
            s = q.put("sp", store_call(out_v[:, GT * a:GT * a + GT, :], b3), [k], by=16, sem=f"store{a}")
            lnslot.free(j, s)
            stores.append(s)

        for a in range(NG):
            back.start(last_block(a))
            back.tick(3)
        back.drain()

        sems = {n: ctx.enter_context(nc.semaphore("s_" + n)) for n in q.count}
        block = ctx.enter_context(nc.Block())

        @block.tensor
        def _(e):
            q.run("pe", e, sems)

        @block.scalar
        def _(e):
            q.run("act", e, sems)

        @block.vector
        def _(e):
            q.run("dve", e, sems)

        @block.gpsimd
        def _(e):
            q.run("pool", e, sems)

        @block.sync
        def _(e):
            q.run("sp", e, sems)
            for s, v in stores:
                e.wait_ge(sems[s], v)


def bn_call(o, i):
    return lambda e: e.bn_stats(o, i)


def aggr_call(o, i):
    return lambda e: e.bn_aggr(o, i)


def store_call(o, i):
    return lambda e: e.dma_start(o, i)


def layout(inputs):
    g = {k: np.asarray(v) for k, v in inputs.items()}

    def c(a):
        return np.ascontiguousarray(a)

    def pack(parts, values):
        at, n = offsets(parts)
        a = np.zeros((128, n), np.float32)
        for name, rows, w in parts:
            o = at[name][0]
            a[0:rows, o:o + w] = values[name]
        return a

    def pairs(w):
        L, e, n = w.shape
        return c(w.reshape(L, e // 128, 128, n).transpose(0, 2, 1, 3).reshape(L, 128, e // 128 * n))

    E = NH * HD
    x = g["x"].reshape(TOK, DM)
    g1 = g["L0_xattn_gate_w1"]
    kv, ckv = g["L2_xattn_sa_kv"], g["L2_xattn_ca_kv"]
    A = {
        "x": c(x), "xT": c(x.T), "ctxT": c(g["ctx_512"].reshape(CK, DC).T),
        "mask": c(g["mask_BxSxS_ik0"].reshape(TOK, SEQ)), "mask2": c(g["mask_Bx1xS2_if1"].reshape(CK)),
        "small": pack(SMALL, {
            "wq0": g["L0_xattn_Wq"], "wk0T": g["L0_xattn_Wk"].T, "wv0": g["L0_xattn_Wv"], "wo0T": g["L0_xattn_Wo"].T,
            "pos0T": g["L0_xattn_mem_pos_embed"][0].T, "g1x": g1[:, :DM].T, "g1p": g1[:, DM:].T,
            "g2": g["L0_xattn_gate_w2"].T, "entw": g["L0_xattn_ent_w"].T,
            "wq1": g["L1_xattn_Wq"], "wk1": g["L1_xattn_Wk"], "wv1": g["L1_xattn_Wv"], "wo1": g["L1_xattn_Wo"]}),
        "small3": pack(SMALL3, {"wq3": g["L3_xattn_Wq"], "wk3": g["L3_xattn_Wk"], "wv3": g["L3_xattn_Wv"]}),
        "wqT": pairs(g["L2_xattn_sa_q"].transpose(0, 2, 1)), "wkT": pairs(kv[:, :, :E].transpose(0, 2, 1)),
        "wv": c(kv[:, :, E:]), "wo": pairs(g["L2_xattn_sa_ow"]),
        "cqT": pairs(g["L2_xattn_ca_q"].transpose(0, 2, 1)), "ckT": pairs(ckv[:, :, :E].transpose(0, 2, 1)),
        "cvT": pairs(ckv[:, :, E:].transpose(0, 2, 1)), "co": pairs(g["L2_xattn_ca_ow"]),
        "w1": c(g["L2_xattn_ff_w1"]), "w2": pairs(g["L2_xattn_ff_w2"]),
        "lrows": c(np.stack([g["L2_xattn_sa_ob"], g["L2_xattn_ca_ob"], g["L2_xattn_ff_b2"]], 1)),
        "rows": c(np.stack([g["L0_xattn_ln_scale"], g["L0_xattn_ln_bias"], g["L1_xattn_bo"]])),
        "rows3": c(np.stack([g["L3_xattn_bv"], g["L3_xattn_gamma"], g["L3_xattn_beta"]])),
        "ident": np.eye(128, dtype=np.float32),
        "hmask": c(np.repeat(np.eye(H0, dtype=np.float32), DM // H0, 0)),
    }
    cols = np.zeros((128, NCOL), np.float32)
    for name, v in (("gate_b1", g["L0_xattn_gate_b1"]), ("gate_b2", np.broadcast_to(g["L0_xattn_gate_b2"], 128)),
                    ("ent_b", np.broadcast_to(g["L0_xattn_ent_b"], 128)), ("l1_bq", g["L1_xattn_bq"]),
                    ("l1_bk", g["L1_xattn_bk"]), ("l1_bv", g["L1_xattn_bv"]), ("l3_bq", g["L3_xattn_bq"]),
                    ("l3_bk", g["L3_xattn_bk"]), ("norm_g", g["L2_xattn_norm_g"]), ("norm_b", g["L2_xattn_norm_b"])):
        cols[0:len(v), COL[name]] = v
    cols[:, PRE_G:PRE_G + NLAYER] = g["L2_xattn_pre_g"].T
    cols[:, PRE_B:PRE_B + NLAYER] = g["L2_xattn_pre_b"].T
    cols[:, FFB:] = g["L2_xattn_ff_b1"].reshape(NLAYER * 4, 128).T
    A["cols"] = cols
    return A


def kernel(**inputs):
    import concourse.bacc as bacc
    from concourse.bass_utils import run_bass_kernel_spmd

    nc = bacc.Bacc("TRN2", target_bir_lowering=False, num_devices=1)
    arrays = layout(inputs)
    aps = {n: nc.dram_tensor("in_" + n, a.shape, mybir.dt.from_np(a.dtype), kind="ExternalInput").ap()
           for n, a in arrays.items()}
    out = nc.dram_tensor("out", (TOK, DM), F32, kind="ExternalOutput").ap()
    decoder_kernel(nc, aps, out)
    r = run_bass_kernel_spmd(nc, [{"in_" + n: a for n, a in arrays.items()}], core_ids=[0])
    return r.results[0]["out"].reshape(NB, SEQ, DM)
```

```python
from contextlib import ExitStack

import numpy as np
import concourse.bass as bass
from concourse import mybir

F32 = mybir.dt.float32
F32R = mybir.dt.float32r
BF16 = mybir.dt.bfloat16
I32 = mybir.dt.int32
ALU = mybir.AluOpType
ACT = mybir.ActivationFunctionType
AX = mybir.AxisListType

NB, SEQ, DM = 8, 256, 128
NCTX, DC = 64, 64
TOK = NB * SEQ
NT = TOK // 128
NLAYER, NH, HD, FF = 6, 16, 64, 512
NHP = NH // 2
CK = NB * NCTX
H0 = 16
NG, GT = 4, 4
GTOK = GT * 128
NEG = -float(2 ** 33)
BIG = 3.0e38

COLS = ["gate_b1", "gate_b2", "ent_b", "l1_bq", "l1_bk", "l1_bv", "l3_bq", "l3_bk", "norm_g", "norm_b"]
COL = {n: i for i, n in enumerate(COLS)}
PRE_G, PRE_B, FFB = len(COLS), len(COLS) + NLAYER, len(COLS) + 2 * NLAYER
NCOL = FFB + NLAYER * 4
ROWS = ["ln_scale", "ln_bias", "l1_bo"]
ROWS3 = ["l3_bv", "l3_gamma", "l3_beta"]
ROW = {n: i for r in (ROWS, ROWS3) for i, n in enumerate(r)}
SMALL = [("wq0", 128, 128), ("wk0T", 64, 128), ("wv0", 128, 64), ("wo0T", 128, 128), ("pos0T", 128, 64),
         ("g1x", 128, 64), ("g1p", 64, 64), ("g2", 64, 1), ("entw", 128, 1),
         ("wq1", 128, 128), ("wk1", 64, 128), ("wv1", 64, 128), ("wo1", 128, 128)]
SMALL3 = [("wq3", 128, 128), ("wk3", 64, 128), ("wv3", 64, 128)]


def offsets(parts):
    at, out = 0, {}
    for name, rows, n in parts:
        out[name] = (at, rows, n)
        at += n
    return out, at


class Queues:

    def __init__(self, names):
        self.work = {n: [] for n in names}
        self.count = {}
        self.waited = {n: {} for n in names}

    def put(self, engine, call, after=(), signal=True, by=1, sem=None):
        waits = []
        for s, v in flat(after):
            if v > self.waited[engine].get(s, 0):
                self.waited[engine][s] = v
                waits = [w for w in waits if w[0] != s] + [(s, v)]
        sem = sem or engine
        if signal:
            self.count[sem] = self.count.get(sem, 0) + by
        self.work[engine].append((waits, call, sem if signal else None, by))
        return (sem, self.count.get(sem, 0))

    def run(self, engine, handle, sems):
        for waits, call, sem, by in self.work[engine]:
            for s, v in waits:
                handle.wait_ge(sems[s], v)
            ins = call(handle)
            if sem:
                ins.then_inc(sems[sem], by)


def flat(after):
    if isinstance(after, tuple) and len(after) == 2 and isinstance(after[0], str):
        return [after]
    out = []
    for a in after:
        out += flat(a)
    return out


class Ring:

    def __init__(self, views):
        self.views, self.at = views, 0
        self.freed, self.held = [[] for _ in views], [False] * len(views)

    def take(self):
        if all(self.held):
            raise ValueError("every buffer is held")
        while self.held[self.at]:
            self.at = (self.at + 1) % len(self.views)
        i = self.at
        self.held[i] = True
        self.at = (i + 1) % len(self.views)
        return i, self.views[i], self.freed[i]

    def free(self, i, after):
        self.freed[i], self.held[i] = flat(after), False


class Background:

    def __init__(self):
        self.chains = []

    def start(self, chain):
        self.chains.append(chain)

    def tick(self, times=1):
        for _ in range(times):
            for chain in list(self.chains):
                try:
                    next(chain)
                except StopIteration:
                    self.chains.remove(chain)

    def until(self, marks, mark):
        while mark not in marks:
            self.tick()

    def drain(self):
        while self.chains:
            self.tick()


def decoder_kernel(nc, A, out):
    q = Queues(["pe", "act", "dve", "pool", "sp"])
    ctx = ExitStack()
    with ctx:
        def sb(name, shape, dt=F32):
            return ctx.enter_context(nc.sbuf_tensor(name, shape, dt))

        def mm(o, l, r, start=True, stop=True, after=(), signal=False):
            return q.put("pe", lambda e: e.matmul(o, l, r, start=start, stop=stop), after, signal)

        def mm3(o, l, r, after=(), signal=False, more=False):
            mm(o, l[0], r[0], True, False, after)
            mm(o, l[0], r[1], False, False)
            return mm(o, l[1], r[0], False, not more, (), signal)

        def tr(o, i, after=(), signal=False):
            return q.put("pe", lambda e: e.transpose(o, i, ident[:, :]), after, signal)

        def act(o, i, f=ACT.Copy, bias=0.0, scale=1.0, accum=None, after=()):
            if f == ACT.Copy:
                return q.put("act", lambda e: e.copy(o, i), after)
            if accum is None:
                return q.put("act", lambda e: e.activation(o, i, f, bias=bias, scale=scale), after)
            return q.put("act", lambda e: e.activation(o, i, f, bias=bias, scale=scale, accum_out=accum), after)

        def copy(eng, o, i, after=()):
            if eng == "act":
                return act(o, i, after=after)
            return q.put(eng, lambda e: e.tensor_copy(o, i), after)

        def tt(eng, o, a, b, op, after=()):
            return q.put(eng, lambda e: e.tensor_tensor(o, a, b, op), after)

        def ts(eng, o, a, s1, s2, op0, op1=None, after=()):
            if op1 is None:
                return q.put(eng, lambda e: e.tensor_scalar(o, a, s1, None, op0), after)
            return q.put(eng, lambda e: e.tensor_scalar(o, a, s1, s2, op0, op1), after)

        def stt(o, a, s, b, op0, op1, after=()):
            return q.put("dve", lambda e: e.scalar_tensor_tensor(out=o, in0=a, scalar=s, in1=b, op0=op0, op1=op1), after)

        def red(o, i, op, after=()):
            return q.put("dve", lambda e: e.tensor_reduce(o, i, AX.X, op), after)

        def recip(o, i, after=()):
            return q.put("dve", lambda e: e.reciprocal(o, i), after)

        def fill(eng, o, v, after=()):
            return q.put(eng, lambda e: e.memset(o, v), after)

        def load(o, i, group, after=()):
            return q.put("sp", lambda e: e.dma_start(o, i), after, by=16, sem="ld_" + group)

        def tables(after=()):
            q.put("act", lambda e: e.preload_act_table_set("natural_log_exp_and_others"), after, signal=False)

        t = sb("t", [128, NT, DM])
        tn_hi = sb("tn_hi", [128, TOK], F32R)
        tn_lo = sb("tn_lo", [128, TOK], F32R)
        maskb = sb("maskb", [128, NT, SEQ], BF16)
        big_hi = sb("big_hi", [128, 8192], F32R)
        big_lo = sb("big_lo", [128, 8192], F32R)
        vals = sb("vals", [128, 8192])
        ag_hi = sb("ag_hi", [128, 2048], F32R)
        ag_lo = sb("ag_lo", [128, 2048], F32R)
        wv_hi = sb("wv_hi", [128, 1024], F32R)
        wv_lo = sb("wv_lo", [128, 1024], F32R)
        wo = sb("wo", [128, NHP, DM])
        stage = sb("stage", [128, 3072])
        uHH = sb("uHH", [128, CK + NCTX], F32R)
        uLL = sb("uLL", [128, CK + NCTX], F32R)
        mHH = sb("mHH", [128, CK], F32R)
        mLL = sb("mLL", [128, CK], F32R)
        work = sb("work", [128, 3, 1024])
        lnbuf = sb("lnbuf", [128, 2, 512])
        pt = sb("pt", [128, 2, 1024])
        ident = sb("ident", [128, 128])
        cols = sb("cols", [128, NCOL])
        rows = sb("rows", [128, len(ROWS), DM])
        lrows = sb("lrows", [128, 3, DM])
        rowscale = sb("rowscale", [128, NT])
        maskrow = sb("maskrow", [128, CK], BF16)
        ones = sb("ones", [128, 128], BF16)
        hmask = sb("hmask", [128, H0])
        st = sb("st", [128, 3, GT, 6])
        mv = sb("mv", [128, 3, GT, 2])
        ve = sb("ve", [128, 3, 3, GT])
        nmx = sb("nmx", [128, 4, 4])
        den = sb("den", [128, 4, 4])
        rden = sb("rden", [128, 4, 4])
        cmx = sb("cmx", [128, 4, 16])
        csum = sb("csum", [128, 4, 16])
        crec = sb("crec", [128, 4, 16])
        gate = sb("gate", [128, NT])
        rmask = sb("rmask", [128, NB])
        rinv = sb("rinv", [128, NB])
        psums = [ctx.enter_context(nc.psum_tensor(f"ps{i}", [128, 512], F32)) for i in range(8)]
        bank = Ring(psums)
        slot = Ring([work[:, i, :] for i in range(3)])
        lnslot = Ring([lnbuf[:, i, :] for i in range(2)])
        ptslot = Ring([pt[:, i, :] for i in range(2)])
        smslot = Ring(list(range(4)))
        csslot = Ring(list(range(4)))
        stslot = Ring(list(range(3)))
        vals_free = [[] for _ in range(4)]
        tn_free = [[] for _ in range(NG)]
        tn_ready = [None] * NG
        t_ready = [[] for _ in range(NT)]
        S = {}
        back = Background()

        def f(ap):
            return ap.bitcast(F32)

        def col(name):
            return cols[:, COL[name]:COL[name] + 1]

        def split(i, hi, lo, after):
            a = act(hi, i, after=after)
            return tt("dve", lo, i, f(hi), ALU.subtract, after=[a])

        def split_sb(i, hi, lo, after, wr=()):
            a = act(hi, i, after=[after, wr])
            return [a, tt("pool", lo, i, f(hi), ALU.subtract, after=[a])]

        so, n_small = offsets(SMALL)
        so3, n_small3 = offsets(SMALL3)
        assert n_small <= 1536
        ctxT = stage[:, 2560:3072]
        wv_raw0 = stage[:, 1536:2560]

        def small(name, o=so):
            at, r, n = o[name]
            return stage[0:r, at:at + n]

        xT = vals[:, 0:TOK]
        kT0, v1 = vals[:, TOK:TOK + CK], vals[:, TOK + CK:TOK + 2 * CK]
        k1, vw = wo[:, 4:8, :], wo[:, 0:4, :]
        loaded_xT = load(xT, A["xT"], "xT")
        load(stage[:, 0:n_small], A["small"], "in")
        load(ctxT[0:64, :], A["ctxT"], "in")
        load(ctxT[64:128, :], A["ctxT"], "in")
        loaded = load(hmask[:, :], A["hmask"], "in")
        loaded_id = load(ident[:, :], A["ident"], "id")
        got_a = load(pt[:, 0, :], A["wqT"][0], "self")
        got_a = load(pt[:, 1, :], A["wkT"][0], "self")
        loaded_cols = load(cols[:, :], A["cols"], "cols")
        mi = lnbuf[:, 0, :].bitcast(I32)
        loaded_m2 = load(mi, A["mask2"].rearrange("(o k) -> o k", o=1).to_broadcast([128, CK]), "m2")
        load(wv_raw0, A["wv"][0], "wv0")
        loaded_x = load(t[:, :, :], A["x"].rearrange("(n p) d -> p n d", p=128), "x")
        loaded_rows = load(rows[:, :, :], A["rows"].rearrange("(o r) d -> o r d", o=1).to_broadcast([128, len(ROWS), DM]), "rows")
        for n in range(NT):
            t_ready[n] = [loaded_x]
        tables()
        ones_set = fill("pool", ones[:, :], 1.0)
        entw = work[:, 0, 0:NB * NB].rearrange("p (b c) -> p b c", b=NB)
        entw_zero = fill("pool", entw, 0.0)
        mrow_zero = fill("pool", maskrow[:, :], 0.0)

        i, ps, freed = bank.take()
        m = mm(ps[:, :], small("wk0T"), ctxT[0:64, :], after=[freed, loaded], signal=True)
        kT0_ready = tt("dve", kT0.rearrange("p (b k) -> p b k", b=NB), ps[:, :].rearrange("p (b k) -> p b k", b=NB),
                       small("pos0T").unsqueeze(1).to_broadcast([128, NB, NCTX]), ALU.add, after=[m])
        bank.free(i, kT0_ready)
        k1f = k1.rearrange("p a d -> p (a d)")
        for w, b_, dst in (("wk1", "l1_bk", k1f), ("wv1", "l1_bv", v1)):
            i, ps, freed = bank.take()
            m = mm(ps[:, :], small(w), ctxT[0:64, :], after=[freed], signal=True)
            kv1_ready = act(dst, ps[:, :], ACT.Identity, bias=col(b_), after=[m, loaded_cols])
            bank.free(i, kv1_ready)
        i, ps, freed = bank.take()
        for a in range(NB // 2):
            v1_read = mm(ps[:, DM * a:DM * a + DM], v1[:, 128 * a:128 * a + 128], small("wo1"), after=[freed, kv1_ready],
                         signal=(a == NB // 2 - 1))
        vw_ready = copy("act", vw, ps[:, :].rearrange("p (a d) -> p a d", a=NB // 2), after=[v1_read])
        bank.free(i, vw_ready)

        for g in range(NG):
            s = slice(GTOK * g, GTOK * g + GTOK)
            tn_ready[g] = split_sb(xT[:, s], tn_hi[:, s], tn_lo[:, s], loaded_xT)
        u_parts = []
        for dst, src in ((slice(0, CK), slice(0, CK)), (slice(CK, CK + NCTX), slice(0, NCTX))):
            u_parts.append(split_sb(ctxT[:, src], uHH[:, dst], uLL[:, dst], loaded))

        for b in range(NB):
            z2 = copy("dve", entw[:, b, b:b + 1], small("entw"), after=[entw_zero, loaded])
        i, ps, freed = bank.take()
        for b in range(NB):
            last = mm(ps[0:NB, 0:SEQ], entw[:, b, :], xT[:, SEQ * b:SEQ * b + SEQ], b == 0, b == NB - 1,
                      after=[freed, z2, loaded_xT], signal=(b == NB - 1))
        e_bank = i

        def entropy_gate(buf):
            e_l, e_p, e_g = buf[0:NB, 128:384], buf[0:NB, 384:640], buf[0:NB, 640:896]
            e_s, e_1 = buf[0:NB, 64:96], buf[0:NB, 896:1024]
            o8 = fill("pool", e_1, 1.0)
            k = ts("dve", e_l, psums[e_bank][0:NB, 0:SEQ], cols[0:NB, COL["ent_b"]:COL["ent_b"] + 1], None, ALU.add,
                   after=[last, loaded_cols])
            bank.free(e_bank, k)
            k = red(e_s[:, 0:1], e_l, ALU.max, after=[k])
            k = ts("dve", e_l, e_l, e_s[:, 0:1], None, ALU.subtract, after=[k])
            k = act(e_p, e_l, ACT.Exp, accum=e_s[:, 1:2], after=[k])
            yield
            k = recip(e_s[:, 2:3], e_s[:, 1:2], after=[k])
            k = ts("dve", e_p, e_p, e_s[:, 2:3], None, ALU.mult, after=[k])
            k = ts("dve", e_l, e_p, 1e-9, None, ALU.add, after=[k])
            k = act(e_g, e_l, ACT.Ln, after=[k])
            yield
            k = tt("dve", e_g, e_g, e_p, ALU.mult, after=[k])
            k = red(e_s[:, 3:4], e_g, ALU.add, after=[k])
            k = ts("dve", e_s[:, 4:5], e_s[:, 3:4], -1.0, None, ALU.is_lt, after=[k])
            k = ts("dve", e_s[:, 8:16], ident[0:NB, 0:NB], e_s[:, 4:5], None, ALU.mult, after=[k, loaded_id])
            yield
            i, ps, freed = bank.take()
            k = mm(ps[:, 0:NB], e_1, e_s[:, 8:16], after=[freed, k, o8], signal=True)
            k = copy("dve", rmask[:, :], ps[:, 0:NB], after=[k])
            bank.free(i, k)
            S["rmask"] = ts("dve", rinv[:, :], rmask[:, :], -1.0, 1.0, ALU.mult, ALU.add, after=[k])

        def output_gate(buf):
            pooled, gbias = buf[0:64, 96:96 + NB], buf[0:64, 104:104 + NB]
            k = red(pooled, ctxT[0:64, :].rearrange("c (b k) -> c b k", b=NB), ALU.add, after=[loaded])
            k = ts("dve", pooled, pooled, 1.0 / NCTX, None, ALU.mult, after=[k])
            i, ps, freed = bank.take()
            k = mm(ps[0:64, 0:NB], small("g1p"), pooled, after=[freed, k], signal=True)
            bias_set = ts("dve", gbias, ps[0:64, 0:NB], cols[0:64, COL["gate_b1"]:COL["gate_b1"] + 1], None, ALU.add,
                          after=[k, loaded_cols])
            bank.free(i, bias_set)
            gi, gps, gfreed = bank.take()
            silu = lnbuf[0:64, 1, :]
            read = []
            for g in range(NG):
                i, ps, freed = bank.take()
                m = mm(ps[0:64, :], small("g1x"), xT[:, GTOK * g:GTOK * g + GTOK], after=[freed, loaded_xT], signal=True)
                yield
                halves = [(slice(SEQ * b, SEQ * b + SEQ), gbias[:, 2 * g + b:2 * g + b + 1]) for b in range(2)]
                for at, bias in halves:
                    a = act(silu[:, at], ps[0:64, at], ACT.Sigmoid, bias=bias, after=[m, bias_set, read])
                for at, bias in halves:
                    h = stt(silu[:, at], ps[0:64, at], bias, silu[:, at], ALU.add, ALU.mult, after=[a])
                bank.free(i, h)
                yield
                for n in range(GT):
                    read = mm(gps[:, GT * g + n:GT * g + n + 1], silu[:, 128 * n:128 * n + 128], small("g2"),
                              after=[h, gfreed], signal=(n == GT - 1))
            S["gate"] = act(gate[:, :], gps[:, 0:NT], ACT.Sigmoid, bias=col("gate_b2"), after=[read])
            bank.free(gi, S["gate"])
            tables()
            S["gate_in"] = [h, read]
            yield
            m01 = ts("dve", lnbuf[:, 1, :], mi, 0.0, None, ALU.not_equal, after=[loaded_m2, read])
            S["mrow"] = ts("dve", maskrow[0:1, :], mi[0:1, :], 0.0, NEG, ALU.is_equal, ALU.mult,
                           after=[loaded_m2, mrow_zero])
            cm = tt("dve", lnbuf[:, 0, :], ctxT, lnbuf[:, 1, :], ALU.mult, after=[m01, S["mrow"], loaded])
            yield
            S["m_parts"] = split_sb(lnbuf[:, 0, :], mHH[:, :], mLL[:, :], cm)
            lnslot.free(0, S["m_parts"])
            lnslot.free(1, cm)

        def masked_heads(j, buf, src, heads):
            for c, h in enumerate(heads):
                k = ts("pool" if c % 4 == 3 else "dve", buf[:, 128 * c:128 * c + 128], small(src), hmask[:, h:h + 1],
                       None, ALU.mult, after=[slot.freed[j], loaded])
                S["mh", c] = k
            return [S["mh", c] for c in range(len(heads))]

        def store_stack(ps, dst, m, after):
            a = act(dst, ps[:, :], after=[m, after])
            return tt("dve", dst[64:128, :], ps[64:128, :], f(dst[64:128, :]), ALU.subtract, after=[a])

        C_hi = big_hi[:, :].rearrange("p (b h k) -> p b h k", b=NB, h=NH)
        C_lo = big_lo[:, :].rearrange("p (b h k) -> p b h k", b=NB, h=NH)
        Vp = vals[:, :].rearrange("p (b h d) -> p b h d", b=NB, h=NHP)

        j0, buf0, _ = slot.take()
        back.start(entropy_gate(buf0))
        back.start(output_gate(buf0))
        back.tick()
        c_ready = []
        for half in range(2):
            j, WM, _ = slot.take()
            wm = masked_heads(j, WM, "wq0", range(8 * half, 8 * half + 8))
            for c in range(8):
                i, ps, freed = bank.take()
                m = mm(ps[:, :], WM[:, 128 * c:128 * c + 128], kT0, after=[freed, wm[c], kT0_ready], signal=True)
                k = split(ps[:, :].rearrange("p (b k) -> p b k", b=NB), C_hi[:, :, 8 * half + c, :],
                          C_lo[:, :, 8 * half + c, :], [m])
                bank.free(i, k)
                c_ready = [k]
                back.tick()
            slot.free(j, m)
        kT0_read = m
        h_ready = []
        H_first = (wv_hi, wv_lo)
        for par in range(2):
            j, WM, _ = slot.take()
            wm = masked_heads(j, WM, "wo0T", range(par, 16, 2))
            for half in range(2):
                i, ps, freed = bank.take()
                for twice in range(2):
                    m = mm(ps[64 * twice:64 * twice + 64, :], small("wv0"), WM[:, 512 * half:512 * half + 512],
                           after=[freed, wm], signal=True)
                k = store_stack(ps, H_first[par][:, 512 * half:512 * half + 512], m, [])
                bank.free(i, k)
                h_ready.append(k)
            slot.free(j, m)
        weights_read = m
        back.tick()

        def self_weights(qT, kT, got, ag_free):
            ready = []
            for half in range(2):
                for par in range(2):
                    i, ps, freed = bank.take()
                    p = slice(64 * par, 64 * par + 64)
                    for c in range(4):
                        hp = 4 * half + c
                        m = mm(ps[:, 128 * c:128 * c + 128], kT[p, 128 * hp:128 * hp + 128], qT[p, 128 * hp:128 * hp + 128],
                               after=[freed, got], signal=(c == 3))
                    at = slice(1024 * half + 512 * par, 1024 * half + 512 * par + 512)
                    k = split(ps[:, :], ag_hi[:, at], ag_lo[:, at], [m, ag_free])
                    bank.free(i, k)
                    ready.append(k)
            S["A"] = ready
            return m

        a_read = self_weights(pt[:, 0, :], pt[:, 1, :], got_a, [])
        ptslot.free(0, a_read)
        ptslot.free(1, a_read)

        back.drain()
        slot.free(j0, [S["gate_in"], S["rmask"]])
        xT_read = [S["gate_in"], last, flat(tn_ready), kT0_read, v1_read]

        def self_mask(room):
            mask_v = A["mask"].rearrange("(n p) k -> p n k", p=128)
            raws = [stage[:, at:at + 2 * SEQ].bitcast(I32).rearrange("p (n k) -> p n k", n=2) for at in (0, 1024)]
            ld = [load(raws[i], mask_v[:, 2 * i:2 * i + 2, :], f"mask{i}", after=room) for i in range(2)]
            yield
            for n in range(0, NT, 2):
                i = n // 2 % 2
                k = ts("pool", maskb[:, n:n + 2, :], raws[i], 0.0, NEG, ALU.is_equal, ALU.mult, after=[ld[i]])
                if n + 4 < NT:
                    ld[i] = load(raws[i], mask_v[:, n + 4:n + 6, :], f"mask{i}", after=k)
                yield
                k = red(rowscale[:, n:n + 2], maskb[:, n:n + 2, :], ALU.max, after=[k])
                S["mask"] = ts("dve", rowscale[:, n:n + 2], rowscale[:, n:n + 2], 0.0, -0.125, ALU.is_equal, ALU.mult,
                               after=[k])
                yield

        def values_through(H, after, free, ready):
            for b in range(NB):
                for par in range(2):
                    for half in range(2):
                        i, ps, freed = bank.take()
                        r = H[par][:, 512 * half:512 * half + 512]
                        at = NCTX * ((b - par) % NB)
                        for n, part in enumerate((uHH, uLL)):
                            m = mm(ps[:, :], part[:, at:at + 2 * NCTX], r, n == 0, n == 1,
                                   after=[freed, after, u_parts], signal=(n == 1))
                        p = slice(64 * par, 64 * par + 64)
                        e = copy("act" if half else "dve", Vp[p, b, 4 * half:4 * half + 4, :],
                                 ps[p, :].rearrange("p (h d) -> p h d", h=4), after=[m, free])
                        bank.free(i, e)
                        ready.setdefault(b, []).append(e)
                yield
            S["H_read"] = m

        def first_values(ready):
            yield from values_through(H_first, h_ready, xT_read, ready)
            S["Wv"] = split_sb(wv_raw0, wv_hi[:, :], wv_lo[:, :], ("ld_wv0", 16), S["H_read"])

        back.start(self_mask([xT_read, weights_read]))
        v_ready = {}
        back.start(first_values(v_ready))

        def cross_tiles(scale, c_ready, v_ready, masked, finish, chain):
            state = {}

            def scores(n):
                b = n // 2
                cs = slice(128 * n, 128 * n + 128)
                j, P, pfreed = slot.take()
                x, _, xfreed = csslot.take()
                subs = []
                for half in range(2):
                    i, ps, freed = bank.take()
                    hs = slice(8 * half, 8 * half + 8)
                    m = mm3(ps[:, :], (tn_hi[:, cs], tn_lo[:, cs]), (C_hi[:, b, hs, :], C_lo[:, b, hs, :]),
                            after=[freed, c_ready, tn_ready[n // GT]], signal=not masked, more=masked)
                    if masked:
                        mr = maskrow[:, NCTX * b:NCTX * b + NCTX].unsqueeze(1).to_broadcast([128, 8, NCTX])
                        m = mm(ps[:, :], ones[:, :], mr, False, True, after=[S["mrow"], ones_set], signal=True)
                    v = ps[:, :].rearrange("p (h k) -> p h k", h=8)
                    k = red(cmx[:, x, hs], v, ALU.max, after=[m, xfreed])
                    k = tt("dve", P[:, 512 * half:512 * half + 512].rearrange("p (h k) -> p h k", h=8), v,
                           cmx[:, x, hs].unsqueeze(2).to_broadcast([128, 8, NCTX]), ALU.subtract, after=[k, pfreed])
                    bank.free(i, k)
                    subs.append(k)
                tn_free[n // GT] = [m]
                S["c_used"] = m
                state[n] = [j, P, x, subs]

            def exponents(n):
                j, P, x, subs = state[n]
                state[n] = [j, P, x, act(P, P, ACT.Exp, scale=scale, after=[subs])]

            def normal(n):
                j, P, x, a = state[n]
                P3 = P.rearrange("p (h k) -> p h k", h=NH)
                k = red(csum[:, x, :], P3, ALU.add, after=[a])
                k = recip(crec[:, x, :], csum[:, x, :], after=[k])
                k = tt("pool", P3, P3, crec[:, x, :].unsqueeze(2).to_broadcast([128, NH, NCTX]), ALU.mult, after=[k])
                csslot.free(x, k)
                state[n] = [j, P, k]

            def turn(n):
                j, P, p_ready = state[n]
                y, T, tfreed = ptslot.take()
                ev = []
                for half in range(2):
                    i, ps, freed = bank.take()
                    for c in range(4):
                        m = tr(ps[:, 128 * c:128 * c + 128], P[:, 512 * half + 128 * c:512 * half + 128 * c + 128],
                               after=[freed, p_ready], signal=(c == 3))
                    ev.append(copy("act", T[:, 512 * half:512 * half + 512], ps[:, :], after=[m, tfreed]))
                    bank.free(i, ev[-1])
                slot.free(j, m)
                state[n] = [y, T, ev]

            def output(n):
                y, T, ev = state.pop(n)
                i, ps, freed = bank.take()
                for hp in range(NHP):
                    m = mm(ps[:, 0:DM], T[:, 128 * hp:128 * hp + 128], Vp[:, n // 2, hp, :], hp == 0, hp == NHP - 1,
                           after=[freed, ev[hp // 4], v_ready[n // 2]], signal=(hp == NHP - 1))
                ptslot.free(y, m)
                vals_free[n // GT] = [m]
                bank.free(i, finish(n, ps[:, 0:DM], m))

            for n in range(NT + 3):
                if 1 <= n <= NT:
                    normal(n - 1)
                back.tick()
                if n < NT:
                    scores(n)
                if n >= 3:
                    output(n - 3)
                    if (n - 3) % GT == GT - 1:
                        back.start(chain((n - 3) // GT))
                if 2 <= n < NT + 2:
                    turn(n - 2)
                if n < NT:
                    exponents(n)
                back.tick()

        def statistics(srcs, eps, after):
            x, _, xfreed = stslot.take()
            n = len(srcs)
            for c, src in enumerate(srcs):
                k = q.put("dve", bn_call(st[:, x, c, :], src), [after[c], xfreed])
                if c == n // 2 - 1:
                    yield
            for c in range(n):
                k2 = q.put("dve", aggr_call(mv[:, x, c, :], st[:, x, c, :]), [k])
            v, y, w = ve[:, x, 0, 0:n], ve[:, x, 1, 0:n], ve[:, x, 2, 0:n]
            k = ts("dve", v, mv[:, x, 0:n, 1], eps, None, ALU.add, after=[k2])
            a = act(y, v, ACT.Ln, after=[k])
            a = act(y, y, ACT.Exp, scale=-0.5, after=[a])
            yield
            k = tt("dve", w, v, y, ALU.mult, after=[a])
            k = tt("dve", w, w, y, ALU.mult, after=[k])
            k = ts("dve", w, w, -0.5, 1.5, ALU.mult, ALU.add, after=[k])
            return x, tt("dve", mv[:, x, 0:n, 1], w, y, ALU.mult, after=[k])

        def load_bias(l, r, after):
            S["lrows", r] = load(lrows[:, r, :], A["lrows"][l, r:r + 1, :].to_broadcast([128, DM]), f"bias{r}", after)

        def layer_norm(g, gcol, bcol, l, r, keep=False):
            j, buf, jfreed = lnslot.take()
            x, k = yield from statistics([t[:, GT * g + c, :] for c in range(GT)], 1e-5,
                                         [t_ready[GT * g + c] for c in range(GT)])
            xs = []
            for c in range(GT):
                xs.append(ts("dve", buf[:, 128 * c:128 * c + 128], t[:, GT * g + c, :], mv[:, x, c, 0:1],
                             mv[:, x, c, 1:2], ALU.subtract, ALU.mult, after=[k, jfreed]))
            stslot.free(x, xs)
            tv = t[:, GT * g:GT * g + GT, :]
            k = tt("pool", tv, tv, lrows[:, r, :].unsqueeze(1).to_broadcast([128, GT, DM]), ALU.add,
                   after=[S["lrows", r], xs])
            for n in range(GT * g, GT * g + GT):
                t_ready[n] = [k]
            if g == NG - 1 and l + 1 < NLAYER:
                load_bias(l + 1, r, k)
            yield
            yield
            i, ps, freed = bank.take()
            for c in range(GT):
                m = tr(ps[:, 128 * c:128 * c + 128], buf[:, 128 * c:128 * c + 128], after=[freed, xs[c]],
                       signal=(c == GT - 1))
            a = act(buf, ps[:, :], ACT.Identity, bias=bcol, scale=gcol, after=[m])
            bank.free(i, a)
            if keep:
                S["kept", g] = (j, buf, a)
            else:
                s = slice(GTOK * g, GTOK * g + GTOK)
                tn_ready[g] = split_sb(buf, tn_hi[:, s], tn_lo[:, s], a, tn_free[g])
                lnslot.free(j, tn_ready[g])
            yield

        norm = (col("norm_g"), col("norm_b"))

        def finish0(n, ps, m):
            if n % GT == 0:
                S["h"] = lnslot.take()
                S["h_done"] = []
            _, buf, freed = S["h"]
            c = n % GT
            k = stt(buf[:, 128 * c:128 * c + 128], ps, gate[:, n:n + 1], t[:, n, :], ALU.mult, ALU.add,
                    after=[m, freed, S["gate"], t_ready[n]])
            S["h_done"].append(k)
            if c == GT - 1:
                S["h_of", n // GT] = (S["h"], S["h_done"])
            return k

        def first_and_second(g):
            (j, buf, _), done = S["h_of", g]
            x, k = yield from statistics([buf[:, 128 * c:128 * c + 128] for c in range(GT)], 1e-5, [[k] for k in done])
            for c in range(GT):
                h = buf[:, 128 * c:128 * c + 128]
                kx = ts("dve", h, h, mv[:, x, c, 0:1], mv[:, x, c, 1:2], ALU.subtract, ALU.mult, after=[k])
            stslot.free(x, kx)
            h3 = buf.rearrange("p (n d) -> p n d", n=GT)
            k = tt("pool", h3, h3, rows[:, ROW["ln_scale"], :].unsqueeze(1).to_broadcast([128, GT, DM]), ALU.mult,
                   after=[kx, loaded_rows])
            k = tt("pool", h3, h3, rows[:, ROW["ln_bias"], :].unsqueeze(1).to_broadcast([128, GT, DM]), ALU.add, after=[k])
            yield
            for b in range(2):
                hb = buf[:, SEQ * b:SEQ * b + SEQ].rearrange("p (n d) -> p n d", n=2)
                tv = t[:, GT * g + 2 * b:GT * g + 2 * b + 2, :]
                e = 2 * g + b
                k2 = ts("dve", hb, hb, rmask[:, e:e + 1], None, ALU.mult, after=[k, S["rmask"]])
                k2 = stt(tv, tv, rinv[:, e:e + 1], hb, ALU.mult, ALU.add, after=[k2])
            lnslot.free(j, k2)
            at = 2048 * g
            tT, q1 = vals[:, at:at + 512], vals[:, at + 512:at + 1024]
            zp = vals[:, at + 1024:at + 1536].rearrange("p (n c) -> p n c", n=GT)
            P3 = vals[:, at + 1536:at + 1792].rearrange("p (n k) -> p n k", n=GT)
            zero = fill("pool", zp, 0.0, after=vals_free[g])
            yield
            yield
            i, ps, freed = bank.take()
            for c in range(GT):
                m = tr(ps[:, 128 * c:128 * c + 128], t[:, GT * g + c, :], after=[freed, k2], signal=(c == GT - 1))
            e = copy("act", tT, ps[:, :], after=[m, vals_free[g]])
            bank.free(i, e)
            yield
            i, ps, freed = bank.take()
            m = mm(ps[:, :], small("wq1"), tT, after=[freed, e], signal=True)
            a = act(q1, ps[:, :], ACT.Identity, bias=col("l1_bq"), after=[m, vals_free[g]])
            bank.free(i, a)
            yield
            i, ps, freed = bank.take()
            for c in range(GT):
                b = 2 * g + c // 2
                m = mm(ps[:, 64 * c:64 * c + 64], q1[:, 128 * c:128 * c + 128], k1f[:, NCTX * b:NCTX * b + NCTX],
                       after=[freed, a, kv1_ready], signal=(c == GT - 1))
            yield
            x, _, xfreed = csslot.take()
            v = ps[:, 0:256].rearrange("p (n k) -> p n k", n=GT)
            k = red(cmx[:, x, 0:GT], v, ALU.max, after=[m, xfreed])
            k = tt("dve", P3, v, cmx[:, x, 0:GT].unsqueeze(2).to_broadcast([128, GT, NCTX]), ALU.subtract,
                   after=[k, vals_free[g]])
            bank.free(i, k)
            a = act(P3, P3, ACT.Exp, scale=float(DM) ** -0.5, after=[k])
            yield
            k = red(csum[:, x, 0:GT], P3, ALU.add, after=[a])
            k = recip(crec[:, x, 0:GT], csum[:, x, 0:GT], after=[k])
            for par in range(2):
                n2 = slice(2 * par, 2 * par + 2)
                kz = tt("dve", zp[:, n2, 64 * par:64 * par + 64], P3[:, n2, :],
                        crec[:, x, n2].unsqueeze(2).to_broadcast([128, 2, NCTX]), ALU.mult, after=[k, zero])
            csslot.free(x, kz)
            yield
            i, ps, freed = bank.take()
            for c in range(GT):
                m = tr(ps[:, 128 * c:128 * c + 128], zp[:, c, :], after=[freed, kz], signal=(c == GT - 1))
            e = copy("act", tT, ps[:, :], after=[m])
            bank.free(i, e)
            yield
            i, ps, freed = bank.take()
            for c in range(GT):
                m = mm(ps[:, 128 * c:128 * c + 128], tT[:, 128 * c:128 * c + 128], vw[:, g, :],
                       after=[freed, e, vw_ready], signal=(c == GT - 1))
            vals_free[g] = [m]
            S["stage_read"] = m
            yield
            tv = t[:, GT * g:GT * g + GT, :]
            k = tt("dve", tv, ps[:, :].rearrange("p (n d) -> p n d", n=GT), tv, ALU.add, after=[m])
            bank.free(i, k)
            k = tt("pool", tv, tv, rows[:, ROW["l1_bo"], :].unsqueeze(1).to_broadcast([128, GT, DM]), ALU.add, after=[k])
            for c in range(GT):
                t_ready[GT * g + c] = [k]
            S["over", 0, g] = True
            yield
            yield from layer_norm(g, *norm, 0, 0)

        for r in range(3):
            load_bias(0, r, [])
        cross_tiles(float(DM // H0) ** -0.5, c_ready, v_ready, False, finish0, first_and_second)

        w_hi = big_hi[:, :].rearrange("p (c b h k) -> p c b h k", c=NHP, b=2, h=2)
        w_lo = big_lo[:, :].rearrange("p (c b h k) -> p c b h k", c=NHP, b=2, h=2)
        V = vals[:, 0:4096].rearrange("p (n e) -> p n e", n=GT)
        oT = vals[:, 4096:8192].rearrange("p (b h k) -> p b h k", b=2, h=NHP)
        hT = vals[:, :].rearrange("p (g c k) -> p g c k", g=NG, c=4)
        w1, w2 = stage[:, 0:512], stage[:, 512:1024]

        def load_self(l, after):
            load(stage[:, 0:1024], A["wqT"][l], "self", after)
            load(stage[:, 1024:2048], A["wkT"][l], "self", after)
            return load(stage[:, 2048:3072], A["wv"][l], "self", after)

        def load_cross(l, after):
            load(stage[:, 0:1024], A["cqT"][l], "cross", after)
            load(stage[:, 1024:1536], A["ckT"][l], "cross", after)
            load(stage[:, 1536:2048], A["cvT"][l], "cross", after)
            return load(stage[:, 2048:3072], A["co"][l], "cross", after)

        def a_slice(h):
            hp, par = h // 2, h % 2
            at = 1024 * (hp // 4) + 512 * par + 128 * (hp % 4)
            return ag_hi[:, at:at + 128], ag_lo[:, at:at + 128]

        def w_project(g, hp, after):
            s = slice(GTOK * g, GTOK * g + GTOK)
            ready = []
            for par in range(2):
                i, ps, freed = bank.take()
                m = mm3(ps[:, :], a_slice(2 * hp + par), (tn_hi[:, s], tn_lo[:, s]),
                        after=[freed, S["A"], tn_ready[g]], signal=True)
                v = ps[:, :].rearrange("p (b k) -> p b k", b=2)
                k = split(v, w_hi[:, hp, :, par, :], w_lo[:, hp, :, par, :], [m, after])
                bank.free(i, k)
                ready.append(k)
            S["w", hp] = ready
            S["A_read"] = m

        def v_project(g, half, n, after):
            i, ps, freed = bank.take()
            cs = slice(GTOK * g + 128 * n, GTOK * g + 128 * n + 128)
            es = slice(512 * half, 512 * half + 512)
            m = mm3(ps[:, :], (tn_hi[:, cs], tn_lo[:, cs]), (wv_hi[:, es], wv_lo[:, es]),
                    after=[freed, S["Wv"], tn_ready[g]], signal=True)
            S["V", half, n] = copy("dve" if n % 2 else "act", V[:, n, es], ps[:, :], after=[m, after])
            bank.free(i, S["V", half, n])
            S["wv_read"] = m

        def ttr(o, i, m, s, acc, after):
            return q.put("dve", lambda e: e.tensor_tensor_reduce(o, i, m, s, BIG, ALU.add, ALU.min, acc), after)

        def unit_scores(g, hp, b):
            j, P, pfreed = slot.take()
            x, _, xfreed = smslot.take()
            P4 = P.rearrange("p (a h k) -> p a h k", a=2, h=2)
            ex = []
            for a in range(2):
                n = GT * g + 2 * b + a
                i, ps, freed = bank.take()
                cs = slice(128 * n, 128 * n + 128)
                m = mm3(ps[:, :], (tn_hi[:, cs], tn_lo[:, cs]), (w_hi[:, hp, b, :, :], w_lo[:, hp, b, :, :]),
                        after=[freed, S["w", hp], tn_ready[g]], signal=True)
                for h in range(2):
                    c = 2 * a + h
                    k = ttr(P4[:, a, h, :], ps[:, 256 * h:256 * h + 256], maskb[:, n, :], rowscale[:, n:n + 1],
                            nmx[:, x, c:c + 1], [m, pfreed, xfreed, S["mask"]])
                    ex.append(act(P4[:, a, h, :], P4[:, a, h, :], ACT.Exp, bias=nmx[:, x, c:c + 1], scale=-1.0,
                                  accum=den[:, x, c:c + 1], after=[k]))
                bank.free(i, k)
            S["scores_read"] = m
            return j, P4, x, ex

        def unit_normal(u):
            j, P4, x, ex = u
            pn = []
            r = recip(rden[:, x, :], den[:, x, :], after=[ex])
            for a in range(2):
                pn.append(tt("pool", P4[:, a, :, :], P4[:, a, :, :],
                             rden[:, x, 2 * a:2 * a + 2].unsqueeze(2).to_broadcast([128, 2, SEQ]), ALU.mult, after=[r]))
            smslot.free(x, pn)
            return j, P4, pn

        def unit_turn(u):
            j, P4, pn = u
            y, T, tfreed = ptslot.take()
            ev = []
            for h in range(2):
                i, ps, freed = bank.take()
                for a in range(2):
                    for kt in range(2):
                        m = tr(ps[:, 256 * kt + 128 * a:256 * kt + 128 * a + 128], P4[:, a, h, 128 * kt:128 * kt + 128],
                               after=[freed, pn[a]], signal=(kt == 1 and a == 1))
                ev.append(copy("dve" if h else "act", T[:, 512 * h:512 * h + 512], ps[:, :], after=[m, tfreed]))
                bank.free(i, ev[-1])
            slot.free(j, m)
            return y, T, ev

        def unit_values(g, hp, b, u):
            y, T, ev = u
            i, ps, freed = bank.take()
            for kt in range(2):
                for h in range(2):
                    e = slice(64 * (2 * hp + h), 64 * (2 * hp + h) + 64)
                    m = mm(ps[64 * h:64 * h + 64, 0:SEQ], V[:, 2 * b + kt, e], T[:, 512 * h + 256 * kt:512 * h + 256 * kt + 256],
                           kt == 0, kt == 1, after=[freed, ev[h], S["V", hp // 4, 2 * b + kt]], signal=(kt == 1))
            ptslot.free(y, m)
            S["v_used", hp // 4] = m
            S["oT", b, hp] = copy("act", oT[:, b, hp, :], ps[:, 0:SEQ], after=[m, S["oT_free", b]])
            bank.free(i, S["oT", b, hp])

        def out_project(g, b):
            i, ps, freed = bank.take()
            for a in range(2):
                for hp in range(NHP):
                    m = mm(ps[:, 128 * a:128 * a + 128], oT[:, b, hp, 128 * a:128 * a + 128], wo[:, hp, :],
                           hp == 0, hp == NHP - 1, after=[freed, S["oT", b, hp], S["Wo"]],
                           signal=(a == 1 and hp == NHP - 1))
            n = GT * g + 2 * b
            tv = t[:, n:n + 2, :]
            k = tt("dve", tv, ps[:, 0:256].rearrange("p (n d) -> p n d", n=2), tv, ALU.add,
                   after=[m, t_ready[n], t_ready[n + 1]])
            bank.free(i, k)
            t_ready[n] = t_ready[n + 1] = [k]
            S["oT_free", b] = m

        def finish2(n, ps, m):
            k = tt("dve", t[:, n, :], ps, t[:, n, :], ALU.add, after=[m, t_ready[n]])
            t_ready[n] = [k]
            return k

        def feed_forward(l, g):
            j, xn, x_ready = S["kept", g]
            yield
            ev = []
            for c in range(4):
                i, ps, freed = bank.take()
                m = mm(ps[:, :], w1[:, 128 * c:128 * c + 128], xn, after=[freed, S["w12"], x_ready], signal=True)
                bc = cols[:, FFB + 4 * l + c:FFB + 4 * l + c + 1]
                ev.append(act(hT[:, g, c, :], ps[:, :], ACT.Relu, bias=bc, after=[m, vals_free[g]]))
                bank.free(i, ev[-1])
                if c == 1:
                    yield
            lnslot.free(j, m)
            yield
            yield
            i, ps, freed = bank.take()
            for a in range(GT):
                for c in range(4):
                    m = mm(ps[:, 128 * a:128 * a + 128], hT[:, g, c, 128 * a:128 * a + 128], w2[:, 128 * c:128 * c + 128],
                           c == 0, c == 3, after=[freed, ev[c], S["w12"]], signal=(a == GT - 1 and c == 3))
            tv = t[:, GT * g:GT * g + GT, :]
            k = tt("dve", tv, ps[:, :].rearrange("p (n d) -> p n d", n=GT), tv, ALU.add,
                   after=[m, t_ready[GT * g:GT * g + GT]])
            bank.free(i, k)
            for n in range(GT * g, GT * g + GT):
                t_ready[n] = [k]
            vals_free[g] = [m]
            S["stage_read"] = m
            S["over", l + 1, g] = True
            yield

        ctx3 = stage[0:64, 1536:1536 + CK]
        stores = []
        out_v = out.rearrange("(n p) d -> p n d", p=128)

        def small3(name):
            at, r, n = so3[name]
            return stage[0:r, 1024 + at:1024 + at + n]

        def last_block(g):
            got, room = S["last_in"], vals_free[g]
            at = 2048 * g
            tT, qT3 = vals[:, at:at + 512], vals[:, at + 512:at + 1024]
            w3, kT3, v3 = vals[:, at + 1024:at + 1280], vals[:, at + 1280:at + 1408], vals[:, at + 1408:at + 1536]
            c3 = ctx3[:, 128 * g:128 * g + 128]
            i, ps, freed = bank.take()
            mm(ps[:, 0:128], small3("wk3"), c3, after=[freed, got])
            m = mm(ps[:, 128:256], c3, small3("wv3"), signal=True)
            k3_ready = ts("dve", kT3, ps[:, 0:128], col("l3_bk"), None, ALU.add, after=[m, room])
            v3_ready = tt("dve", v3, ps[:, 128:256], rows[:, ROW["l3_bv"], :], ALU.add, after=[m, room])
            bank.free(i, v3_ready)
            i, ps, freed = bank.take()
            for c in range(GT):
                m = tr(ps[:, 128 * c:128 * c + 128], t[:, GT * g + c, :], after=[freed, t_ready[GT * g + c]],
                       signal=(c == GT - 1))
            e = copy("act", tT, ps[:, :], after=[m, room])
            bank.free(i, e)
            yield
            yield
            i, ps, freed = bank.take()
            m = mm(ps[:, :], small3("wq3"), tT, after=[freed, e, got], signal=True)
            q_ready = act(qT3, ps[:, :], ACT.Identity, bias=col("l3_bq"), after=[m])
            bank.free(i, q_ready)
            yield
            yield
            i, ps, freed = bank.take()
            for c in range(2):
                m = mm(ps[64 * c:64 * c + 64, 0:SEQ], kT3[:, NCTX * c:NCTX * c + NCTX], qT3[:, SEQ * c:SEQ * c + SEQ],
                       after=[freed, q_ready, k3_ready], signal=(c == 1))
            x, _, xfreed = csslot.take()
            k = red(cmx[:, x, 0:1], ps[:, 0:SEQ], ALU.max, after=[m, xfreed])
            k = ts("dve", cmx[:, x, 1:2], cmx[:, x, 0:1], -float(DM) ** -0.5, None, ALU.mult, after=[k])
            e = act(w3, ps[:, 0:SEQ], ACT.Exp, bias=cmx[:, x, 1:2], scale=float(DM) ** -0.5,
                    accum=csum[:, x, 0:1], after=[k])
            bank.free(i, e)
            yield
            k = recip(crec[:, x, 0:1], csum[:, x, 0:1], after=[e])
            k = ts("dve", v3, v3, crec[:, x, 0:1], None, ALU.mult, after=[k, v3_ready])
            csslot.free(x, k)
            yield
            i, ps, freed = bank.take()
            i2, ps2, freed2 = bank.take()
            for c in range(GT):
                p = slice(64 * (c // 2), 64 * (c // 2) + 64)
                o = (ps if c < 2 else ps2)[:, DM * (c % 2):DM * (c % 2) + DM]
                m = mm(o, w3[p, 128 * (c % 2):128 * (c % 2) + 128], v3[p, :], after=[freed, freed2, k, e],
                       signal=(c % 2 == 1))
            yield
            j, buf, jfreed = lnslot.take()
            b3 = buf.rearrange("p (n d) -> p n d", n=GT)
            for c, o in enumerate((ps, ps2)):
                r = tt("dve", b3[:, 2 * c:2 * c + 2, :], o[:, 0:256].rearrange("p (n d) -> p n d", n=2),
                       t[:, GT * g + 2 * c:GT * g + 2 * c + 2, :], ALU.add, after=[m, jfreed, t_ready[GT * g]])
            bank.free(i, r)
            bank.free(i2, r)
            x, k = yield from statistics([buf[:, DM * c:DM * c + DM] for c in range(GT)], 1e-6, [[r]] * GT)
            for c in range(GT):
                h = buf[:, DM * c:DM * c + DM]
                kx = ts("dve", h, h, mv[:, x, c, 0:1], mv[:, x, c, 1:2], ALU.subtract, ALU.mult, after=[k])
            stslot.free(x, kx)
            k = tt("dve", b3, b3, rows[:, ROW["l3_gamma"], :].unsqueeze(1).to_broadcast([128, GT, DM]), ALU.mult,
                   after=[kx])
            k = tt("dve", b3, b3, rows[:, ROW["l3_beta"], :].unsqueeze(1).to_broadcast([128, GT, DM]), ALU.add, after=[k])
            s = q.put("sp", store_call(out_v[:, GT * g:GT * g + GT, :], b3), [k], by=16, sem=f"store{g}")
            lnslot.free(j, s)
            stores.append(s)

        def after_cross(l):
            def chain(g):
                yield from layer_norm(g, cols[:, PRE_G + l:PRE_G + l + 1], cols[:, PRE_B + l:PRE_B + l + 1], l, 2, True)
                yield from feed_forward(l, g)
                if l + 1 < NLAYER:
                    yield from layer_norm(g, *norm, l + 1, 0)
                else:
                    yield from last_block(g)
            return chain

        w_free = {hp: [S["c_used"]] for hp in range(NHP)}
        stage_free = [S["mask"], S["rmask"], c_ready, v1_read, xT_read]
        units = [(g, hp, b) for g in range(NG) for hp in range(NHP) for b in range(2)]
        wo_read = []
        for l in range(NLAYER):
            v_free, S["oT_free", 0] = [vals_free[0], vals_free[1]], vals_free[2]
            w_project(0, 0, w_free[0])
            w_project(0, 1, w_free[1])
            scored, turned = {}, {}
            for n in range(len(units) + 3):
                g, hp, b = units[n] if n < len(units) else (NG, 0, 0)
                s = n % 16
                if g < NG:
                    scored[n] = unit_scores(g, hp, b)
                if n >= 1 and n - 1 in scored:
                    scored[n - 1] = unit_normal(scored[n - 1])
                if g < NG and b == 1:
                    w_free[hp] = [S["scores_read"]]
                    S["tn_units", g] = S["scores_read"]
                    if g + 1 < NG:
                        w_project(g + 1, hp, w_free[hp])
                elif g == 0 and hp + 2 < NHP:
                    w_project(0, hp + 2, w_free[hp + 2])
                if g == 0 and s < 2:
                    for kt in (2 * s, 2 * s + 1):
                        v_project(0, 0, kt, v_free)
                if 3 <= s < 7 and g < NG:
                    v_project(g, 1, s - 3, [v_free, S["v_used", 1] if g else []])
                if 11 <= s < 15 and g + 1 < NG:
                    v_project(g + 1, 0, s - 11, [S["v_used", 0]])
                if 1 <= g < NG and s in (2, 3):
                    out_project(g - 1, s - 2)
                    if s == 3:
                        tn_free[g - 1] = [S["tn_units", g - 1], S["A_read"], S["wv_read"]]
                        back.start(layer_norm(g - 1, *norm, l, 1))
                if n in (3, 4):
                    back.tick()
                if n == 4:
                    back.until(S, ("over", l, NG - 1))
                    S["Wo"] = load(wo[:, :, :], A["wo"][l].rearrange("p (c d) -> p c d", c=NHP), "wo",
                                   [S["stage_read"], wo_read])
                    S["oT_free", 1] = vals_free[3]
                    got_cross = load_cross(l, [stage_free, S["Wv"], S["stage_read"]])
                if n >= 3:
                    unit_values(*units[n - 3], turned.pop(n - 3))
                back.tick()
                if n >= 2 and n - 2 in scored:
                    turned[n - 2] = unit_turn(scored.pop(n - 2))
                back.tick()
            out_project(NG - 1, 0)
            out_project(NG - 1, 1)
            tn_free[NG - 1] = [S["tn_units", NG - 1], S["A_read"], S["wv_read"]]
            back.start(layer_norm(NG - 1, *norm, l, 1))
            back.tick()
            wo_read = [S["oT_free", 0], S["oT_free", 1]]
            self_read = [S["v_used", 0], S["v_used", 1], wo_read]

            qT, kT, vT, co = stage[:, 0:1024], stage[:, 1024:1536], stage[:, 1536:2048], stage[:, 2048:3072]
            done = {}
            for what, lhs, rhs, dst in (("G", kT, qT, ag_hi), ("H", vT, co, ag_lo)):
                done[what] = []
                for par in range(2):
                    for half in range(2):
                        i, ps, freed = bank.take()
                        p = slice(64 * par, 64 * par + 64)
                        for c in range(4):
                            hp = 4 * half + c
                            for o in range(2):
                                m = mm(ps[64 * o:64 * o + 64, 128 * c:128 * c + 128], lhs[p, 64 * hp:64 * hp + 64],
                                       rhs[p, 128 * hp:128 * hp + 128], after=[freed, got_cross],
                                       signal=(c == 3 and o == 1))
                        at = slice(1024 * par + 512 * half, 1024 * par + 512 * half + 512)
                        k = store_stack(ps, dst[:, at], m, [S["A_read"]])
                        bank.free(i, k)
                        done[what].append(k)
                back.tick()
            got = load_self(l + 1, m) if l + 1 < NLAYER else [m]
            for h in range(NH):
                par, hp = h % 2, h // 2
                i, ps, freed = bank.take()
                G = ag_hi[:, 1024 * par + 128 * hp:1024 * par + 128 * hp + 128]
                mm(ps[:, :], G, mHH[:, :], True, False, after=[freed, done["G"], S["m_parts"]])
                m = mm(ps[:, :], G, mLL[:, :], False, True, signal=True)
                v = ps[:, :].rearrange("p (b k) -> p b k", b=NB)
                k = split(v, C_hi[:, :, h, :], C_lo[:, :, h, :], [m, list(w_free.values())])
                bank.free(i, k)
                c_ready = [k]
                if h % 4 == 3:
                    back.tick()
            v_ready = {}

            def values_and_weights(l, v_ready, after, free, got):
                yield from values_through((ag_lo[:, 0:1024], ag_lo[:, 1024:2048]), after, free, v_ready)
                staged = [S["H_read"]]
                if l + 1 < NLAYER:
                    staged = [self_weights(stage[:, 0:1024], stage[:, 1024:2048], got, [S["H_read"]])]
                    yield
                    S["Wv"] = split_sb(stage[:, 2048:3072], wv_hi[:, :], wv_lo[:, :], got, S["wv_read"])
                load(w1, A["w1"][l], "w12", staged)
                S["w12"] = load(w2, A["w2"][l], "w12", staged)
                if l + 1 == NLAYER:
                    load(ctx3, A["ctxT"], "last", got)
                    load(rows[:, :, :], A["rows3"].rearrange("(o r) d -> o r d", o=1).to_broadcast([128, len(ROWS3), DM]),
                         "last")
                    S["last_in"] = load(stage[:, 1024:1024 + n_small3], A["small3"], "last", got)

            back.start(values_and_weights(l, v_ready, done["H"], self_read, got))
            cross_tiles(0.125, c_ready, v_ready, True, finish2, after_cross(l))
            w_free = {hp: [S["c_used"]] for hp in range(NHP)}
            stage_free = []
        back.drain()

        sems = {n: ctx.enter_context(nc.semaphore("s_" + n)) for n in q.count}
        block = ctx.enter_context(nc.Block())

        @block.tensor
        def _(e):
            q.run("pe", e, sems)

        @block.scalar
        def _(e):
            q.run("act", e, sems)

        @block.vector
        def _(e):
            q.run("dve", e, sems)

        @block.gpsimd
        def _(e):
            q.run("pool", e, sems)

        @block.sync
        def _(e):
            q.run("sp", e, sems)
            for s, v in stores:
                e.wait_ge(sems[s], v)


def bn_call(o, i):
    return lambda e: e.bn_stats(o, i)


def aggr_call(o, i):
    return lambda e: e.bn_aggr(o, i)


def store_call(o, i):
    return lambda e: e.dma_start(o, i)


def layout(inputs):
    g = {k: np.asarray(v) for k, v in inputs.items()}

    def c(a):
        return np.ascontiguousarray(a)

    def pack(parts, values):
        at, n = offsets(parts)
        a = np.zeros((128, n), np.float32)
        for name, rows, w in parts:
            o = at[name][0]
            a[0:rows, o:o + w] = values[name]
        return a

    def pairs(w):
        L, e, n = w.shape
        return c(w.reshape(L, e // 128, 128, n).transpose(0, 2, 1, 3).reshape(L, 128, e // 128 * n))

    E = NH * HD
    x = g["x"].reshape(TOK, DM)
    g1 = g["L0_xattn_gate_w1"]
    kv, ckv = g["L2_xattn_sa_kv"], g["L2_xattn_ca_kv"]
    A = {
        "x": c(x), "xT": c(x.T), "ctxT": c(g["ctx_512"].reshape(CK, DC).T),
        "mask": c(g["mask_BxSxS_ik0"].reshape(TOK, SEQ)), "mask2": c(g["mask_Bx1xS2_if1"].reshape(CK)),
        "small": pack(SMALL, {
            "wq0": g["L0_xattn_Wq"], "wk0T": g["L0_xattn_Wk"].T, "wv0": g["L0_xattn_Wv"], "wo0T": g["L0_xattn_Wo"].T,
            "pos0T": g["L0_xattn_mem_pos_embed"][0].T, "g1x": g1[:, :DM].T, "g1p": g1[:, DM:].T,
            "g2": g["L0_xattn_gate_w2"].T, "entw": g["L0_xattn_ent_w"].T,
            "wq1": g["L1_xattn_Wq"], "wk1": g["L1_xattn_Wk"], "wv1": g["L1_xattn_Wv"], "wo1": g["L1_xattn_Wo"]}),
        "small3": pack(SMALL3, {"wq3": g["L3_xattn_Wq"], "wk3": g["L3_xattn_Wk"], "wv3": g["L3_xattn_Wv"]}),
        "wqT": pairs(g["L2_xattn_sa_q"].transpose(0, 2, 1)), "wkT": pairs(kv[:, :, :E].transpose(0, 2, 1)),
        "wv": c(kv[:, :, E:]), "wo": pairs(g["L2_xattn_sa_ow"]),
        "cqT": pairs(g["L2_xattn_ca_q"].transpose(0, 2, 1)), "ckT": pairs(ckv[:, :, :E].transpose(0, 2, 1)),
        "cvT": pairs(ckv[:, :, E:].transpose(0, 2, 1)), "co": pairs(g["L2_xattn_ca_ow"]),
        "w1": c(g["L2_xattn_ff_w1"]), "w2": pairs(g["L2_xattn_ff_w2"]),
        "lrows": c(np.stack([g["L2_xattn_sa_ob"], g["L2_xattn_ca_ob"], g["L2_xattn_ff_b2"]], 1)),
        "rows": c(np.stack([g["L0_xattn_ln_scale"], g["L0_xattn_ln_bias"], g["L1_xattn_bo"]])),
        "rows3": c(np.stack([g["L3_xattn_bv"], g["L3_xattn_gamma"], g["L3_xattn_beta"]])),
        "ident": np.eye(128, dtype=np.float32),
        "hmask": c(np.repeat(np.eye(H0, dtype=np.float32), DM // H0, 0)),
    }
    cols = np.zeros((128, NCOL), np.float32)
    for name, v in (("gate_b1", g["L0_xattn_gate_b1"]), ("gate_b2", np.broadcast_to(g["L0_xattn_gate_b2"], 128)),
                    ("ent_b", np.broadcast_to(g["L0_xattn_ent_b"], 128)), ("l1_bq", g["L1_xattn_bq"]),
                    ("l1_bk", g["L1_xattn_bk"]), ("l1_bv", g["L1_xattn_bv"]), ("l3_bq", g["L3_xattn_bq"]),
                    ("l3_bk", g["L3_xattn_bk"]), ("norm_g", g["L2_xattn_norm_g"]), ("norm_b", g["L2_xattn_norm_b"])):
        cols[0:len(v), COL[name]] = v
    cols[:, PRE_G:PRE_G + NLAYER] = g["L2_xattn_pre_g"].T
    cols[:, PRE_B:PRE_B + NLAYER] = g["L2_xattn_pre_b"].T
    cols[:, FFB:] = g["L2_xattn_ff_b1"].reshape(NLAYER * 4, 128).T
    A["cols"] = cols
    return A


def kernel(**inputs):
    import concourse.bacc as bacc
    from concourse.bass_utils import run_bass_kernel_spmd

    nc = bacc.Bacc("TRN2", target_bir_lowering=False, num_devices=1)
    arrays = layout(inputs)
    aps = {n: nc.dram_tensor("in_" + n, a.shape, mybir.dt.from_np(a.dtype), kind="ExternalInput").ap()
           for n, a in arrays.items()}
    out = nc.dram_tensor("out", (TOK, DM), F32, kind="ExternalOutput").ap()
    decoder_kernel(nc, aps, out)
    r = run_bass_kernel_spmd(nc, [{"in_" + n: a for n, a in arrays.items()}], core_ids=[0])
    return r.results[0]["out"].reshape(NB, SEQ, DM)
```
